# Optimizing a Trainium2 kernel written in Bass

```python
import numpy as np
import jax
import jax.numpy as jnp

def _softmax(x, axis=-1):
    return jax.nn.softmax(x, axis=axis)

def _gelu(x):
    return jax.nn.gelu(x, approximate=True)

def _silu(x):
    return jax.nn.silu(x)

def _sigmoid(x):
    return jax.nn.sigmoid(x)

def _layernorm(x, axis=-1, eps=1e-05):
    m = jnp.mean(x, axis=axis, keepdims=True)
    v = jnp.var(x, axis=axis, keepdims=True)
    return (x - m) / jnp.sqrt(v + eps)

def _scatter_add(tgt, idx, src, axis=0):
    return tgt.at[idx].add(src)

def _segment_sum(src, seg, n):
    return jax.ops.segment_sum(src, seg, n)
kernel_name = 'mk_decoder_preln_d2_seqx_r4_243368'

def setup_inputs(seed: int=0):
    np.random.seed(seed)
    _w = jnp.asarray

    def _rec_inputs():
        import jax
        import jax.numpy as jnp
        _rk = jax.random.key(seed)
        x = -0.0002928 + 1 * jax.random.normal(jax.random.fold_in(_rk, 1), (8, 256, 256), jnp.float32)
        _lenS = 256 - jax.random.randint(jax.random.fold_in(_rk, 7), (8,), 0, max(1, 256 // 4) + 1, jnp.int32)
        _lenS2 = 77 - jax.random.randint(jax.random.fold_in(_rk, 8), (8,), 0, max(1, 77 // 4) + 1, jnp.int32)
        _ctx_1024P = jax.random.normal(jax.random.fold_in(_rk, 11), (8, 16, 256), jnp.float32)
        _ctx_1024c = jax.random.dirichlet(jax.random.fold_in(_rk, 511), 0.3 * jnp.ones((16,), jnp.float32), (8, 77))
        _ctx_1024t = jnp.einsum('bsk,bkd->bsd', _ctx_1024c, _ctx_1024P)
        _ctx_1024t = _ctx_1024t * jax.lax.rsqrt(jnp.mean(jnp.square(_ctx_1024t)) + 1e-12) * 0.953939
        ctx_1024 = 4.13588e-05 + 0.999923 * (_ctx_1024t + 0.3 * jax.random.normal(jax.random.fold_in(_rk, 611), (8, 77, 256), jnp.float32))
        return (x, ctx_1024)
    x, ctx_1024 = _rec_inputs()

    def _L0_attn_setup():
        import jax, jax.numpy as jnp
        import numpy as np
        B, N, D_MODEL, N_HEADS, WINDOW = (2, 512, 256, 16, 128)
        HEAD_DIM = D_MODEL // N_HEADS
        key = jax.random.key(seed)
        k1, k2, k3 = jax.random.split(key, 3)
        x = jax.random.normal(k1, (B, N, D_MODEL), dtype=jnp.float32)
        W_qkv = jax.random.normal(k2, (D_MODEL, 3 * D_MODEL), dtype=jnp.float32) * 0.02
        W_proj = jax.random.normal(k3, (D_MODEL, D_MODEL), dtype=jnp.float32) * 0.02
        b_proj = jnp.zeros((D_MODEL,), dtype=jnp.float32)
        return {'x': x, 'W_qkv': W_qkv, 'W_proj': W_proj, 'b_proj': b_proj}
    _L0_attn_all = _L0_attn_setup()
    _L0_attn_in = {k: v for k, v in _L0_attn_all.items() if k in ('W_qkv', 'W_proj', 'b_proj')}
    del _L0_attn_all

    def _L0_xattn_setup():
        import jax, jax.numpy as jnp
        import numpy as np
        FEATURE_DIM = 256
        NUM_HEADS = 16
        HEAD_DIM = FEATURE_DIM // NUM_HEADS
        key = jax.random.key(seed)
        ks = jax.random.split(key, 11)
        B, SQ, SKV, D = (4, 256, 512, FEATURE_DIM)
        s = 1.0 / np.sqrt(D)
        return {'query': jax.random.normal(ks[0], (B, SQ, D), jnp.float32), 'key': jax.random.normal(ks[1], (B, SKV, D), jnp.float32), 'value': jax.random.normal(ks[2], (B, SKV, D), jnp.float32), 'wq': jax.random.normal(ks[3], (D, D), jnp.float32) * s, 'bq': jnp.zeros((D,), jnp.float32), 'wk': jax.random.normal(ks[4], (D, D), jnp.float32) * s, 'bk': jnp.zeros((D,), jnp.float32), 'wv': jax.random.normal(ks[5], (D, D), jnp.float32) * s, 'bv': jnp.zeros((D,), jnp.float32), 'wo': jax.random.normal(ks[6], (D, D), jnp.float32) * s, 'bo': jnp.zeros((D,), jnp.float32)}
    _L0_xattn_all = _L0_xattn_setup()
    _L0_xattn_in = {k: v for k, v in _L0_xattn_all.items() if k in ('wq', 'bq', 'wk', 'bk', 'wv', 'bv', 'wo', 'bo')}
    del _L0_xattn_all

    def _L0_ffn_setup():
        import jax, jax.numpy as jnp
        import numpy as np
        EMB_DIM = 256
        HIDDEN = int(2 / 3 * 4 * EMB_DIM)
        NUM_EXPERTS = 8
        TOP_K = 2
        B, S = (4, 256)
        key = jax.random.key(seed)
        ks = jax.random.split(key, 5)
        sc = 1.0 / np.sqrt(EMB_DIM)
        sh = 1.0 / np.sqrt(HIDDEN)
        return {'x': jax.random.normal(ks[0], (B, S, EMB_DIM), dtype=jnp.float32), 'Wg': jax.random.normal(ks[1], (NUM_EXPERTS, EMB_DIM), dtype=jnp.float32) * sc, 'W1': jax.random.normal(ks[2], (NUM_EXPERTS, HIDDEN, EMB_DIM), dtype=jnp.float32) * sc, 'W2': jax.random.normal(ks[3], (NUM_EXPERTS, HIDDEN, EMB_DIM), dtype=jnp.float32) * sc, 'W3': jax.random.normal(ks[4], (NUM_EXPERTS, EMB_DIM, HIDDEN), dtype=jnp.float32) * sh}
    _L0_ffn_all = _L0_ffn_setup()
    _L0_ffn_in = {k: v for k, v in _L0_ffn_all.items() if k in ('Wg', 'W1', 'W2', 'W3')}
    del _L0_ffn_all

    def _L1_attn_setup():
        import jax, jax.numpy as jnp
        import numpy as np
        DIM = 256
        HEADS = 16
        DIM_HEAD = 64
        B, S = (4, 512)
        key = jax.random.key(seed)
        ks = jax.random.split(key, 6)
        sd = 1.0 / np.sqrt(DIM)
        return {'latents': jax.random.normal(ks[0], (B, S, DIM), dtype=jnp.float32), 'ln_gamma': jnp.ones((DIM,), dtype=jnp.float32), 'ln_beta': jnp.zeros((DIM,), dtype=jnp.float32), 'Wq': jax.random.normal(ks[1], (DIM, HEADS * DIM_HEAD), dtype=jnp.float32) * sd, 'Wk': jax.random.normal(ks[2], (DIM, HEADS * DIM_HEAD), dtype=jnp.float32) * sd, 'Wv': jax.random.normal(ks[3], (DIM, HEADS * DIM_HEAD), dtype=jnp.float32) * sd, 'Wo': jax.random.normal(ks[4], (HEADS * DIM_HEAD, DIM), dtype=jnp.float32) * sd}
    _L1_attn_all = _L1_attn_setup()
    _L1_attn_in = {k: v for k, v in _L1_attn_all.items() if k in ('ln_gamma', 'ln_beta', 'Wq', 'Wk', 'Wv', 'Wo')}
    del _L1_attn_all

    def _L1_xattn_setup():
        import jax, jax.numpy as jnp
        import numpy as np
        EMBED = 256
        HEADS = 16
        HEAD_DIM = EMBED // HEADS
        key = jax.random.key(seed)
        ks = jax.random.split(key, 8)
        N, L = (2, 1024)
        return {'value': jax.random.normal(ks[0], (N, L, EMBED), dtype=jnp.float32), 'key': jax.random.normal(ks[1], (N, L, EMBED), dtype=jnp.float32), 'query': jax.random.normal(ks[2], (N, L, EMBED), dtype=jnp.float32), 'Wv': jax.random.normal(ks[3], (HEAD_DIM, HEAD_DIM), dtype=jnp.float32) * HEAD_DIM ** (-0.5), 'Wk': jax.random.normal(ks[4], (HEAD_DIM, HEAD_DIM), dtype=jnp.float32) * HEAD_DIM ** (-0.5), 'Wq': jax.random.normal(ks[5], (HEAD_DIM, HEAD_DIM), dtype=jnp.float32) * HEAD_DIM ** (-0.5), 'Wo': jax.random.normal(ks[6], (EMBED, EMBED), dtype=jnp.float32) * EMBED ** (-0.5), 'bo': jnp.zeros((EMBED,), dtype=jnp.float32)}
    _L1_xattn_all = _L1_xattn_setup()
    _L1_xattn_in = {k: v for k, v in _L1_xattn_all.items() if k in ('Wv', 'Wk', 'Wq', 'Wo', 'bo')}
    del _L1_xattn_all

    def _L1_ffn_setup():
        import jax, jax.numpy as jnp
        import numpy as np
        B, S, H, M, E, K = (4, 512, 256, 1024, 8, 2)
        key = jax.random.key(seed)
        ks = jax.random.split(key, 6)
        x = jax.random.normal(ks[0], (B, S, H), dtype=jnp.float32)
        Wr = jax.random.normal(ks[1], (E, H), dtype=jnp.float32) * (1.0 / np.sqrt(H))
        W1 = jax.random.normal(ks[2], (E, M, H), dtype=jnp.float32) * np.sqrt(2.0 / (H + M))
        b1 = jax.random.normal(ks[3], (E, M), dtype=jnp.float32) * 1e-06
        W2 = jax.random.normal(ks[4], (E, H, M), dtype=jnp.float32) * np.sqrt(2.0 / (H + M))
        b2 = jax.random.normal(ks[5], (E, H), dtype=jnp.float32) * 1e-06
        return {'x': x, 'Wr': Wr, 'W1': W1, 'b1': b1, 'W2': W2, 'b2': b2}
    _L1_ffn_all = _L1_ffn_setup()
    _L1_ffn_in = {k: v for k, v in _L1_ffn_all.items() if k in ('Wr', 'W1', 'b1', 'W2', 'b2')}
    del _L1_ffn_all
    return {'x': x, 'ctx_1024': ctx_1024, 'L0_attn_W_qkv': _L0_attn_in['W_qkv'], 'L0_attn_W_proj': _L0_attn_in['W_proj'], 'L0_attn_b_proj': _L0_attn_in['b_proj'], 'L0_xattn_wq': _L0_xattn_in['wq'], 'L0_xattn_bq': _L0_xattn_in['bq'], 'L0_xattn_wk': _L0_xattn_in['wk'], 'L0_xattn_bk': _L0_xattn_in['bk'], 'L0_xattn_wv': _L0_xattn_in['wv'], 'L0_xattn_bv': _L0_xattn_in['bv'], 'L0_xattn_wo': _L0_xattn_in['wo'], 'L0_xattn_bo': _L0_xattn_in['bo'], 'L0_ffn_Wg': _L0_ffn_in['Wg'], 'L0_ffn_W1': _L0_ffn_in['W1'], 'L0_ffn_W2': _L0_ffn_in['W2'], 'L0_ffn_W3': _L0_ffn_in['W3'], 'L1_attn_ln_gamma': _L1_attn_in['ln_gamma'], 'L1_attn_ln_beta': _L1_attn_in['ln_beta'], 'L1_attn_Wq': _L1_attn_in['Wq'], 'L1_attn_Wk': _L1_attn_in['Wk'], 'L1_attn_Wv': _L1_attn_in['Wv'], 'L1_attn_Wo': _L1_attn_in['Wo'], 'L1_xattn_Wv': _L1_xattn_in['Wv'], 'L1_xattn_Wk': _L1_xattn_in['Wk'], 'L1_xattn_Wq': _L1_xattn_in['Wq'], 'L1_xattn_Wo': _L1_xattn_in['Wo'], 'L1_xattn_bo': _L1_xattn_in['bo'], 'L1_ffn_Wr': _L1_ffn_in['Wr'], 'L1_ffn_W1': _L1_ffn_in['W1'], 'L1_ffn_b1': _L1_ffn_in['b1'], 'L1_ffn_W2': _L1_ffn_in['W2'], 'L1_ffn_b2': _L1_ffn_in['b2']}

def reference(x, ctx_1024, L0_attn_W_qkv, L0_attn_W_proj, L0_attn_b_proj, L0_xattn_wq, L0_xattn_bq, L0_xattn_wk, L0_xattn_bk, L0_xattn_wv, L0_xattn_bv, L0_xattn_wo, L0_xattn_bo, L0_ffn_Wg, L0_ffn_W1, L0_ffn_W2, L0_ffn_W3, L1_attn_ln_gamma, L1_attn_ln_beta, L1_attn_Wq, L1_attn_Wk, L1_attn_Wv, L1_attn_Wo, L1_xattn_Wv, L1_xattn_Wk, L1_xattn_Wq, L1_xattn_Wo, L1_xattn_bo, L1_ffn_Wr, L1_ffn_W1, L1_ffn_b1, L1_ffn_W2, L1_ffn_b2):
    import jax
    import jax.numpy as jnp

    def _L0_attn_ref(x, W_qkv, W_proj, b_proj):
        import jax, jax.numpy as jnp
        import numpy as np
        B, N, D_MODEL, N_HEADS, WINDOW = (2, 512, 256, 16, 128)
        HEAD_DIM = D_MODEL // N_HEADS
        Bx, Nx, C = x.shape
        H, Dh = (N_HEADS, C // N_HEADS)
        scale = Dh ** (-0.5)
        window = min(WINDOW, Nx)
        half = window // 2
        qkv = (x @ W_qkv).reshape(Bx, Nx, 3, H, Dh).transpose(2, 0, 3, 1, 4)
        q, k, v = (qkv[0], qkv[1], qkv[2])
        i = jnp.arange(Nx)[:, None]
        j = jnp.arange(Nx)[None, :]
        allowed = jnp.abs(i - j) <= half
        attn = jnp.einsum('bhqd,bhkd->bhqk', q, k) * scale
        attn = jnp.where(allowed[None, None], attn, -jnp.inf)
        attn = jax.nn.softmax(attn, axis=-1)
        out = jnp.einsum('bhqk,bhkd->bhqd', attn, v)
        out = out.transpose(0, 2, 1, 3).reshape(Bx, Nx, C)
        return out @ W_proj + b_proj

    def _L0_xattn_ref(query, key, value, wq, bq, wk, bk, wv, bv, wo, bo):
        import jax, jax.numpy as jnp
        import numpy as np
        FEATURE_DIM = 256
        NUM_HEADS = 16
        HEAD_DIM = FEATURE_DIM // NUM_HEADS
        B, SQ, D = query.shape
        H, HD = (NUM_HEADS, HEAD_DIM)
        q = (query @ wq.T + bq).reshape(B, SQ, H, HD).transpose(0, 2, 1, 3)
        k = (key @ wk.T + bk).reshape(B, -1, H, HD).transpose(0, 2, 1, 3)
        v = (value @ wv.T + bv).reshape(B, -1, H, HD).transpose(0, 2, 1, 3)
        scores = jnp.einsum('bhqd,bhkd->bhqk', q, k) / jnp.sqrt(jnp.asarray(HD, q.dtype))
        attn = jax.nn.softmax(scores, axis=-1)
        ctx = jnp.einsum('bhqk,bhkd->bhqd', attn, v)
        ctx = ctx.transpose(0, 2, 1, 3).reshape(B, SQ, D)
        return ctx @ wo.T + bo

    def _L0_ffn_ref(x, Wg, W1, W2, W3):
        import jax, jax.numpy as jnp
        import numpy as np
        EMB_DIM = 256
        HIDDEN = int(2 / 3 * 4 * EMB_DIM)
        NUM_EXPERTS = 8
        TOP_K = 2
        B, S = (4, 256)
        gate_logits = jnp.einsum('bsd,ed->bse', x, Wg)
        top_v, top_i = jax.lax.top_k(gate_logits, TOP_K)
        mask = jnp.any(top_i[..., :, None] == jnp.arange(NUM_EXPERTS), axis=-2)
        sparse_logits = jnp.where(mask, gate_logits, -jnp.inf)
        gating = jax.nn.softmax(sparse_logits, axis=-1)
        h1 = jnp.einsum('bsd,ehd->bseh', x, W1)
        h2 = jnp.einsum('bsd,ehd->bseh', x, W2)
        hidden = jax.nn.silu(h1) * h2
        expert_out = jnp.einsum('bseh,edh->bsed', hidden, W3)
        return jnp.einsum('bsed,bse->bsd', expert_out, gating)

    def _L1_attn_ref(latents, ln_gamma, ln_beta, Wq, Wk, Wv, Wo):
        import jax, jax.numpy as jnp
        import numpy as np
        DIM = 256
        HEADS = 16
        DIM_HEAD = 64
        B, S = (4, 512)
        mu = jnp.mean(latents, axis=-1, keepdims=True)
        var = jnp.mean((latents - mu) ** 2, axis=-1, keepdims=True)
        x = (latents - mu) * jax.lax.rsqrt(var + 1e-05) * ln_gamma + ln_beta
        b, s, _ = x.shape
        q = (x @ Wq).reshape(b, s, HEADS, DIM_HEAD).transpose(0, 2, 1, 3)
        k = (x @ Wk).reshape(b, s, HEADS, DIM_HEAD).transpose(0, 2, 1, 3)
        v = (x @ Wv).reshape(b, s, HEADS, DIM_HEAD).transpose(0, 2, 1, 3)
        scale = 1.0 / np.sqrt(np.sqrt(DIM_HEAD))
        scores = jnp.einsum('bhqd,bhkd->bhqk', q * scale, k * scale)
        weights = jax.nn.softmax(scores.astype(jnp.float32), axis=-1).astype(scores.dtype)
        out = jnp.einsum('bhqk,bhkd->bhqd', weights, v)
        out = out.transpose(0, 2, 1, 3).reshape(b, s, HEADS * DIM_HEAD)
        return out @ Wo

    def _L1_xattn_ref(value, key, query, Wv, Wk, Wq, Wo, bo):
        import jax, jax.numpy as jnp
        import numpy as np
        EMBED = 256
        HEADS = 16
        HEAD_DIM = EMBED // HEADS
        N, Lq = (query.shape[0], query.shape[1])
        Lk, Lv = (key.shape[1], value.shape[1])
        v = value.reshape(N, Lv, HEADS, HEAD_DIM)
        k = key.reshape(N, Lk, HEADS, HEAD_DIM)
        q = query.reshape(N, Lq, HEADS, HEAD_DIM)
        v = jnp.einsum('nlhd,ed->nlhe', v, Wv)
        k = jnp.einsum('nlhd,ed->nlhe', k, Wk)
        q = jnp.einsum('nlhd,ed->nlhe', q, Wq)
        energy = jnp.einsum('nqhd,nkhd->nhqk', q, k)
        attention = jax.nn.softmax(energy * EMBED ** (-0.5), axis=3)
        out = jnp.einsum('nhqk,nkhd->nqhd', attention, v).reshape(N, Lq, EMBED)
        return out @ Wo.T + bo

    def _L1_ffn_ref(x, Wr, W1, b1, W2, b2):
        import jax, jax.numpy as jnp
        import numpy as np
        B, S, H, M, E, K = (4, 512, 256, 1024, 8, 2)
        logits = jnp.einsum('bsh,eh->bse', x, Wr)
        probs = jax.nn.softmax(logits, axis=-1)
        top_v, top_i = jax.lax.top_k(probs, K)
        top_v = top_v / jnp.sum(top_v, axis=-1, keepdims=True)
        out = jnp.zeros_like(x)
        for e in range(E):
            w_e = jnp.sum(jnp.where(top_i == e, top_v, 0.0), axis=-1)
            h = jnp.einsum('bsh,mh->bsm', x, W1[e]) + b1[e]
            h = jax.nn.gelu(h, approximate=False)
            y = jnp.einsum('bsm,hm->bsh', h, W2[e]) + b2[e]
            out = out + y * w_e[..., None]
        return out
    x = x + _L0_attn_ref(_layernorm(x, axis=-1), L0_attn_W_qkv, L0_attn_W_proj, L0_attn_b_proj)
    x = x + _L0_xattn_ref(_layernorm(x, axis=-1), ctx_1024, ctx_1024, L0_xattn_wq, L0_xattn_bq, L0_xattn_wk, L0_xattn_bk, L0_xattn_wv, L0_xattn_bv, L0_xattn_wo, L0_xattn_bo)
    x = x + _L0_ffn_ref(_layernorm(x, axis=-1), L0_ffn_Wg, L0_ffn_W1, L0_ffn_W2, L0_ffn_W3)
    x = x + _L1_attn_ref(_layernorm(x, axis=-1), L1_attn_ln_gamma, L1_attn_ln_beta, L1_attn_Wq, L1_attn_Wk, L1_attn_Wv, L1_attn_Wo)
    x = x + _L1_xattn_ref(ctx_1024, ctx_1024, _layernorm(x, axis=-1), L1_xattn_Wv, L1_xattn_Wk, L1_xattn_Wq, L1_xattn_Wo, L1_xattn_bo)
    x = x + _L1_ffn_ref(_layernorm(x, axis=-1), L1_ffn_Wr, L1_ffn_W1, L1_ffn_b1, L1_ffn_W2, L1_ffn_b2)
    return x

_drawn_inputs = setup_inputs


def setup_inputs(seed=0):
    import zlib

    import numpy as np

    out = dict(_drawn_inputs(seed))
    spreads = {'L0_attn_b_proj': (0.0, 0.1),
     'L0_xattn_bq': (0.0, 0.1),
     'L0_xattn_bk': (0.0, 0.1),
     'L0_xattn_bv': (0.0, 0.1),
     'L0_xattn_bo': (0.0, 0.1),
     'L1_attn_ln_gamma': (1.0, 0.2),
     'L1_attn_ln_beta': (0.0, 0.1),
     'L1_xattn_bo': (0.0, 0.1)}
    factors = {}
    for name, (base, spread) in spreads.items():
        noise = np.random.default_rng([zlib.crc32(name.encode()), seed]).standard_normal(out[name].shape)
        drawn = base * np.exp(spread * noise) if base else spread * noise
        out[name] = jnp.asarray(drawn.astype(out[name].dtype))
    for name, factor in factors.items():
        out[name] = (out[name] * factor).astype(out[name].dtype)
    return out
```

```python
from contextlib import ExitStack

import concourse.bass as bass
from concourse import mybir

P = 128
ALU = mybir.AluOpType
ACT = mybir.ActivationFunctionType
AX = mybir.AxisListType
F32 = mybir.dt.float32
BF16 = mybir.dt.bfloat16
I32 = mybir.dt.int32
U32 = mybir.dt.uint32

B, S, D = 8, 256, 256
SC = 77
HEADS = 16
QT_N = S // P
DT = D // P
TILES = B * QT_N
LN_EPS = 1e-5
LOOK = 3
HALF_WINDOW = 64
MASKED = -1.0e30


def count(per_batch, b, j):
    return (b + 1) * per_batch + j + 1


def attention(nc, name, env, dh, windowed=False, cross=False, affine=None, q_scale=1.0,
              wq=None, wk=None, wv=None, wo=None, bq=None, bk=None, bv=None, bo=None,
              ctx_dram=None, x_landed=(), w_landed=()):
    X, ident, identb, neg_half, eps = env["X"], env["ident"], env["identb"], env["neg_half"], env["eps"]
    wmask = env.get("wmask")
    hpc = P // dh
    nct = HEADS // hpc
    hmask = env["hmask16"] if dh == 16 else env["hmask64"]
    G = 2 if cross else 1
    NU = HEADS // G
    keys = SC if cross else S
    width = SC if cross else (S - HALF_WINDOW if windowed else S)
    first_key = (0, HALF_WINDOW) if windowed else (0, 0)
    dv = 32 if dh == 16 else 64
    HG = P // dv
    NG = HEADS // HG
    UG = HG // G
    chunks = [(0, SC)] if cross else [(0, P), (P, width - P)]
    NC = len(chunks)
    if windowed:
        v_rows = [(first_key[q] + o, n) for q in range(QT_N) for o, n in chunks]
    elif cross:
        v_rows = [(0, SC)]
    else:
        v_rows = [(0, P), (P, P)]
    NV = len(v_rows)
    vw = HEADS * dh
    per_bank = 512 // S
    fev = [("xt", 0)]
    if cross:
        fev.append(("ct", 0))
    qev = [("q", i) for i in range((nct + per_bank - 1) // per_bank)]
    if cross:
        kev = [("k", 0), ("v", 0)]
        vev = []
    else:
        kev = [("k", i) for i in range((nct + per_bank - 1) // per_bank)]
        vev = [("v", v, i) for v in range(NV) for i in range((vw + 511) // 512)]
        if vw < 512:
            vev = [("v", v, 0) for v in range(0, NV, 2)]
    fev += qev + vev
    NF, NK = len(fev), len(kev)
    f_at = {e: i for i, e in enumerate(fev)}
    plan = {}
    start = 2
    plan.setdefault(start, []).append(("f", fev[0]))
    if cross:
        plan[start].append(("f", fev[1]))
    order = []
    if cross:
        order = [("f", qev[0]), ("k", kev[0]), ("k", kev[1])]
        order += [("f", e) for e in vev]
    else:
        for a, c in zip(qev, kev):
            order += [("k", c), ("f", a)]
        order += [("f", e) for e in vev]
    per_step = (len(order) + NU - LOOK - start - 3) // (NU - LOOK - start - 2)
    for i, o in enumerate(order):
        plan.setdefault(start + 1 + i // per_step, []).append(o)

    with ExitStack() as stack:
        def sb(n, shape, dt=F32):
            return stack.enter_context(nc.sbuf_tensor(f"{name}_{n}", shape, dt))

        used = []

        def sem(n):
            used.append(nc.alloc_semaphore(f"{name}_{n}"))
            return used[-1]

        ps_s = stack.enter_context(nc.psum_tensor(f"{name}_ps_s", [P, 2, 512], F32))
        ps_t = stack.enter_context(nc.psum_tensor(f"{name}_ps_t", [P, 2, 512], F32))
        ps_o = stack.enter_context(nc.psum_tensor(f"{name}_ps_o", [P, 512], F32))
        ps_f = stack.enter_context(nc.psum_tensor(f"{name}_ps_f", [P, 2, 512], F32))
        ps_k = stack.enter_context(nc.psum_tensor(f"{name}_ps_k", [P, 512], F32))

        stats = sb("stats", [P, QT_N, 6])
        mv = sb("mv", [P, QT_N, 2])
        veps = sb("veps", [P, QT_N])
        rstd = sb("rstd", [P, QT_N])
        carrier = sb("carrier", [P, 1])
        xn = sb("xn", [P, QT_N, D])
        xt = sb("xt", [P, DT, S])
        ctx_in = sb("ctx_in", [P, 2, D]) if cross else None
        ct = sb("ct", [P, DT, SC]) if cross else None
        q_t = [sb(f"q_t{i}", [P, nct, S]) for i in range(2)]
        k_m = [sb(f"k_m{i}", [P, HEADS, keys]) for i in range(2)]
        v_w = dv if dh == 16 else dh
        v_s = [sb(f"v_s{i}", [P, NV, HEADS, v_w]) for i in range(2)]
        shifted = sb("shifted", [P, 2, QT_N * G, width]) if cross else None
        prob = sb("prob", [P, 4, QT_N * G, width])
        nmax = sb("nmax", [P, 4, QT_N * G])
        total = sb("total", [P, 4, QT_N * G])
        rtot = sb("rtot", [P, 4, QT_N * G])
        prob_t = [sb(f"prob_t{i}", [P, UG, 512]) for i in range(2)]
        o_t = sb("o_t", [P, NG, S])

        stats_done, var_done, rstd_done, xn_done = sem("stats"), sem("var"), sem("rstd"), sem("xn")
        ctx_landed = [sem("ctx0"), sem("ctx1")] if cross else None
        front_done, front_free = sem("front_done"), sem("front_free")
        keys_done, keys_free = sem("keys_done"), sem("keys_free")
        scores_done, max_done, shift_done = sem("scores"), sem("max"), sem("shift")
        exp_done, total_done, rtot_done, norm_done = sem("exp"), sem("total"), sem("rtot"), sem("norm")
        turned, turned_free = sem("turned"), [sem("turned_free0"), sem("turned_free1")]
        out_done, out_free = sem("out_done"), sem("out_free")
        init_done = sem("init")
        NO = NG + 1
        bias_done, veps_done, carried = sem("bias"), sem("veps"), sem("carried")

        def unit(kind, b, j):
            nb = 0
            if j >= NU:
                if kind == "last":
                    return None
                return b + 1, 1, j - NU
            if kind == "first":
                return None
            return b, 0, j

        def run(step, front, tail, eng):
            front(-1, 0)
            for i in range(NU - LOOK, NU):
                step("first", -1, 1, i)
            with eng.Fori(0, B // 2 - 1) as pair:
                for par in range(2):
                    b = pair * 2 + par
                    for i in range(NU):
                        front(b, 1 - par, i)
                        step("mid", b, par, i)
                    tail(b, par)
            for par in range(2):
                b = B - 2 + par
                for i in range(NU):
                    if par == 0:
                        front(b, 1, i)
                    step("mid" if par == 0 else "last", b, par, i)
                tail(b, par)

        with nc.Block() as block:
            def evacuate(eng, which, b, par, j):
                g, r = j // UG, j % UG
                eng.wait_ge(turned, count(NU, b, j))
                if r < 2:
                    eng.wait_ge(out_done, count(NO, b, g - 2) if g >= 2 else count(NO, b - 1, NG - 2 + g))
                dst, src = prob_t[g % 2], ps_t
                parts = [(SC, 0, 512)] if cross else [(n, c * S, S) for c, (_, n) in enumerate(chunks)]
                if not cross and not windowed:
                    parts = [(P, 0, 512)]
                for n, o, w in parts:
                    if which == "vector":
                        ins = eng.tensor_copy(dst[0:n, r, o:o + w], src[0:n, j % 2, o:o + w])
                    else:
                        ins = eng.activation(dst[0:n, r, o:o + w], src[0:n, j % 2, o:o + w], ACT.Copy)
                ins.then_inc(turned_free[j % 2], 1)

            @block.sync
            def _(eng):
                if not cross:
                    return

                def load(b, par, i):
                    if i is not None and i != 0:
                        return
                    if i is not None:
                        eng.wait_ge(front_done, count(NF, b - 1, f_at[("ct", 0)]))
                    eng.dma_start(ctx_in[0:SC, par, :], ctx_dram[bass.ds(b + 1, 1)].rearrange("a s d -> (a s) d")
                                  ).then_inc(ctx_landed[par], 16)

                run(lambda *a: None, lambda b, par, i=None: load(b, par, i), lambda b, par: None, eng)

            @block.vector
            def _(eng):
                for s, n in ((stats_done, QT_N), (var_done, 1), (xn_done, QT_N), (keys_free, NK),
                             (max_done, NU), (shift_done, NU), (total_done, NU), (rtot_done, NU),
                             (turned_free[1], NU // 2)):
                    eng.sem_inc(s, n)
                eng.sem_inc(out_free, 1)
                if dh == 16:
                    for i in range(2):
                        eng.memset(v_s[i][:, :, :, :], 0.0).then_inc(init_done, 1)

                for s, v in x_landed[:1]:
                    eng.wait_ge(s, v)

                def front(b, par, i=None):
                    nb = b + 1
                    if i is None or i == 0:
                        if i == 0:
                            for s, v in x_landed[1:]:
                                eng.wait_ge(s, v)
                        for q in range(QT_N):
                            eng.bn_stats(stats[:, q, :], X[:, bass.ds(nb * QT_N + q, 1), :].rearrange("p a d -> p (a d)")
                                         ).then_inc(stats_done, 1)
                        if i is not None:
                            eng.wait_ge(carried, nb)
                        eng.wait_ge(stats_done, count(QT_N, nb, QT_N - 1))
                        eng.tensor_copy(carrier[:, :], stats[:, 0, 0:1]).then_inc(carried, 1)
                        for q in range(QT_N):
                            ins = eng.bn_aggr(mv[:, q, :], stats[:, q, :])
                        ins.then_inc(var_done, 1)
                    if i is None or i == 1:
                        eng.wait_ge(rstd_done, count(1, nb, 0))
                        for q in range(QT_N):
                            if q == 0:
                                eng.wait_ge(front_done, count(NF, nb - 1, 0))
                            eng.tensor_scalar(xn[:, q, :], X[:, bass.ds(nb * QT_N + q, 1), :].rearrange("p a d -> p (a d)"),
                                              mv[:, q, 0:1], rstd[:, q:q + 1], ALU.subtract, ALU.mult
                                              ).then_inc(xn_done, 1)
                    for st, evs in sorted(plan.items()):
                        if i is not None and st != i:
                            continue
                        for ring, ev in evs:
                            if ring == "k":
                                key_event(nb, par, ev)

                def key_event(nb, par, ev):
                    e = kev.index(ev)
                    eng.wait_ge(keys_done, count(NK, nb, e))
                    if ev[0] == "k" and cross:
                        for c in range(nct):
                            src = ps_k[:, c * SC:(c + 1) * SC].unsqueeze(1).to_broadcast([P, hpc, SC])
                            m = hmask[:, 0:hpc].unsqueeze(2).to_broadcast([P, hpc, SC])
                            dst = k_m[par][:, c * hpc:(c + 1) * hpc, :]
                            if bk is not None:
                                ins = eng.scalar_tensor_tensor(out=dst, in0=src, scalar=bk[:, c:c + 1], in1=m,
                                                               op0=ALU.add, op1=ALU.mult)
                            else:
                                ins = eng.tensor_tensor(dst, src, m, ALU.mult)
                        ins.then_inc(keys_free, 1)
                    elif ev[0] == "v":
                        dst = v_s[par][0:SC, 0, :, 0:dh]
                        src = ps_k[0:SC, 0:D].rearrange("p (h d) -> p h d", d=dh)
                        if dh == 16:
                            eng.wait_ge(init_done, 2)
                        if bv is not None:
                            ins = eng.tensor_tensor(dst, src, bv[0:SC, :].rearrange("p (h d) -> p h d", d=dh), ALU.add)
                        else:
                            ins = eng.tensor_copy(dst, src)
                        ins.then_inc(keys_free, 1)
                    else:
                        for cc in range(per_bank):
                            c = ev[1] * per_bank + cc
                            for h0 in range(0, hpc, 2):
                                src = ps_k[:, cc * S:(cc + 1) * S].unsqueeze(1).to_broadcast([P, 2, S])
                                m = hmask[:, h0:h0 + 2].unsqueeze(2).to_broadcast([P, 2, S])
                                ins = eng.tensor_tensor(k_m[par][:, c * hpc + h0:c * hpc + h0 + 2, :], src, m, ALU.mult)
                        ins.then_inc(keys_free, 1)

                def step(kind, b, par, i):
                    u = unit(kind, b, i)
                    if u and u[2] % 2 == 1:
                        evacuate(eng, "vector", u[0], par, u[2])
                    u = unit(kind, b, i + LOOK)
                    if u:
                        nb, nxt, j = u
                        eng.wait_ge(scores_done, count(NU, nb, j))
                        eng.wait_ge(exp_done, count(NU, nb, j - 4))
                        src = ps_s[:, j % 2, 0:QT_N * G * width].rearrange("p (a k) -> p a k", k=width)
                        eng.tensor_reduce(nmax[:, j % 4, :], src, AX.X, ALU.max, negate=True).then_inc(max_done, 1)
                        if cross:
                            eng.wait_ge(max_done, count(NU, nb, j))
                            eng.wait_ge(exp_done, count(NU, nb, j - 2))
                            eng.tensor_tensor(shifted[:, j % 2, :, :], src,
                                              nmax[:, j % 4, :].unsqueeze(2).to_broadcast([P, QT_N * G, width]),
                                              ALU.add).then_inc(shift_done, 1)
                    u = unit(kind, b, i + LOOK - 1)
                    if u:
                        totals(u[0], u[2])

                def totals(nb, j):
                    eng.wait_ge(exp_done, count(NU, nb, j))
                    eng.wait_ge(norm_done, count(NU, nb, j - 4))
                    if cross:
                        eng.tensor_reduce(total[:, j % 4, :], prob[:, j % 4, :, :], AX.X, ALU.add).then_inc(total_done, 1)
                        eng.wait_ge(total_done, count(NU, nb, j))
                    eng.reciprocal(rtot[:, j % 4, :], total[:, j % 4, :]).then_inc(rtot_done, 1)

                def tail(b, par):
                    eng.wait_ge(out_done, count(NO, b, NG))
                    xb = X[:, bass.ds(b * QT_N, QT_N), :]
                    if bo is not None:
                        bo_add = eng.tensor_tensor(xb, xb, bo[:, :].unsqueeze(1).to_broadcast([P, QT_N, D]), ALU.add)
                        bo_add.then_inc(bias_done, 1)
                        eng.wait_ge(bias_done, b + 1)
                    eng.tensor_tensor(xb, xb, ps_o[:, :].rearrange("p (q d) -> p q d", q=QT_N), ALU.add
                                      ).then_inc(out_free, 1)

                run(step, front, tail, eng)

            @block.scalar
            def _(eng):
                for s, n in ((front_free, NF), (exp_done, NU), (turned_free[0], NU // 2)):
                    eng.sem_inc(s, n)
                eng.sem_inc(out_free, NG)

                def front(b, par, i=None):
                    nb = b + 1
                    for st, evs in sorted(plan.items()):
                        if i is not None and st != i:
                            continue
                        for ring, ev in evs:
                            if ring == "f":
                                event(nb, par, ev)

                def event(nb, par, ev):
                    e = f_at[ev]
                    bank = ps_f[:, e % 2, :]
                    eng.wait_ge(front_done, count(NF, nb, e))
                    if ev[0] == "xt":
                        if affine is None:
                            ins = eng.activation(xt[:, :, :], bank.rearrange("p (c s) -> p c s", c=DT), ACT.Copy)
                        else:
                            for c in range(DT):
                                ins = eng.activation(xt[:, c, :], bank[:, c * S:(c + 1) * S], ACT.Identity,
                                                     bias=affine[1][:, c:c + 1], scale=affine[0][:, c:c + 1])
                    elif ev[0] == "ct":
                        ins = eng.activation(ct[:, :, :], bank[:, 0:DT * SC].rearrange("p (c s) -> p c s", c=DT), ACT.Copy)
                    elif ev[0] == "q":
                        for cc in range(per_bank):
                            c = ev[1] * per_bank + cc
                            if bq is not None:
                                ins = eng.activation(q_t[par][:, c, :], bank[:, cc * S:(cc + 1) * S], ACT.Identity,
                                                     bias=bq[:, c:c + 1], scale=q_scale)
                            elif cc == 0:
                                ins = eng.activation(q_t[par][:, c:c + per_bank, :],
                                                     bank.rearrange("p (c s) -> p c s", c=per_bank), ACT.Copy,
                                                     scale=q_scale)
                    else:
                        if dh == 16:
                            eng.wait_ge(init_done, 2)
                            for vv in range(2):
                                v, n = ev[1] + vv, v_rows[ev[1] + vv][1]
                                ins = eng.activation(v_s[par][0:n, v, :, 0:dh],
                                                     bank[0:n, vv * D:(vv + 1) * D].rearrange("p (h d) -> p h d", d=dh),
                                                     ACT.Copy)
                        else:
                            hh = 512 // dh
                            ins = eng.activation(v_s[par][:, ev[1], ev[2] * hh:(ev[2] + 1) * hh, :],
                                                 bank.rearrange("p (h d) -> p h d", d=dh), ACT.Copy)
                    ins.then_inc(front_free, 1)

                def group_out(b, g):
                    eng.wait_ge(out_done, count(NO, b, g))
                    eng.activation(o_t[:, g, :], ps_o[:, 0:S], ACT.Copy).then_inc(out_free, 1)

                def step(kind, b, par, i):
                    u = unit(kind, b, i)
                    if u and u[2] % 2 == 0:
                        evacuate(eng, "scalar", u[0], par, u[2])
                    if kind != "first" and i % UG == 0 and i >= UG:
                        group_out(b, i // UG - 1)
                    u = unit(kind, b, i + LOOK)
                    if u:
                        nb, nxt, j = u
                        eng.wait_ge(turned, count(NU, nb, j - 4))
                        if cross:
                            eng.wait_ge(shift_done, count(NU, nb, j))
                            eng.activation(prob[:, j % 4, :, :], shifted[:, j % 2, :, :], ACT.Exp).then_inc(exp_done, 1)
                        else:
                            eng.wait_ge(max_done, count(NU, nb, j))
                            eng.wait_ge(rtot_done, count(NU, nb, j - 4))
                            for q in range(QT_N):
                                ins = eng.activation(prob[:, j % 4, q, :], ps_s[:, j % 2, q * width:(q + 1) * width],
                                                     ACT.Exp, bias=nmax[:, j % 4, q:q + 1],
                                                     accum_out=total[:, j % 4, q:q + 1])
                            ins.then_inc(exp_done, 1)

                def tail(b, par):
                    group_out(b, NG - 1)

                run(step, front, tail, eng)

            @block.gpsimd
            def _(eng):
                eng.sem_inc(rstd_done, 1)
                eng.sem_inc(norm_done, NU)

                def front(b, par, i=None):
                    nb = b + 1
                    if i is None or i == 0:
                        eng.wait_ge(var_done, count(1, nb, 0))
                        eng.tensor_tensor(veps[:, :], mv[:, :, 1], eps[:, 0:QT_N], ALU.add).then_inc(veps_done, 1)
                        eng.wait_ge(veps_done, nb + 1)
                        eng.tensor_tensor(rstd[:, :], veps[:, :], neg_half[:, 0:QT_N], ALU.pow).then_inc(rstd_done, 1)

                def step(kind, b, par, i):
                    u = unit(kind, b, i + LOOK - 1)
                    if not u:
                        return
                    nb, nxt, j = u
                    eng.wait_ge(rtot_done, count(NU, nb, j))
                    eng.tensor_tensor(prob[:, j % 4, :, :], prob[:, j % 4, :, :],
                                      rtot[:, j % 4, :].unsqueeze(2).to_broadcast([P, QT_N * G, width]), ALU.mult
                                      ).then_inc(norm_done, 1)

                run(step, front, lambda b, par: None, eng)

            @block.tensor
            def _(eng):
                for s, n in ((front_done, NF), (keys_done, NK), (scores_done, NU), (turned, NU), (out_done, NO)):
                    eng.sem_inc(s, n)
                for s, v in w_landed:
                    eng.wait_ge(s, v)

                def front(b, par, i=None):
                    nb = b + 1
                    for st, evs in sorted(plan.items()):
                        if i is not None and st != i:
                            continue
                        for ring, ev in evs:
                            if ring == "f":
                                front_event(nb, par, ev)
                            else:
                                key_event(nb, par, ev)

                def project(out, w, c0, n, rhs, kt_rows=P):
                    for t in range(DT):
                        ins = eng.matmul(out, w[:, t, c0:c0 + n], rhs[:, t, :], start=(t == 0), stop=(t == DT - 1))
                    return ins

                def front_event(nb, par, ev):
                    e = f_at[ev]
                    bank = ps_f[:, e % 2, :]
                    before = e - 2 if e >= 2 else max(p for p in range(NF) if p % 2 == e % 2) - NF
                    eng.wait_ge(front_free, count(NF, nb, before))
                    if ev[0] == "xt":
                        eng.wait_ge(xn_done, count(QT_N, nb, QT_N - 1))
                        for c in range(DT):
                            for q in range(QT_N):
                                ins = eng.transpose(bank[:, c * S + q * P:c * S + (q + 1) * P],
                                                    xn[:, q, c * P:(c + 1) * P], ident[:, :])
                    elif ev[0] == "ct":
                        eng.wait_ge(ctx_landed[par], nb * 8 + 16 - 8 * par)
                        for c in range(DT):
                            ins = eng.transpose(bank[:, c * SC:(c + 1) * SC], ctx_in[0:SC, par, c * P:(c + 1) * P],
                                                ident[0:SC, 0:SC])
                    elif ev[0] == "q":
                        eng.wait_ge(front_free, count(NF, nb, f_at[("xt", 0)]))
                        for cc in range(per_bank):
                            ins = project(bank[:, cc * S:(cc + 1) * S], wq, (ev[1] * per_bank + cc) * P, P, xt)
                    else:
                        eng.wait_ge(front_free, count(NF, nb, f_at[("xt", 0)]))
                        if dh == 16:
                            pieces = [(v_rows[ev[1] + vv], vv * D, 0, D) for vv in range(2)]
                        else:
                            pieces = [(v_rows[ev[1]], 0, ev[2] * 512, 512)]
                        for (r0, n), o, c0, w in pieces:
                            for t in range(DT):
                                ins = eng.matmul(bank[0:n, o:o + w], xt[:, t, r0:r0 + n], wv[:, t, c0:c0 + w],
                                                 start=(t == 0), stop=(t == DT - 1))
                    ins.then_inc(front_done, 1)

                def key_event(nb, par, ev):
                    e = kev.index(ev)
                    eng.wait_ge(keys_free, count(NK, nb, e - 1))
                    if cross:
                        eng.wait_ge(front_free, count(NF, nb, f_at[("ct", 0)]))
                    else:
                        eng.wait_ge(front_free, count(NF, nb, f_at[("xt", 0)]))
                    if cross and ev[0] == "k":
                        for c in range(nct):
                            ins = project(ps_k[:, c * SC:(c + 1) * SC], wk, c * P, P, ct)
                    elif cross:
                        for t in range(DT):
                            ins = eng.matmul(ps_k[0:SC, 0:D], ct[:, t, :], wv[:, t, :], start=(t == 0), stop=(t == DT - 1))
                    else:
                        for cc in range(per_bank):
                            ins = project(ps_k[:, cc * S:(cc + 1) * S], wk, (ev[1] * per_bank + cc) * P, P, xt)
                    ins.then_inc(keys_done, 1)

                def scores(nb, par, j):
                    if cross:
                        eng.wait_ge(shift_done, count(NU, nb, j - 2))
                    else:
                        eng.wait_ge(exp_done, count(NU, nb, j - 2))
                    c = j * G // hpc
                    last_k = 0 if cross else c // per_bank
                    eng.wait_ge(keys_free, count(NK, nb, last_k))
                    eng.wait_ge(front_free, count(NF, nb, f_at[("q", c // per_bank)]))
                    for q in range(QT_N):
                        n = G * width
                        out = ps_s[:, j % 2, q * n:(q + 1) * n]
                        k0 = first_key[q]
                        if cross:
                            rhs = k_m[par][:, j * G:(j + 1) * G, :].rearrange("p h k -> p (h k)")
                        else:
                            rhs = k_m[par][:, j, k0:k0 + width]
                        ins = eng.matmul(out, q_t[par][:, c, q * P:(q + 1) * P], rhs, start=True, stop=not windowed)
                        if windowed:
                            ins = eng.matmul(out, identb[:, :], wmask[:, q, :], start=False, stop=True)
                    ins.then_inc(scores_done, 1)

                def turn(b, par, j):
                    eng.wait_ge(norm_done, count(NU, b, j))
                    eng.wait_ge(turned_free[j % 2], count(NU // 2, b, j // 2 - 1))
                    if cross:
                        for g in range(G):
                            for q in range(QT_N):
                                o = (g * QT_N + q) * P
                                ins = eng.transpose(ps_t[0:SC, j % 2, o:o + P], prob[:, j % 4, q * G + g, :], ident[:, :])
                    else:
                        for c, (k0, n) in enumerate(chunks):
                            for q in range(QT_N):
                                o = (c * QT_N + q) * P
                                ins = eng.transpose(ps_t[0:n, j % 2, o:o + P], prob[:, j % 4, q, k0:k0 + n], ident[:, :])
                    ins.then_inc(turned, 1)

                def values(b, par, g):
                    for p2 in range(2):
                        last = [j for j in range(g * UG, (g + 1) * UG) if j % 2 == p2][-1]
                        eng.wait_ge(turned_free[p2], count(NU // 2, b, last // 2))
                    if g == 0:
                        if cross:
                            eng.wait_ge(keys_free, count(NK, b, 1))
                        else:
                            eng.wait_ge(front_free, count(NF, b, NF - 1))
                        eng.wait_ge(out_free, count(NO, b - 1, NO - 1))
                    else:
                        eng.wait_ge(out_free, count(NO, b, g - 1))
                    pt = prob_t[g % 2]
                    combos = []
                    if cross:
                        combos = [(0, S, 0, SC, 0, True, True)]
                    elif windowed:
                        for q in range(QT_N):
                            for c in range(NC):
                                combos.append((q * P, P, q * NC + c, chunks[c][1], (c * QT_N + q) * P, c == 0, c == NC - 1))
                    else:
                        for c in range(NC):
                            combos.append((0, S, c, P, c * S, c == 0, c == NC - 1))
                    for oc, w, v, n, po, st, sp in combos:
                        for hh in range(HG):
                            h = g * HG + hh
                            r, sub = hh // G, hh % G
                            o = po + sub * S if cross else po
                            ins = eng.matmul(ps_o[hh * dv:(hh + 1) * dv, oc:oc + w], v_s[par][0:n, v, h, :],
                                             pt[0:n, r, o:o + w], start=st, stop=sp)
                    ins.then_inc(out_done, 1)

                def step(kind, b, par, i):
                    u = unit(kind, b, i)
                    if u:
                        turn(u[0], par, u[2])
                    if kind != "first" and i % UG == 0 and i >= UG:
                        values(b, par, i // UG - 1)
                    u = unit(kind, b, i + LOOK)
                    if u:
                        nb, nxt, j = u
                        scores(nb, (par + nxt) % 2, j)

                def tail(b, par):
                    values(b, par, NG - 1)
                    eng.wait_ge(out_free, count(NO, b, NG - 1))
                    for q in range(QT_N):
                        for g in range(NG):
                            ins = eng.matmul(ps_o[:, q * D:(q + 1) * D], o_t[:, g, q * P:(q + 1) * P], wo[:, g, :],
                                             start=(g == 0), stop=(g == NG - 1))
                    ins.then_inc(out_done, 1)

                run(step, front, tail, eng)
        nc.clear_and_free_semaphores(used)
        nc.all_engine_barrier()


EXPERTS = 8
TOP = 2
MAX_BLOCKS = TILES * TOP + EXPERTS
ROWS = (MAX_BLOCKS + 2) * P


def moe(nc, name, env, hidden, gated, wr, w_landed, wa_dram, wb_dram, wd_dram, b1_dram=None, b2_dram=None,
        rows_dram=None, outs_dram=None, zeroed=()):
    X, ident, neg_half = env["X"], env["ident"], env["neg_half"]
    HC = (hidden + 3) // 4 * 2
    halves = [(0, HC), (HC, hidden - HC)]
    ktiles = [[(o + k, min(P, n - k)) for k in range(0, n, P)] for o, n in halves]
    KT = len(ktiles[0])
    NH = 2 if gated else 1
    n_w = 2 * KT + NH + (0 if gated else 2)

    used = []

    def sem(n):
        used.append(nc.alloc_semaphore(f"{name}_{n}"))
        return used[-1]

    with ExitStack() as stack:
        def sb(n, shape, dt=F32):
            return stack.enter_context(nc.sbuf_tensor(f"{name}_{n}", shape, dt))

        gate = sb("gate", [P, TILES, TOP])
        slot = sb("slot", [P, TILES, TOP], I32)
        blocks_i = sb("blocks_i", [P, EXPERTS], I32)
        base_i = sb("base_i", [P, EXPERTS + 1], I32)
        rows_landed, y_stored = sem("rows_landed"), sem("y_stored")
        with ExitStack() as inner:
            def tb(n, shape, dt=F32):
                return inner.enter_context(nc.sbuf_tensor(f"{name}_{n}", shape, dt))

            ps_x = inner.enter_context(nc.psum_tensor(f"{name}_ps_xt", [P, 2, 512], F32))
            ps_l = inner.enter_context(nc.psum_tensor(f"{name}_ps_l", [P, 512], F32))
            ps_c = inner.enter_context(nc.psum_tensor(f"{name}_ps_c", [P, 2, 512], F32))
            stats = tb("stats", [P, TILES, 6])
            mv = tb("mv", [P, TILES, 2])
            veps = tb("veps", [P, TILES])
            halfs = tb("halfs", [P, TILES])
            rstd = tb("rstd", [P, TILES])
            xn = tb("xn", [P, TILES, D])
            xt = tb("xt", [P, 2, DT, P])
            logits = tb("logits", [P, TILES, EXPERTS])
            top = tb("top", [P, TILES, 8])
            index = tb("index", [P, TILES, 8], U32)
            index_f = tb("index_f", [P, TILES, TOP])
            experts = tb("experts", [P, EXPERTS])
            chosen = tb("chosen", [P, TOP, TILES, EXPERTS])
            both = tb("both", [P, TILES, EXPERTS])
            before = tb("before", [P, P])
            ones = tb("ones", [P, P])
            per_tile = tb("per_tile", [P, EXPERTS, TILES])
            running = tb("running", [P, EXPERTS, TILES])
            carry = tb("carry", [P, EXPERTS, TILES])
            blocks_f = tb("blocks_f", [P, EXPERTS])
            cum_f = tb("cum_f", [P, EXPERTS + 1])
            ones8 = tb("ones8", [P, EXPERTS])
            place = tb("place", [P, TILES, EXPERTS])
            picked = tb("picked", [P, TOP, TILES, EXPERTS])
            slot_f = tb("slot_f", [P, TOP, TILES])
            ediff = tb("ediff", [P, TILES])
            consts = sem("consts")
            link_v = sem("link_v")
            stats_done, rstd_done, xn_done = sem("stats"), sem("rstd"), sem("xn")
            turned, xt_done, logits_done = sem("turned"), sem("xt"), sem("logits")
            diff_done, exp_done = sem("diff"), sem("exp")
            both_done, counted, slot_done = sem("both"), sem("counted"), sem("slot")
            scattered = sem("scattered")
            with nc.Block() as block:
                @block.gpsimd
                def _(eng):
                    eng.memset(halfs[:, :], -0.5).then_inc(consts, 1)
                    eng.memset(ones[:, :], 1.0).then_inc(consts, 1)
                    eng.memset(before[:, :], 1.0).then_inc(consts, 1)
                    eng.iota(experts[:, :], pattern=[[1, EXPERTS]], base=0, channel_multiplier=0,
                             allow_small_or_imprecise_dtypes=True).then_inc(consts, 1)
                    eng.memset(ones8[:, :], 1.0).then_inc(consts, 1)
                    eng.wait_ge(consts, 5)
                    eng.affine_select(out=before[:, :], in_=before[:, :], compare_op=ALU.is_gt, fill=0.0,
                                      base=0, pattern=[[1, P]], channel_multiplier=-1).then_inc(consts, 1)
                    eng.wait_ge(stats_done, TILES + 1)
                    eng.tensor_tensor(rstd[:, :], veps[:, :], halfs[:, :], ALU.pow).then_inc(rstd_done, 1)
                    eng.wait_ge(slot_done, 1)
                    eng.wait_ge(xn_done, TILES)
                    for s, v in zeroed:
                        eng.wait_ge(s, v)
                    for t in range(TILES):
                        for k in range(TOP):
                            eng.indirect_dma_start(rows_dram, bass.IndirectOffsetOnAxis(ap=slot[:, t, k:k + 1], axis=0),
                                                   xn[:, t, :], None).then_inc(scattered, 16)
                    eng.wait_ge(scattered, 16 * TILES * TOP)

                @block.vector
                def _(eng):
                    n = [0]

                    def linked(ins):
                        n[0] += 1
                        ins.then_inc(link_v, 1)
                        eng.wait_ge(link_v, n[0])

                    for t in range(TILES):
                        ins = eng.bn_stats(stats[:, t, :], X[:, t, :])
                    linked(ins)
                    for t in range(TILES):
                        ins = eng.bn_aggr(mv[:, t, :], stats[:, t, :]).then_inc(stats_done, 1)
                    eng.wait_ge(stats_done, TILES)
                    eng.tensor_scalar(veps[:, :], mv[:, :, 1], LN_EPS, None, ALU.add).then_inc(stats_done, 1)
                    eng.wait_ge(rstd_done, 1)
                    for t in range(TILES):
                        eng.tensor_scalar(xn[:, t, :], X[:, t, :], mv[:, t, 0:1], rstd[:, t:t + 1],
                                          ALU.subtract, ALU.mult).then_inc(xn_done, 1)
                    eng.wait_ge(logits_done, TILES)
                    linked(eng.tensor_copy(logits[:, :, :], ps_l[:, 0:TILES * EXPERTS].rearrange("p (t e) -> p t e", e=EXPERTS)))
                    for t in range(TILES):
                        ins = eng.max(top[:, t, :], logits[:, t, :])
                    linked(ins)
                    eng.tensor_tensor(ediff[:, :], top[:, :, 1], top[:, :, 0], ALU.subtract).then_inc(diff_done, 1)
                    for t in range(TILES):
                        ins = eng.max_index(index[:, t, :], top[:, t, :], logits[:, t, :])
                    linked(ins)
                    linked(eng.tensor_copy(index_f[:, :, :], index[:, :, 0:TOP]))
                    eng.wait_ge(consts, 6)
                    for k in range(TOP):
                        ins = eng.tensor_tensor(chosen[:, k, :, :], experts[:, :].unsqueeze(1).to_broadcast([P, TILES, EXPERTS]),
                                                index_f[:, :, k].unsqueeze(2).to_broadcast([P, TILES, EXPERTS]), ALU.is_equal)
                    linked(ins)
                    eng.tensor_tensor(both[:, :, :], chosen[:, 0, :, :], chosen[:, 1, :, :], ALU.add).then_inc(both_done, 1)
                    eng.wait_ge(exp_done, 1)
                    linked(eng.tensor_scalar(ediff[:, :], gate[:, :, 1], 1.0, None, ALU.add))
                    linked(eng.reciprocal(gate[:, :, 0], ediff[:, :]))
                    linked(eng.tensor_tensor(ediff[:, :], gate[:, :, 0], gate[:, :, 1], ALU.mult))
                    linked(eng.tensor_copy(gate[:, :, 1], ediff[:, :]))
                    eng.wait_ge(counted, 2)
                    linked(eng.tensor_copy(per_tile[:, :, :], ps_c[:, 1, 0:TILES * EXPERTS].rearrange("p (t e) -> p e t", e=EXPERTS)))
                    linked(eng.memset(carry[:, :, :], 1.0))
                    linked(eng.memset(carry[:, :, 0:1], 0.0))
                    linked(eng.tensor_tensor_scan(running[:, :, :].rearrange("p e t -> p (e t)"),
                                                  carry[:, :, :].rearrange("p e t -> p (e t)"),
                                                  per_tile[:, :, :].rearrange("p e t -> p (e t)"), 0.0, ALU.mult, ALU.add))
                    linked(eng.tensor_scalar(blocks_i[:, :], running[:, :, TILES - 1], float(P - 1), None, ALU.add))
                    linked(eng.tensor_scalar(blocks_i[:, :], blocks_i[:, :], 7, None, ALU.logical_shift_right))
                    linked(eng.tensor_copy(blocks_f[:, :], blocks_i[:, :]))
                    linked(eng.tensor_scalar(blocks_f[:, :], blocks_f[:, :], 1.0, None, ALU.max))
                    linked(eng.tensor_copy(blocks_i[:, :], blocks_f[:, :]))
                    linked(eng.memset(cum_f[:, :], 0.0))
                    linked(eng.tensor_tensor_scan(cum_f[:, 1:EXPERTS + 1], ones8[:, :], blocks_f[:, :], 0.0, ALU.mult, ALU.add))
                    linked(eng.tensor_copy(base_i[:, :], cum_f[:, :]))
                    linked(eng.tensor_tensor(running[:, :, :], running[:, :, :], per_tile[:, :, :], ALU.subtract))
                    linked(eng.scalar_tensor_tensor(out=running[:, :, :],
                                                    in0=cum_f[:, 0:EXPERTS].unsqueeze(2).to_broadcast([P, EXPERTS, TILES]),
                                                    scalar=float(P), in1=running[:, :, :], op0=ALU.mult, op1=ALU.add))
                    linked(eng.tensor_tensor(place[:, :, :], running[:, :, :].rearrange("p e t -> p t e"),
                                             ps_c[:, 0, 0:TILES * EXPERTS].rearrange("p (t e) -> p t e", e=EXPERTS), ALU.add))
                    linked(eng.tensor_tensor(picked[:, :, :, :], chosen[:, :, :, :],
                                             place[:, :, :].unsqueeze(1).to_broadcast([P, TOP, TILES, EXPERTS]), ALU.mult))
                    linked(eng.tensor_reduce(slot_f[:, :, :], picked[:, :, :, :], AX.X, ALU.add))
                    eng.tensor_copy(slot[:, :, :], slot_f[:, :, :].rearrange("p k t -> p t k")).then_inc(slot_done, 1)

                @block.scalar
                def _(eng):
                    for t in range(TILES):
                        eng.wait_ge(turned, t + 1)
                        if t >= 2:
                            eng.wait_ge(logits_done, t - 1)
                        eng.activation(xt[:, t % 2, :, :], ps_x[:, t % 2, 0:D].rearrange("p (c s) -> p c s", c=DT),
                                       ACT.Copy).then_inc(xt_done, 1)
                    eng.wait_ge(diff_done, 1)
                    eng.activation(gate[:, :, 1], ediff[:, :], ACT.Exp).then_inc(exp_done, 1)

                @block.tensor
                def _(eng):
                    for s, v in w_landed:
                        eng.wait_ge(s, v)

                    def turn(t):
                        eng.wait_ge(xn_done, t + 1)
                        if t >= 2:
                            eng.wait_ge(xt_done, t - 1)
                        for c in range(DT):
                            ins = eng.transpose(ps_x[:, t % 2, c * P:(c + 1) * P], xn[:, t, c * P:(c + 1) * P], ident[:, :])
                        ins.then_inc(turned, 1)

                    turn(0)
                    for t in range(TILES):
                        if t + 1 < TILES:
                            turn(t + 1)
                        eng.wait_ge(xt_done, t + 1)
                        for c in range(DT):
                            ins = eng.matmul(ps_l[:, t * EXPERTS:(t + 1) * EXPERTS], xt[:, t % 2, c, :], wr[:, c, :],
                                             start=(c == 0), stop=(c == DT - 1))
                        ins.then_inc(logits_done, 1)
                    eng.wait_ge(both_done, 1)
                    for i, m in enumerate((before, ones)):
                        eng.matmul(ps_c[:, i, 0:TILES * EXPERTS], m[:, :], both[:, :, :].rearrange("p t e -> p (t e)"),
                                   start=True, stop=True).then_inc(counted, 1)

        with ExitStack() as inner:
            def tb(n, shape, dt=F32):
                return inner.enter_context(nc.sbuf_tensor(f"{name}_{n}", shape, dt))

            ps_h = inner.enter_context(nc.psum_tensor(f"{name}_ps_h", [P, 2, NH, 512], F32))
            ps_t = inner.enter_context(nc.psum_tensor(f"{name}_ps_t", [P, 2, 512], F32))
            ps_y = inner.enter_context(nc.psum_tensor(f"{name}_ps_y", [P, 512], F32))
            ps_x = inner.enter_context(nc.psum_tensor(f"{name}_ps_x", [P, 512], F32))
            w_up = [tb(f"w_up{i}", [P, NH, DT, hidden]) for i in range(2)]
            w_down = [tb(f"w_down{i}", [P, 2 * KT, D]) for i in range(2)]
            b_up = [tb(f"b_up{i}", [P, hidden]) for i in range(2)] if not gated else None
            b_down = [tb(f"b_down{i}", [P, D]) for i in range(2)] if not gated else None
            rows = tb("rows", [P, D])
            rows_t = tb("rows_t", [P, DT, P])
            mid = tb("mid", [P, 2, HC])
            hid = tb("hid", [P, 2, HC])
            hid_t = tb("hid_t", [P, 2, KT, P])
            y = tb("y", [P, D])
            weights_landed = [sem("weights0"), sem("weights1")]
            rows_turned, rows_ready = sem("rows_turned"), sem("rows_ready")
            up_done, mid_done, hid_done = sem("up"), sem("mid"), sem("hid")
            hid_turned, hid_t_done = sem("hid_turned"), sem("hid_t")
            down_done, y_done = sem("down"), sem("y")

            def experts_loop(eng, body):
                with eng.Fori(0, EXPERTS // 2) as pair:
                    for par in range(2):
                        e = pair * 2 + par
                        count_e = eng.value_load(blocks_i[0:1, bass.ds(e, 1)], min_val=1, max_val=TILES)
                        base_e = eng.value_load(base_i[0:1, bass.ds(e, 1)], min_val=0, max_val=MAX_BLOCKS)
                        with eng.Fori(0, count_e) as i:
                            n = nc.s_assert_within(base_e + i, 0, MAX_BLOCKS - 1, skip_runtime_bounds_check_because=
                                                   "the experts' block counts sum to MAX_BLOCKS at most")
                            body(n, par, pair)

            with nc.Block() as block:
                @block.sync
                def _(eng):
                    eng.sem_inc(y_stored, 16)

                    def load(n):
                        eng.dma_start(rows[:, :], rows_dram[bass.ds(n * P, P), :]).then_inc(rows_landed, 16)

                    load(0)
                    eng.wait_ge(rows_turned, count(1, 0, 0))
                    load(1)

                    def body(n, par, pair):
                        eng.wait_ge(rows_turned, count(1, n + 1, 0))
                        load(n + 2)
                        eng.wait_ge(y_done, count(1, n, 0))
                        eng.dma_start(outs_dram[bass.ds(n * P, P), :], y[:, :]).then_inc(y_stored, 16)

                    experts_loop(eng, body)

                @block.gpsimd
                def _(eng):
                    def load(e, par):
                        s = weights_landed[par]
                        one = lambda d: d[bass.ds(e, 1)].rearrange("a r c -> (a r) c")
                        for j, d in enumerate((wa_dram, wb_dram)[:NH]):
                            eng.dma_start(w_up[par][:, j, :, :], one(d).rearrange("(c p) h -> p c h", p=P)).then_inc(s, 16)
                        for c in range(2):
                            for k, (r0, n) in enumerate(ktiles[c]):
                                eng.dma_start(w_down[par][0:n, c * KT + k, :], one(wd_dram)[r0:r0 + n, :]).then_inc(s, 16)
                        if not gated:
                            eng.dma_start(b_up[par][:, :], b1_dram[bass.ds(e, 1), :].to_broadcast([P, hidden])).then_inc(s, 16)
                            eng.dma_start(b_down[par][:, :], b2_dram[bass.ds(e, 1), :].to_broadcast([P, D])).then_inc(s, 16)

                    load(0, 0)
                    load(1, 1)
                    with eng.Fori(0, EXPERTS // 2 - 1) as pair:
                        for par in range(2):
                            e = pair * 2 + par
                            done = eng.value_load(base_i[0:1, bass.ds(e + 1, 1)], min_val=1, max_val=MAX_BLOCKS)
                            eng.wait_ge(y_done, count(1, done - 1, 0))
                            load(e + 2, par)

                @block.tensor
                def _(eng):
                    for s, n in ((rows_turned, 1), (up_done, 2), (hid_turned, 2), (down_done, 1)):
                        eng.sem_inc(s, n)

                    def turn_rows(n):
                        eng.wait_ge(rows_landed, (n + 1) * 16)
                        eng.wait_ge(rows_ready, count(1, n - 1, 0))
                        for c in range(DT):
                            ins = eng.transpose(ps_x[:, c * P:(c + 1) * P], rows[:, c * P:(c + 1) * P], ident[:, :])
                        ins.then_inc(rows_turned, 1)

                    def up(n, par, c):
                        eng.wait_ge(hid_done if gated else mid_done, count(2, n - 1, c))
                        o, w = halves[c]
                        for j in range(NH):
                            for t in range(DT):
                                ins = eng.matmul(ps_h[:, c, j, 0:w], rows_t[:, t, :], w_up[par][:, j, t, o:o + w],
                                                 start=(t == 0), stop=(t == DT - 1))
                        ins.then_inc(up_done, 1)

                    def turn_hidden(n, c):
                        eng.wait_ge(hid_done, count(2, n, c))
                        eng.wait_ge(hid_t_done, count(2, n - 1, c))
                        for k, (r0, w) in enumerate(ktiles[c]):
                            o = r0 - halves[c][0]
                            ins = eng.transpose(ps_t[0:w, c, k * P:(k + 1) * P], hid[:, c, o:o + w], ident[:, :])
                        ins.then_inc(hid_turned, 1)

                    def down(n, par, c):
                        eng.wait_ge(hid_t_done, count(2, n, c))
                        if c == 0:
                            eng.wait_ge(y_done, count(1, n - 1, 0))
                        for k, (r0, w) in enumerate(ktiles[c]):
                            ins = eng.matmul(ps_y[:, 0:D], hid_t[0:w, c, k, :], w_down[par][0:w, c * KT + k, :],
                                             start=(c == 0 and k == 0), stop=(c == 1 and k == KT - 1))
                        if c == 1:
                            ins.then_inc(down_done, 1)

                    turn_rows(0)

                    def body(n, par, pair):
                        eng.wait_ge(weights_landed[par], (pair + 1) * (16 * n_w))
                        eng.wait_ge(rows_ready, count(1, n, 0))
                        up(n, par, 0)
                        up(n, par, 1)
                        turn_hidden(n, 0)
                        turn_rows(n + 1)
                        down(n, par, 0)
                        turn_hidden(n, 1)
                        down(n, par, 1)

                    experts_loop(eng, body)

                @block.scalar
                def _(eng):
                    eng.sem_inc(rows_ready, 1)
                    eng.sem_inc(mid_done if gated else hid_done, 2)

                    def rows_out(n):
                        eng.wait_ge(rows_turned, count(1, n, 0))
                        eng.activation(rows_t[:, :, :], ps_x[:, 0:D].rearrange("p (c s) -> p c s", c=DT),
                                       ACT.Copy).then_inc(rows_ready, 1)

                    rows_out(0)

                    def body(n, par, pair):
                        for c in range(2):
                            w = halves[c][1]
                            if gated:
                                eng.wait_ge(up_done, count(2, n, c))
                                eng.wait_ge(hid_done, count(2, n - 1, c))
                                eng.activation(mid[:, c, 0:w], ps_h[:, c, 0, 0:w], ACT.Silu).then_inc(mid_done, 1)
                            else:
                                eng.wait_ge(mid_done, count(2, n, c))
                                eng.wait_ge(hid_turned, count(2, n - 1, c))
                                eng.activation(hid[:, c, 0:w], mid[:, c, 0:w], ACT.Gelu).then_inc(hid_done, 1)
                        rows_out(n + 1)

                    experts_loop(eng, body)

                @block.vector
                def _(eng):
                    eng.sem_inc(hid_done if gated else mid_done, 2)
                    eng.sem_inc(hid_t_done, 2)
                    eng.sem_inc(y_done, 1)

                    def first(n, par, c):
                        w = halves[c][1]
                        eng.wait_ge(up_done, count(2, n, c))
                        if gated:
                            eng.wait_ge(mid_done, count(2, n, c))
                            eng.wait_ge(hid_turned, count(2, n - 1, c))
                            eng.tensor_tensor(hid[:, c, 0:w], mid[:, c, 0:w], ps_h[:, c, 1, 0:w], ALU.mult).then_inc(hid_done, 1)
                        else:
                            eng.wait_ge(hid_done, count(2, n - 1, c))
                            o = halves[c][0]
                            eng.tensor_tensor(mid[:, c, 0:w], ps_h[:, c, 0, 0:w], b_up[par][:, o:o + w], ALU.add).then_inc(mid_done, 1)

                    def turned(n, c):
                        eng.wait_ge(hid_turned, count(2, n, c))
                        if c == 0:
                            eng.wait_ge(down_done, count(1, n - 1, 0))
                        full = sum(w == P for _, w in ktiles[c])
                        ins = eng.tensor_copy(hid_t[:, c, 0:full, :], ps_t[:, c, 0:full * P].rearrange("p (k s) -> p k s", s=P))
                        if full < KT:
                            w = ktiles[c][-1][1]
                            ins = eng.tensor_copy(hid_t[0:w, c, full, :], ps_t[0:w, c, full * P:KT * P])
                        ins.then_inc(hid_t_done, 1)

                    def body(n, par, pair):
                        if not gated:
                            eng.wait_ge(weights_landed[par], (pair + 1) * (16 * n_w))
                        first(n, par, 0)
                        first(n, par, 1)
                        turned(n, 0)
                        turned(n, 1)
                        eng.wait_ge(down_done, count(1, n, 0))
                        eng.wait_ge(y_stored, (n + 1) * 16)
                        if gated:
                            eng.tensor_copy(y[:, :], ps_y[:, 0:D]).then_inc(y_done, 1)
                        else:
                            eng.tensor_tensor(y[:, :], ps_y[:, 0:D], b_down[par][:, :], ALU.add).then_inc(y_done, 1)

                    experts_loop(eng, body)

        with ExitStack() as inner:
            got = inner.enter_context(nc.sbuf_tensor(f"{name}_got", [P, TILES, TOP, D], F32))
            gathered = [sem(f"gathered{i}") for i in range(TILES)]
            first_added, carried = sem("first_added"), sem("carried")
            carrier = inner.enter_context(nc.sbuf_tensor(f"{name}_carrier", [P, 1], F32))
            with nc.Block() as block:
                @block.gpsimd
                def _(eng):
                    last = eng.value_load(base_i[0:1, EXPERTS:EXPERTS + 1], min_val=EXPERTS, max_val=MAX_BLOCKS)
                    eng.wait_ge(y_stored, (last + 1) * 16)
                    eng.wait_ge(rows_landed, (last + 2) * 16)
                    eng.tensor_tensor(carrier[:, :], gate[:, 0, 0:1], gate[:, 0, 0:1], ALU.add).then_inc(carried, 1)
                    eng.wait_ge(carried, 1)
                    for t in range(TILES):
                        for k in range(TOP):
                            eng.indirect_dma_start(got[:, t, k, :], None, outs_dram,
                                                   bass.IndirectOffsetOnAxis(ap=slot[:, t, k:k + 1], axis=0)
                                                   ).then_inc(gathered[t], 16)

                @block.vector
                def _(eng):
                    def second(t):
                        eng.wait_ge(first_added, t + 1)
                        eng.scalar_tensor_tensor(out=X[:, t, :], in0=got[:, t, 1, :], scalar=gate[:, t, 1:2],
                                                 in1=X[:, t, :], op0=ALU.mult, op1=ALU.add)

                    for t in range(TILES):
                        eng.wait_ge(gathered[t], 16 * TOP)
                        eng.scalar_tensor_tensor(out=X[:, t, :], in0=got[:, t, 0, :], scalar=gate[:, t, 0:1],
                                                 in1=X[:, t, :], op0=ALU.mult, op1=ALU.add).then_inc(first_added, 1)
                        if t >= 1:
                            second(t - 1)
                    second(TILES - 1)
    nc.clear_and_free_semaphores(used)
    nc.all_engine_barrier()


OUT_NAME = "out_0_dram"


def decoder(nc, a):
    with ExitStack() as stack:
        def sb(n, shape, dt=F32):
            return stack.enter_context(nc.sbuf_tensor(n, shape, dt))

        def sem(n):
            return nc.alloc_semaphore(n)

        X = sb("X", [P, TILES, D])
        ident, identb = sb("ident", [P, P]), sb("identb", [P, P], BF16)
        hmask16, hmask64 = sb("hmask16", [P, 8]), sb("hmask64", [P, 2])
        wmask = sb("wmask", [P, QT_N, S - HALF_WINDOW], BF16)
        neg_half, eps = sb("neg_half", [P, QT_N]), sb("eps", [P, QT_N])
        env = dict(X=X, ident=ident, identb=identb, hmask16=hmask16, hmask64=hmask64, wmask=wmask, neg_half=neg_half, eps=eps)
        zero = sb("zero", [P, 1, D])
        wq0, wk0, wv0 = sb("wq0", [P, DT, D]), sb("wk0", [P, DT, D]), sb("wv0", [P, DT, D])
        wo0, bo0 = sb("wo0", [P, 4, D]), sb("bo0", [P, D])
        wq1, wk1, wv1 = sb("wq1", [P, DT, D]), sb("wk1", [P, DT, D]), sb("wv1", [P, DT, D])
        wo1, bo1, bv1 = sb("wo1", [P, 4, D]), sb("bo1", [P, D]), sb("bv1", [P, D])
        bq1, bq1s, bk1 = sb("bq1", [P, DT]), sb("bq1s", [P, DT]), sb("bk1", [P, DT])
        wr0, wr1 = sb("wr0", [P, DT, EXPERTS]), sb("wr1", [P, DT, EXPERTS])
        wq3, wk3, wv3 = sb("wq3", [P, DT, D]), sb("wk3", [P, DT, D]), sb("wv3", [P, DT, D])
        wo3, bo3 = sb("wo3", [P, 4, D]), sb("bo3", [P, D])
        gamma, beta = sb("gamma", [P, DT]), sb("beta", [P, DT])

        consts, cleared, x_first, x_rest = sem("consts"), sem("cleared"), sem("x_first"), sem("x_rest")
        w0_landed, w1_landed, w3_landed = sem("w0_landed"), sem("w1_landed"), sem("w3_landed")
        wr_landed, ln_landed = sem("wr_landed"), sem("ln_landed")
        bias_scaled, zeroed, stored = sem("bias_scaled"), sem("zeroed"), sem("stored")
        rows_dram = nc.dram_tensor("expert_rows", [ROWS, D], F32, kind="Internal").ap()
        outs_dram = nc.dram_tensor("expert_outs", [ROWS, D], F32, kind="Internal").ap()

        x_v = a["x"].rearrange("b (q p) d -> p (b q) d", p=P)
        out_v = a["out"].rearrange("b (q p) d -> p (b q) d", p=P)

        def tiled(w):
            return w.rearrange("(t p) n -> p t n", p=P)

        def padded(eng, dst, w, s):
            for j in range(4):
                eng.dma_start(dst[32 * j:32 * j + 16, :, :], w.rearrange("(g j d) n -> j d g n", j=4, d=16)[j]).then_inc(s, 16)

        with nc.Block() as block:
            @block.vector
            def _(eng):
                for m in (wo0, wo1, wo3, wq3, wk3, wv3):
                    eng.memset(m[:, :, :], 0.0).then_inc(cleared, 1)
                eng.memset(zero[:, :, :], 0.0).then_inc(cleared, 1)

            @block.gpsimd
            def _(eng):
                n = [0]

                def linked(ins):
                    n[0] += 1
                    ins.then_inc(consts, 1)
                    eng.wait_ge(consts, n[0])

                for m in (ident, identb):
                    linked(eng.memset(m[:, :], 0.0))
                    linked(eng.affine_select(out=m[:, :], in_=m[:, :], compare_op=ALU.not_equal, fill=1.0, base=0,
                                             pattern=[[-1, P]], channel_multiplier=1))
                for m, w in ((hmask16, 16), (hmask64, 64)):
                    linked(eng.memset(m[:, :], 1.0))
                    linked(eng.affine_select(out=m[:, :], in_=m[:, :], compare_op=ALU.is_ge, fill=0.0, base=0,
                                             pattern=[[-w, P // w]], channel_multiplier=1))
                    linked(eng.affine_select(out=m[:, :], in_=m[:, :], compare_op=ALU.is_ge, fill=0.0, base=w - 1,
                                             pattern=[[w, P // w]], channel_multiplier=-1))
                linked(eng.memset(wmask[:, :, :], 0.0))
                for q in range(QT_N):
                    apart = q * (P - HALF_WINDOW)
                    m = wmask[:, q, :]
                    for sign in (1, -1):
                        linked(eng.affine_select(out=m, in_=m, compare_op=ALU.is_ge, fill=MASKED,
                                                 base=HALF_WINDOW - sign * apart, pattern=[[sign, S - HALF_WINDOW]],
                                                 channel_multiplier=-sign))
                linked(eng.memset(neg_half[:, :], -0.5))
                linked(eng.memset(eps[:, :], LN_EPS))

            @block.scalar
            def _(eng):
                for dst, w in ((wq0, "wq0"), (wk0, "wk0"), (wv0, "wv0")):
                    eng.dma_start(dst[:, :, :], tiled(a[w])).then_inc(w0_landed, 16)
                eng.wait_ge(cleared, 7)
                padded(eng, wo0, a["wo0"], w0_landed)
                eng.dma_start(bo0[:, :], a["bo0"].unsqueeze(0).to_broadcast([P, D])).then_inc(w0_landed, 16)

            @block.sync
            def _(eng):
                eng.dma_start(X[:, 0:QT_N, :], x_v[:, 0:QT_N, :]).then_inc(x_first, 16)
                eng.dma_start(X[:, QT_N:TILES, :], x_v[:, QT_N:TILES, :]).then_inc(x_rest, 16)

                def column(dst, v, s):
                    eng.dma_start(dst[:, :], v.rearrange("(t p) -> p t", p=P), allow_slow_non_contiguous=True).then_inc(s, 16)

                def row(dst, v, s):
                    eng.dma_start(dst[:, :], v.unsqueeze(0).to_broadcast([P, D])).then_inc(s, 16)

                for dst, w in ((wq1, "wq1"), (wk1, "wk1"), (wv1, "wv1")):
                    eng.dma_start(dst[:, :, :], tiled(a[w])).then_inc(w1_landed, 16)
                column(bq1, a["bq1"], w1_landed)
                column(bk1, a["bk1"], w1_landed)
                row(bv1, a["bv1"], w1_landed)
                row(bo1, a["bo1"], w1_landed)
                eng.wait_ge(cleared, 7)
                padded(eng, wo1, a["wo1"], w1_landed)
                for d in (rows_dram, outs_dram):
                    eng.dma_start(d.rearrange("(k p) d -> p k d", p=P), zero[:, :, :].to_broadcast([P, ROWS // P, D])
                                  ).then_inc(zeroed, 16)
                for dst, w in ((wr0, "wr0"), (wr1, "wr1")):
                    eng.dma_start(dst[:, :, :], tiled(a[w])).then_inc(wr_landed, 16)
                column(gamma, a["gamma"], ln_landed)
                column(beta, a["beta"], ln_landed)
                for dst, w in ((wq3, "wq3"), (wk3, "wk3"), (wv3, "wv3")):
                    for h in range(HEADS):
                        r = h % 8 * 16
                        eng.dma_start(dst[r:r + 16, h // 8, h * 16:(h + 1) * 16], a[w]).then_inc(w3_landed, 16)
                padded(eng, wo3, a["wo3"], w3_landed)
                row(bo3, a["bo3"], w3_landed)

        W0, W1, W3 = 3 * 16 + 5 * 16, 7 * 16 + 4 * 16, 3 * HEADS * 16 + 5 * 16
        attention(nc, "L0a", env, dh=16, windowed=True, q_scale=16 ** -0.5, wq=wq0, wk=wk0, wv=wv0, wo=wo0, bo=bo0,
                  x_landed=((x_first, 16), (x_rest, 16)), w_landed=((w0_landed, W0),))
        with nc.Block() as block:
            @block.scalar
            def _(eng):
                eng.wait_ge(w1_landed, W1)
                eng.activation(bq1s[:, :], bq1[:, :], ACT.Copy, scale=16 ** -0.5).then_inc(bias_scaled, 1)
                eng.wait_ge(bias_scaled, 1)
        attention(nc, "L0x", env, dh=16, cross=True, q_scale=16 ** -0.5, wq=wq1, wk=wk1, wv=wv1, wo=wo1, bq=bq1s,
                  bk=bk1, bv=bv1, bo=bo1, ctx_dram=a["ctx"], w_landed=((w1_landed, W1),))
        moe(nc, "L0f", env, 682, True, wr0, ((wr_landed, 32),), a["w1_0"], a["w2_0"], a["w3_0"],
            rows_dram=rows_dram, outs_dram=outs_dram, zeroed=((zeroed, 32),))
        with ExitStack() as inner:
            wq2, wk2, wv2 = (inner.enter_context(nc.sbuf_tensor(n, [P, DT, 1024], F32)) for n in ("wq2", "wk2", "wv2"))
            wo2 = inner.enter_context(nc.sbuf_tensor("wo2", [P, 8, D], F32))
            w2_landed = sem("w2_landed")
            with nc.Block() as block:
                @block.sync
                def _(eng):
                    for dst, w in ((wq2, "wq2"), (wk2, "wk2"), (wv2, "wv2"), (wo2, "wo2")):
                        eng.dma_start(dst[:, :, :], tiled(a[w])).then_inc(w2_landed, 16)
            attention(nc, "L1a", env, dh=64, q_scale=1 / 8, wq=wq2, wk=wk2, wv=wv2, wo=wo2, affine=(gamma, beta),
                      w_landed=((w2_landed, 64), (ln_landed, 32)))
        attention(nc, "L1x", env, dh=16, cross=True, q_scale=D ** -0.5, wq=wq3, wk=wk3, wv=wv3, wo=wo3, bo=bo3,
                  ctx_dram=a["ctx"], w_landed=((w3_landed, W3),))
        moe(nc, "L1f", env, 1024, False, wr1, ((wr_landed, 32),), a["w1_1"], None, a["w2_1"], a["b1_1"], a["b2_1"],
            rows_dram=rows_dram, outs_dram=outs_dram, zeroed=())
        with nc.Block() as block:
            @block.sync
            def _(eng):
                eng.dma_start(out_v, X[:, :, :]).then_inc(stored, 16)
                eng.wait_ge(stored, 16)


def kernel(**inputs):
    import numpy as np
    import concourse.bacc as bacc
    from concourse.bass_utils import run_bass_kernel_spmd

    i = {k: np.asarray(v) for k, v in inputs.items()}
    qkv = i["L0_attn_W_qkv"]
    laid = {
        "x": i["x"], "ctx": i["ctx_1024"],
        "wq0": qkv[:, 0:256], "wk0": qkv[:, 256:512], "wv0": qkv[:, 512:768],
        "wo0": i["L0_attn_W_proj"], "bo0": i["L0_attn_b_proj"],
        "wq1": i["L0_xattn_wq"].T, "wk1": i["L0_xattn_wk"].T, "wv1": i["L0_xattn_wv"].T, "wo1": i["L0_xattn_wo"].T,
        "bq1": i["L0_xattn_bq"], "bk1": i["L0_xattn_bk"], "bv1": i["L0_xattn_bv"], "bo1": i["L0_xattn_bo"],
        "wr0": i["L0_ffn_Wg"].T, "w1_0": i["L0_ffn_W1"].transpose(0, 2, 1), "w2_0": i["L0_ffn_W2"].transpose(0, 2, 1),
        "w3_0": i["L0_ffn_W3"].transpose(0, 2, 1),
        "gamma": i["L1_attn_ln_gamma"], "beta": i["L1_attn_ln_beta"],
        "wq2": i["L1_attn_Wq"], "wk2": i["L1_attn_Wk"], "wv2": i["L1_attn_Wv"], "wo2": i["L1_attn_Wo"],
        "wq3": i["L1_xattn_Wq"].T, "wk3": i["L1_xattn_Wk"].T, "wv3": i["L1_xattn_Wv"].T, "wo3": i["L1_xattn_Wo"].T,
        "bo3": i["L1_xattn_bo"],
        "wr1": i["L1_ffn_Wr"].T, "w1_1": i["L1_ffn_W1"].transpose(0, 2, 1), "b1_1": i["L1_ffn_b1"],
        "w2_1": i["L1_ffn_W2"].transpose(0, 2, 1), "b2_1": i["L1_ffn_b2"],
    }
    nc = bacc.Bacc("TRN2", target_bir_lowering=False, num_devices=1)
    arrays, aps = {}, {}
    for name, v in laid.items():
        v = np.ascontiguousarray(v)
        arrays[f"in_{name}_dram"] = v
        aps[name] = nc.dram_tensor(f"in_{name}_dram", v.shape, mybir.dt.from_np(v.dtype), kind="ExternalInput").ap()
    aps["out"] = nc.dram_tensor(OUT_NAME, (B, S, D), F32, kind="ExternalOutput").ap()
    decoder(nc, aps)
    r = run_bass_kernel_spmd(nc, [arrays], core_ids=[0])
    return r.results[0][OUT_NAME]
```

```python
from contextlib import ExitStack

import concourse.bass as bass
from concourse import mybir

P = 128
ALU = mybir.AluOpType
ACT = mybir.ActivationFunctionType
AX = mybir.AxisListType
F32 = mybir.dt.float32
BF16 = mybir.dt.bfloat16
I32 = mybir.dt.int32
U32 = mybir.dt.uint32

B, S, D = 8, 256, 256
SC = 77
HEADS = 16
QT_N = S // P
DT = D // P
TILES = B * QT_N
LN_EPS = 1e-5
LOOK = 4
TL = 2
NB = 4
HALF_WINDOW = 64
MASKED = -1.0e30
EXPERTS = 8
TOP = 2
REGION = TILES
TABLE_BLOCKS = EXPERTS * REGION + 2


def count(per_batch, b, j):
    return (b + 1) * per_batch + j + 1


def attention(nc, name, env, dh, windowed=False, cross=False, affine=None, q_scale=1.0,
              wq=None, wk=None, wv=None, wo=None, bq=None, bk=None, bv=None, bo=None,
              ctx_dram=None, x_landed=(), w_landed=(), route=None):
    X, ident, identb, neg_half, eps = env["X"], env["ident"], env["identb"], env["neg_half"], env["eps"]
    wmask = env.get("wmask")
    hpc = P // dh
    nct = HEADS // hpc
    hmask = env["hmask16"] if dh == 16 else env["hmask64"]
    G = 2 if cross else 1
    NU = HEADS // G
    keys = SC if cross else S
    width = SC if cross else (S - HALF_WINDOW if windowed else S)
    first_key = (0, HALF_WINDOW) if windowed else (0, 0)
    dv = 32 if dh == 16 else 64
    HG = P // dv
    NG = HEADS // HG
    UG = HG // G
    GP = dv // dh
    NT = NG // GP
    NF_OUT = NT + 1
    NV = 1 if cross else S // P
    v_n = SC if cross else P

    def head_of(slot):
        return slot // 8 * 8 + slot % 4 * 2 + slot % 8 // 4 if dh == 16 else slot

    vw = HEADS * dh
    per_bank = 512 // S
    fev = [("ct", 0), ("xt", 0)] if cross else [("xt", 0)]
    qev = [("q", i) for i in range((nct + per_bank - 1) // per_bank)]
    if cross:
        kev = [("k", 0), ("v", 0)]
        vev = []
    else:
        kev = [("k", i) for i in range((nct + per_bank - 1) // per_bank)]
        vev = [("v", v, i) for v in range(NV) for i in range((vw + 511) // 512)]
        if vw < 512:
            vev = [("v", 0, 0)]
    fev += qev + vev
    NF, NK = len(fev), len(kev)
    f_at = {e: i for i, e in enumerate(fev)}
    plan = {}
    start = 2
    if cross:
        plan = {1: [("f", ("ct", 0))], 2: [("f", ("xt", 0))], 3: [("f", qev[0]), ("k", kev[0])], 4: [("k", kev[1])]}
    else:
        plan[start] = [("f", ("xt", 0))]
        order = []
        for a, c in zip(qev, kev):
            order += [("k", c), ("f", a)]
        order += [("f", e) for e in vev]
        per_step = (len(order) + NU - LOOK - start - 3) // (NU - LOOK - start - 2)
        for i, o in enumerate(order):
            plan.setdefault(start + 1 + i // per_step, []).append(o)

    with ExitStack() as stack:
        def sb(n, shape, dt=F32):
            return stack.enter_context(nc.sbuf_tensor(f"{name}_{n}", shape, dt))

        used = []

        def sem(n):
            used.append(nc.alloc_semaphore(f"{name}_{n}"))
            return used[-1]

        ps_s = stack.enter_context(nc.psum_tensor(f"{name}_ps_s", [P, 2, 512], F32))
        ps_t = stack.enter_context(nc.psum_tensor(f"{name}_ps_t", [P, 2, 512], F32))
        ps_o = stack.enter_context(nc.psum_tensor(f"{name}_ps_o", [P, 512], F32))
        RING = 1 if route else 2
        ps_f = stack.enter_context(nc.psum_tensor(f"{name}_ps_f", [P, RING, 512], F32))
        ps_r = stack.enter_context(nc.psum_tensor(f"{name}_ps_r", [P, 512], F32)) if route else None
        ps_k = stack.enter_context(nc.psum_tensor(f"{name}_ps_k", [P, 512], F32))

        stats = sb("stats", [P, QT_N, 6])
        mv = sb("mv", [P, QT_N, 2])
        veps = sb("veps", [P, QT_N])
        rstd = sb("rstd", [P, QT_N])
        carrier = sb("carrier", [P, 1])
        xn = sb("xn", [P, QT_N, D])
        xt = sb("xt", [P, DT, S])
        ctx_in = sb("ctx_in", [P, 2, D]) if cross else None
        ct = sb("ct", [P, DT, SC]) if cross else None
        q_t = [sb(f"q_t{i}", [P, nct, S]) for i in range(2)]
        k_m = [sb(f"k_m{i}", [P, HEADS, keys]) for i in range(2)]
        v_w = dv if dh == 16 else dh
        v_s = [sb(f"v_s{i}", [P, NV, HEADS, v_w]) for i in range(2)]
        pitch = S + HALF_WINDOW if windowed else width
        prob = sb("prob", [P, NB, QT_N * G, pitch])
        prob_flat = prob[:, :, :, :].rearrange("p j r k -> p j (r k)")
        nmax = sb("nmax", [P, NB, QT_N * G])
        total = sb("total", [P, NB, QT_N * G])
        rtot = sb("rtot", [P, NB, QT_N * G])
        prob_t = [sb(f"prob_t{i}", [P, UG, 512]) for i in range(2)]
        o_t = sb("o_t", [P, NT, S])

        stats_done, var_done, rstd_done, xn_done = sem("stats"), sem("var"), sem("rstd"), sem("xn")
        ctx_landed = [sem("ctx0"), sem("ctx1")] if cross else None
        front_done, front_free = sem("front_done"), sem("front_free")
        keys_done, keys_free = sem("keys_done"), sem("keys_free")
        scores_done, max_done = sem("scores"), sem("max")
        exp_done, rtot_done, norm_done = sem("exp"), sem("rtot"), sem("norm")
        turned, turned_free = sem("turned"), [sem("turned_free0"), sem("turned_free1")]
        out_done, out_free = sem("out_done"), sem("out_free")
        init_done = sem("init")
        INITS = (2 if dh == 16 else 0) + (NB if windowed else 0)
        NO = NG + 1
        bias_done, veps_done, carried = sem("bias"), sem("veps"), sem("carried")
        if route:
            r_stats, r_mv = sb("r_stats", [P, QT_N, 6]), sb("r_mv", [P, QT_N, 2])
            r_veps, r_rstd = sb("r_veps", [P, QT_N]), sb("r_rstd", [P, QT_N])
            xr, xr_t = sb("xr", [P, 2, QT_N, D]), sb("xr_t", [P, DT, S])
            logits, top = sb("logits", [P, QT_N, EXPERTS]), sb("top", [P, QT_N, 8])
            index, index_f = sb("index", [P, QT_N, 8], U32), sb("index_f", [P, QT_N, TOP])
            chosen, both = sb("chosen", [P, TOP, QT_N, EXPERTS]), sb("both", [P, QT_N, EXPERTS])
            counts = sb("counts", [P, 2, QT_N, EXPERTS])
            place, picked = sb("place", [P, QT_N, EXPERTS]), sb("picked", [P, TOP, QT_N, EXPERTS])
            slot_f, slot_i = sb("slot_f", [P, TOP, QT_N]), sb("slot_i", [P, 2, QT_N, TOP], I32)
            apart, odds, first_gate = sb("apart", [P, QT_N]), sb("odds", [P, QT_N]), sb("first_gate", [P, QT_N])
            r_carrier = sb("r_carrier", [P, 1])
            r_carried, r_copied = sem("r_carried"), sem("r_copied")
            r_cell = sb("r_cell", [P, 1])
            r_link = sem("r_link")
            r_var_done, r_veps_done, r_rstd_done, r_xn_done = (sem(n) for n in ("r_var", "r_veps", "r_rstd", "r_xn"))
            r_filled, r_emptied = sem("r_filled"), sem("r_emptied")
            both_done, apart_done, odds_done = sem("both"), sem("apart"), sem("odds")
            slot_done, scattered = sem("slot"), [sem("scattered0"), sem("scattered1")]
            LINKS = 15

        def unit(kind, b, j):
            nb = 0
            if j >= NU:
                if kind == "last":
                    return None
                return b + 1, 1, j - NU
            if kind == "first":
                return None
            return b, 0, j

        def run(step, front, tail, eng):
            front(-1, 0)
            for i in range(NU - LOOK, NU):
                step("first", -1, 1, i)

            def batch(kind, b, par):
                for i in range(NU):
                    if kind != "last":
                        front(b, 1 - par, i)
                    step(kind, b, par, i)

            batch("start", 0, 0)
            with eng.Fori(0, B // 2 - 1) as pair:
                for par in (1, 0):
                    batch("mid", pair * 2 + 2 - par, par)
            batch("last", B - 1, 1)
            tail(B - 1, 1)

        with nc.Block() as block:
            def spaced(v):
                return v.rearrange("p (a two) (half d) -> p a (two half) d", two=2, half=2)[:, :, 0::3, :]

            def pairs(v):
                return v.rearrange("p (a two d) -> p a two d", two=2, d=16)

            def evacuate(eng, which, b, par, j):
                g, r = j // UG, j % UG
                eng.wait_ge(turned, count(NU, b, j))
                if r < 2:
                    eng.wait_ge(out_done, count(NO, b, g - 2) if g >= 2 else count(NO, b - 1, NG - 2 + g))
                dst, src = prob_t[g % 2], ps_t
                if which == "vector":
                    ins = eng.tensor_copy(dst[0:v_n, r, :], src[0:v_n, j % 2, :])
                else:
                    ins = eng.activation(dst[0:v_n, r, :], src[0:v_n, j % 2, :], ACT.Copy)
                ins.then_inc(turned_free[j % 2], 1)

            @block.sync
            def _(eng):
                if not cross:
                    return

                def load(b, par, i):
                    if i is not None and i != 0:
                        return
                    if i is not None:
                        eng.wait_ge(front_done, count(NF, b - 1, f_at[("ct", 0)]))
                    eng.dma_start(ctx_in[0:SC, par, :], ctx_dram[bass.ds(b + 1, 1)].rearrange("a s d -> (a s) d")
                                  ).then_inc(ctx_landed[par], 16)

                run(lambda *a: None, lambda b, par, i=None: load(b, par, i), lambda b, par: None, eng)

            @block.vector
            def _(eng):
                if route:
                    for s, n in ((r_link, LINKS), (r_var_done, 1), (r_xn_done, 1), (r_copied, 3), (both_done, 1), (apart_done, 1), (slot_done, 1)):
                        eng.sem_inc(s, n)
                for s, n in ((stats_done, QT_N), (var_done, 1), (xn_done, QT_N), (keys_free, NK),
                             (max_done, NU), (rtot_done, NU),
                             (turned_free[1], NU // 2)):
                    eng.sem_inc(s, n)
                eng.sem_inc(out_free, 1)
                if windowed:
                    for j in range(NB):
                        eng.memset(prob[:, j, :, :], 0.0).then_inc(init_done, 1)
                if dh == 16:
                    for i in range(2):
                        eng.memset(v_s[i][:, :, :, :], 0.0).then_inc(init_done, 1)

                for s, v in x_landed[:1]:
                    eng.wait_ge(s, v)

                def front(b, par, i=None):
                    nb = b + 1
                    if i is None or i == 0:
                        if i == 0:
                            for s, v in x_landed[1:]:
                                eng.wait_ge(s, v)
                        for q in range(QT_N):
                            eng.bn_stats(stats[:, q, :], X[:, bass.ds(nb * QT_N + q, 1), :].rearrange("p a d -> p (a d)")
                                         ).then_inc(stats_done, 1)
                        if i is not None:
                            eng.wait_ge(carried, nb)
                        eng.wait_ge(stats_done, count(QT_N, nb, QT_N - 1))
                        eng.tensor_copy(carrier[:, :], stats[:, 0, 0:1]).then_inc(carried, 1)
                        for q in range(QT_N):
                            ins = eng.bn_aggr(mv[:, q, :], stats[:, q, :])
                        ins.then_inc(var_done, 1)
                    if i is None or i == 1:
                        eng.wait_ge(rstd_done, count(1, nb, 0))
                        for q in range(QT_N):
                            if q == 0:
                                eng.wait_ge(front_done, count(NF, nb - 1, f_at[("xt", 0)]))
                            eng.tensor_scalar(xn[:, q, :], X[:, bass.ds(nb * QT_N + q, 1), :].rearrange("p a d -> p (a d)"),
                                              mv[:, q, 0:1], rstd[:, q:q + 1], ALU.subtract, ALU.mult
                                              ).then_inc(xn_done, 1)
                    for st, evs in sorted(plan.items()):
                        if i is not None and st != i:
                            continue
                        for ring, ev in evs:
                            if ring == "k" and (i is None or not windowed):
                                key_event(nb, par, ev)
                    if windowed and i is not None and 0 <= i - key_step < HEADS // 2:
                        masked_keys(nb, par, (i - key_step) * 2 // hpc, (i - key_step) * 2 % hpc)

                key_step = [st for st, evs in plan.items() for ring, _ in evs if ring == "k"][0]

                def masked_keys(nb, par, c, h0):
                    eng.wait_ge(keys_done, count(NK, nb, c // per_bank))
                    src = ps_k[:, c % per_bank * S:(c % per_bank + 1) * S].unsqueeze(1).to_broadcast([P, 2, S])
                    m = hmask[:, h0:h0 + 2].unsqueeze(2).to_broadcast([P, 2, S])
                    ins = eng.tensor_tensor(k_m[par][:, c * hpc + h0:c * hpc + h0 + 2, :], src, m, ALU.mult)
                    if (c + 1) % per_bank == 0 and h0 + 2 == hpc:
                        ins.then_inc(keys_free, 1)

                def key_event(nb, par, ev):
                    e = kev.index(ev)
                    eng.wait_ge(keys_done, count(NK, nb, e))
                    if ev[0] == "k" and cross:
                        for c in range(nct):
                            src = ps_k[:, c * SC:(c + 1) * SC].unsqueeze(1).to_broadcast([P, hpc, SC])
                            m = hmask[:, 0:hpc].unsqueeze(2).to_broadcast([P, hpc, SC])
                            dst = k_m[par][:, c * hpc:(c + 1) * hpc, :]
                            if bk is not None:
                                ins = eng.scalar_tensor_tensor(out=dst, in0=src, scalar=bk[:, c:c + 1], in1=m,
                                                               op0=ALU.add, op1=ALU.mult)
                            else:
                                ins = eng.tensor_tensor(dst, src, m, ALU.mult)
                        ins.then_inc(keys_free, 1)
                    elif ev[0] == "v":
                        dst = spaced(v_s[par][0:SC, 0, :, :])
                        src = pairs(ps_k[0:SC, 0:D])
                        eng.wait_ge(init_done, INITS)
                        if bv is not None:
                            ins = eng.tensor_tensor(dst, src, pairs(bv[0:SC, :]), ALU.add)
                        else:
                            ins = eng.tensor_copy(dst, src)
                        ins.then_inc(keys_free, 1)
                    else:
                        for c in range(ev[1] * per_bank, (ev[1] + 1) * per_bank):
                            for h0 in range(0, hpc, 2):
                                masked_keys(nb, par, c, h0)

                def step(kind, b, par, i):
                    u = unit(kind, b, i + TL)
                    if u:
                        totals(u[0], u[2])
                    u = unit(kind, b, i)
                    if u and u[2] % 2 == 1:
                        evacuate(eng, "vector", u[0], par, u[2])
                    if kind in ("mid", "last") and i == 1:
                        add_projection(b - 1)
                    u = unit(kind, b, i + LOOK)
                    if u:
                        nb, nxt, j = u
                        eng.wait_ge(scores_done, count(NU, nb, j))
                        eng.wait_ge(exp_done, count(NU, nb, j - NB))
                        src = ps_s[:, j % 2, 0:QT_N * G * width].rearrange("p (a k) -> p a k", k=width)
                        eng.tensor_reduce(nmax[:, j % NB, :], src, AX.X, ALU.max, negate=True).then_inc(max_done, 1)
                    if kind in ("mid", "last"):
                        route_step(b - 1, 1 - par, i)

                def route_step(b, par, i):
                    if not route:
                        return
                    links = [{1: 0, 5: 1, 7: 8}.get(i, 0)]

                    def linked(ins):
                        ins.then_inc(r_link, 1)
                        eng.wait_ge(r_link, count(LINKS, b, links[0]))
                        links[0] += 1

                    def carry(j):
                        eng.wait_ge(r_copied, count(3, b, j - 1))
                        eng.tensor_copy(r_carrier[:, :], eps[:, 0:1]).then_inc(r_copied, 1)

                    if i == 1:
                        eng.wait_ge(out_free, count(NF_OUT, b, NT))
                        carry(0)
                        for q in range(QT_N):
                            ins = eng.bn_stats(r_stats[:, q, :], X[:, bass.ds(b * QT_N + q, 1), :].rearrange("p a d -> p (a d)"))
                        linked(ins)
                        carry(1)
                        for q in range(QT_N):
                            ins = eng.bn_aggr(r_mv[:, q, :], r_stats[:, q, :])
                        ins.then_inc(r_var_done, 1)
                    elif i == 2:
                        eng.wait_ge(r_rstd_done, count(1, b, 0))
                        eng.wait_ge(scattered[par], 32 * (b - par) + 16)
                        for q in range(QT_N):
                            ins = eng.tensor_scalar(xr[:, par, q, :], X[:, bass.ds(b * QT_N + q, 1), :].rearrange("p a d -> p (a d)"),
                                                    r_mv[:, q, 0:1], r_rstd[:, q:q + 1], ALU.subtract, ALU.mult)
                        ins.then_inc(r_xn_done, 1)
                    elif i == 5:
                        eng.wait_ge(r_emptied, count(3, b, 1))
                        carry(2)
                        for q in range(QT_N):
                            ins = eng.max(top[:, q, :], logits[:, q, :])
                        linked(ins)
                        eng.tensor_tensor(apart[:, :], top[:, :, 1], top[:, :, 0], ALU.subtract).then_inc(apart_done, 1)
                        for q in range(QT_N):
                            ins = eng.max_index(index[:, q, :], top[:, q, :], logits[:, q, :])
                        linked(ins)
                        linked(eng.tensor_copy(index_f[:, :, :], index[:, :, 0:TOP]))
                        for k in range(TOP):
                            ins = eng.tensor_tensor(chosen[:, k, :, :], route["experts"][:, :].unsqueeze(1).to_broadcast([P, QT_N, EXPERTS]),
                                                    index_f[:, :, k].unsqueeze(2).to_broadcast([P, QT_N, EXPERTS]), ALU.is_equal)
                        linked(ins)
                        eng.tensor_tensor(both[:, :, :], chosen[:, 0, :, :], chosen[:, 1, :, :], ALU.add).then_inc(both_done, 1)
                        eng.wait_ge(odds_done, count(1, b, 0))
                        gate = route["gate"][:, bass.ds(b * QT_N, QT_N), :]
                        linked(eng.tensor_scalar(first_gate[:, :], odds[:, :], 1.0, None, ALU.add))
                        linked(eng.reciprocal(first_gate[:, :], first_gate[:, :]))
                        eng.tensor_copy(gate[:, :, 0], first_gate[:, :])
                        linked(eng.tensor_tensor(gate[:, :, 1], first_gate[:, :], odds[:, :], ALU.mult))
                        assert links[0] == 8
                    elif i == 7:
                        taken = route["taken"]
                        eng.wait_ge(r_emptied, count(3, b, 2))
                        for q in range(QT_N):
                            linked(eng.tensor_tensor(place[:, q, :], counts[:, 0, q, :], taken[:, :], ALU.add))
                            linked(eng.tensor_tensor(taken[:, :], counts[:, 1, q, :], taken[:, :], ALU.add))
                        linked(eng.tensor_tensor(picked[:, :, :, :], chosen[:, :, :, :],
                                                 place[:, :, :].unsqueeze(1).to_broadcast([P, TOP, QT_N, EXPERTS]), ALU.mult))
                        linked(eng.tensor_reduce(slot_f[:, :, :], picked[:, :, :, :], AX.X, ALU.add))
                        by_token = slot_f[:, :, :].rearrange("p k t -> p t k")
                        eng.tensor_copy(route["slot"][:, bass.ds(b * QT_N, QT_N), :], by_token)
                        eng.wait_ge(scattered[par], 32 * (b - par) + 16)
                        linked(eng.tensor_copy(slot_i[:, par, :, :], by_token))
                        assert links[0] == LINKS
                        eng.sem_inc(slot_done, 1)

                def totals(nb, j):
                    eng.wait_ge(exp_done, count(NU, nb, j))
                    eng.wait_ge(norm_done, count(NU, nb, j - NB))
                    eng.reciprocal(rtot[:, j % NB, :], total[:, j % NB, :]).then_inc(rtot_done, 1)

                def add_projection(b):
                    eng.wait_ge(out_done, count(NO, b, NG))
                    xb = X[:, bass.ds(b * QT_N, QT_N), :]
                    if bo is not None:
                        eng.wait_ge(bias_done, count(1, b, 0))
                    eng.tensor_tensor(xb, xb, ps_o[:, :].rearrange("p (q d) -> p q d", q=QT_N), ALU.add
                                      ).then_inc(out_free, 1)

                def tail(b, par):
                    add_projection(b)
                    for i in range(NU):
                        route_step(b, par, i)

                run(step, front, tail, eng)

            @block.scalar
            def _(eng):
                for s, n in ((front_free, NF), (exp_done, NU), (turned_free[0], NU // 2)):
                    eng.sem_inc(s, n)
                eng.sem_inc(out_free, NT)
                if route:
                    eng.sem_inc(r_emptied, 3)
                    eng.sem_inc(odds_done, 1)
                if windowed:
                    eng.wait_ge(init_done, INITS)

                def front(b, par, i=None):
                    nb = b + 1
                    for st, evs in sorted(plan.items()):
                        if i is not None and st != i:
                            continue
                        for ring, ev in evs:
                            if ring == "f":
                                event(nb, par, ev)

                def event(nb, par, ev):
                    e = f_at[ev]
                    bank = ps_f[:, e % RING, :]
                    eng.wait_ge(front_done, count(NF, nb, e))
                    if ev[0] == "xt":
                        if affine is None:
                            ins = eng.activation(xt[:, :, :], bank.rearrange("p (c s) -> p c s", c=DT), ACT.Copy)
                        else:
                            for c in range(DT):
                                ins = eng.activation(xt[:, c, :], bank[:, c * S:(c + 1) * S], ACT.Identity,
                                                     bias=affine[1][:, c:c + 1], scale=affine[0][:, c:c + 1])
                    elif ev[0] == "ct":
                        ins = eng.activation(ct[:, :, :], bank[:, 0:DT * SC].rearrange("p (c s) -> p c s", c=DT), ACT.Copy)
                    elif ev[0] == "q":
                        for cc in range(per_bank):
                            c = ev[1] * per_bank + cc
                            if bq is not None:
                                ins = eng.activation(q_t[par][:, c, :], bank[:, cc * S:(cc + 1) * S], ACT.Identity,
                                                     bias=bq[:, c:c + 1], scale=q_scale)
                            elif cc == 0:
                                ins = eng.activation(q_t[par][:, c:c + per_bank, :],
                                                     bank.rearrange("p (c s) -> p c s", c=per_bank), ACT.Copy,
                                                     scale=q_scale)
                    else:
                        if dh == 16:
                            eng.wait_ge(init_done, INITS)
                            for v in range(NV):
                                ins = eng.activation(spaced(v_s[par][:, v, :, :]), pairs(bank[:, v * D:(v + 1) * D]), ACT.Copy)
                        else:
                            hh = 512 // dh
                            ins = eng.activation(v_s[par][:, ev[1], ev[2] * hh:(ev[2] + 1) * hh, :],
                                                 bank.rearrange("p (h d) -> p h d", d=dh), ACT.Copy)
                    ins.then_inc(front_free, 1)

                def group_out(b, g):
                    if (g + 1) % GP:
                        return
                    eng.wait_ge(out_done, count(NO, b, g))
                    eng.activation(o_t[:, g // GP, :], ps_o[:, 0:S], ACT.Copy).then_inc(out_free, 1)

                def step(kind, b, par, i):
                    u = unit(kind, b, i)
                    if u and u[2] % 2 == 0:
                        evacuate(eng, "scalar", u[0], par, u[2])
                    if kind != "first" and i % UG == 0 and i >= UG:
                        group_out(b, i // UG - 1)
                    if kind in ("mid", "last") and i == 0:
                        group_out(b - 1, NG - 1)
                    u = unit(kind, b, i + LOOK)
                    if u:
                        nb, nxt, j = u
                        eng.wait_ge(turned, count(NU, nb, j - NB))
                        eng.wait_ge(max_done, count(NU, nb, j))
                        eng.wait_ge(rtot_done, count(NU, nb, j - NB))
                        for r in range(QT_N * G):
                            ins = eng.activation(prob[:, j % NB, r, 0:width], ps_s[:, j % 2, r * width:(r + 1) * width],
                                                 ACT.Exp, bias=nmax[:, j % NB, r:r + 1],
                                                 accum_out=total[:, j % NB, r:r + 1])
                        ins.then_inc(exp_done, 1)
                    if kind in ("mid", "last"):
                        route_step(b - 1, i)

                def route_step(b, i):
                    if not route or i not in (3, 4, 5, 6):
                        return
                    if i == 5:
                        eng.wait_ge(apart_done, count(1, b, 0))
                        eng.activation(odds[:, :], apart[:, :], ACT.Exp).then_inc(odds_done, 1)
                        return
                    e = (3, 4, 6).index(i)
                    eng.wait_ge(r_filled, count(3, b, e))
                    w = QT_N * EXPERTS
                    if e == 0:
                        ins = eng.activation(xr_t[:, :, :], ps_r[:, :].rearrange("p (c s) -> p c s", c=DT), ACT.Copy)
                    elif e == 1:
                        ins = eng.activation(logits[:, :, :].rearrange("p q e -> p (q e)"), ps_r[:, 0:w], ACT.Copy)
                    else:
                        ins = eng.activation(counts[:, :, :, :].rearrange("p a q e -> p (a q e)"), ps_r[:, 0:2 * w], ACT.Copy)
                    ins.then_inc(r_emptied, 1)

                def tail(b, par):
                    group_out(b, NG - 1)
                    for i in range(NU):
                        route_step(b, i)

                run(step, front, tail, eng)

            @block.gpsimd
            def _(eng):
                if route:
                    for s, n in ((r_rstd_done, 1), (r_carried, 1)):
                        eng.sem_inc(s, n)
                    for i in range(2):
                        eng.dma_start(route["table"][(TABLE_BLOCKS - 2 + i) * P:(TABLE_BLOCKS - 1 + i) * P, :],
                                      route["zero"][:, 0, :]).then_inc(scattered[i], 16)
                eng.sem_inc(rstd_done, 1)
                eng.sem_inc(bias_done, 1)
                eng.sem_inc(norm_done, NU)

                def front(b, par, i=None):
                    nb = b + 1
                    if i is None or i == 0:
                        eng.wait_ge(var_done, count(1, nb, 0))
                        eng.tensor_tensor(veps[:, :], mv[:, :, 1], eps[:, 0:QT_N], ALU.add).then_inc(veps_done, 1)
                        eng.wait_ge(veps_done, nb + 1)
                        eng.tensor_tensor(rstd[:, :], veps[:, :], neg_half[:, 0:QT_N], ALU.pow).then_inc(rstd_done, 1)

                def route_step(b, par, i):
                    if not route:
                        return
                    if i == 1:
                        eng.wait_ge(r_var_done, count(1, b, 0))
                        eng.tensor_tensor(r_veps[:, :], r_mv[:, :, 1], eps[:, 0:QT_N], ALU.add).then_inc(r_veps_done, 1)
                        eng.wait_ge(r_veps_done, b + 1)
                        eng.tensor_tensor(r_rstd[:, :], r_veps[:, :], neg_half[:, 0:QT_N], ALU.pow).then_inc(r_rstd_done, 1)
                    elif i == 7:
                        eng.wait_ge(slot_done, count(1, b, 0))
                        eng.wait_ge(r_carried, count(1, b - 1, 0))
                        eng.tensor_tensor(r_cell[:, :], eps[:, 0:1], eps[:, 0:1], ALU.add).then_inc(r_carried, 1)
                        for s, v in route["zeroed"]:
                            eng.wait_ge(s, v)
                        for q in range(QT_N):
                            for k in range(TOP):
                                eng.indirect_dma_start(route["table"], bass.IndirectOffsetOnAxis(ap=slot_i[:, par, q, k:k + 1], axis=0),
                                                       xr[:, par, q, :], None).then_inc(scattered[par], 16)

                def step(kind, b, par, i):
                    if kind in ("mid", "last"):
                        route_step(b - 1, 1 - par, i)
                    if bo is not None and i == 4 and kind != "first":
                        xb = X[:, bass.ds(b * QT_N, QT_N), :]
                        eng.wait_ge(xn_done, count(QT_N, b, QT_N - 1))
                        eng.tensor_tensor(xb, xb, bo[:, :].unsqueeze(1).to_broadcast([P, QT_N, D]), ALU.add
                                          ).then_inc(bias_done, 1)
                    u = unit(kind, b, i + TL)
                    if not u:
                        return
                    nb, nxt, j = u
                    eng.wait_ge(rtot_done, count(NU, nb, j))
                    eng.tensor_tensor(prob[:, j % NB, :, 0:width], prob[:, j % NB, :, 0:width],
                                      rtot[:, j % NB, :].unsqueeze(2).to_broadcast([P, QT_N * G, width]), ALU.mult
                                      ).then_inc(norm_done, 1)

                def tail(b, par):
                    if route:
                        for i in range(NU):
                            route_step(b, par, i)
                        for s in scattered:
                            eng.wait_ge(s, B // 2 * 64 + 16)

                run(step, front, tail, eng)

            @block.tensor
            def _(eng):
                for s, n in ((front_done, NF), (keys_done, NK), (scores_done, NU), (turned, NU), (out_done, NO)):
                    eng.sem_inc(s, n)
                if route:
                    eng.sem_inc(r_filled, 3)
                for s, v in w_landed:
                    eng.wait_ge(s, v)

                def front(b, par, i=None):
                    nb = b + 1
                    for st, evs in sorted(plan.items()):
                        if i is not None and st != i:
                            continue
                        for ring, ev in evs:
                            if ring == "f":
                                front_event(nb, par, ev)
                            else:
                                key_event(nb, par, ev)

                def project(out, w, c0, n, rhs, kt_rows=P):
                    for t in range(DT):
                        ins = eng.matmul(out, w[:, t, c0:c0 + n], rhs[:, t, :], start=(t == 0), stop=(t == DT - 1))
                    return ins

                def front_event(nb, par, ev):
                    e = f_at[ev]
                    bank = ps_f[:, e % RING, :]
                    before = e - RING if e >= RING else max(p for p in range(NF) if p % RING == e % RING) - NF
                    eng.wait_ge(front_free, count(NF, nb, before))
                    if ev[0] == "xt":
                        eng.wait_ge(xn_done, count(QT_N, nb, QT_N - 1))
                        for c in range(DT):
                            for q in range(QT_N):
                                ins = eng.transpose(bank[:, c * S + q * P:c * S + (q + 1) * P],
                                                    xn[:, q, c * P:(c + 1) * P], ident[:, :])
                    elif ev[0] == "ct":
                        eng.wait_ge(ctx_landed[par], nb * 8 + 16 - 8 * par)
                        for c in range(DT):
                            ins = eng.transpose(bank[:, c * SC:(c + 1) * SC], ctx_in[0:SC, par, c * P:(c + 1) * P],
                                                ident[0:SC, 0:SC])
                    elif ev[0] == "q":
                        eng.wait_ge(front_free, count(NF, nb, f_at[("xt", 0)]))
                        for cc in range(per_bank):
                            ins = project(bank[:, cc * S:(cc + 1) * S], wq, (ev[1] * per_bank + cc) * P, P, xt)
                    else:
                        eng.wait_ge(front_free, count(NF, nb, f_at[("xt", 0)]))
                        if dh == 16:
                            pieces = [(v * P, v * D, 0, D) for v in range(NV)]
                        else:
                            pieces = [(ev[1] * P, 0, ev[2] * 512, 512)]
                        for r0, o, c0, w in pieces:
                            for t in range(DT):
                                ins = eng.matmul(bank[:, o:o + w], xt[:, t, r0:r0 + P], wv[:, t, c0:c0 + w],
                                                 start=(t == 0), stop=(t == DT - 1))
                    ins.then_inc(front_done, 1)

                def key_event(nb, par, ev):
                    e = kev.index(ev)
                    eng.wait_ge(keys_free, count(NK, nb, e - 1))
                    if cross:
                        eng.wait_ge(front_free, count(NF, nb, f_at[("ct", 0)]))
                    else:
                        eng.wait_ge(front_free, count(NF, nb, f_at[("xt", 0)]))
                    if cross and ev[0] == "k":
                        for c in range(nct):
                            ins = project(ps_k[:, c * SC:(c + 1) * SC], wk, c * P, P, ct)
                    elif cross:
                        for t in range(DT):
                            ins = eng.matmul(ps_k[0:SC, 0:D], ct[:, t, :], wv[:, t, :], start=(t == 0), stop=(t == DT - 1))
                    else:
                        for cc in range(per_bank):
                            ins = project(ps_k[:, cc * S:(cc + 1) * S], wk, (ev[1] * per_bank + cc) * P, P, xt)
                    ins.then_inc(keys_done, 1)

                def scores(nb, par, j):
                    eng.wait_ge(exp_done, count(NU, nb, j - 2))
                    c = j * G // hpc
                    last_k = 0 if cross else c // per_bank
                    eng.wait_ge(keys_free, count(NK, nb, last_k))
                    eng.wait_ge(front_free, count(NF, nb, f_at[("q", c // per_bank)]))
                    for q in range(QT_N):
                        n = G * width
                        out = ps_s[:, j % 2, q * n:(q + 1) * n]
                        k0 = first_key[q]
                        h = head_of(j * G)
                        rhs = k_m[par][:, h:h + 3:2, :] if cross else k_m[par][:, h, k0:k0 + width]
                        ins = eng.matmul(out, q_t[par][:, c, q * P:(q + 1) * P], rhs, start=True, stop=not windowed)
                        if windowed:
                            ins = eng.matmul(out, identb[:, :], wmask[:, q, :], start=False, stop=True)
                    ins.then_inc(scores_done, 1)

                def turn(b, par, j):
                    eng.wait_ge(norm_done, count(NU, b, j))
                    eng.wait_ge(turned_free[j % 2], count(NU // 2, b, j // 2 - 1))
                    if cross:
                        for g in range(G):
                            for q in range(QT_N):
                                o = (g * QT_N + q) * P
                                ins = eng.transpose(ps_t[0:SC, j % 2, o:o + P], prob[:, j % NB, q * G + g, :], ident[:, :])
                    else:
                        for q in range(QT_N):
                            for c in range(NV):
                                o = (c * QT_N + q) * P
                                ins = eng.transpose(ps_t[:, j % 2, o:o + P], prob_flat[:, j % NB, q * S + c * P:q * S + (c + 1) * P],
                                                    ident[:, :])
                    ins.then_inc(turned, 1)

                def values(b, par, g):
                    for p2 in range(2):
                        last = [j for j in range(g * UG, (g + 1) * UG) if j % 2 == p2][-1]
                        eng.wait_ge(turned_free[p2], count(NU // 2, b, last // 2))
                    if g == 0:
                        if cross:
                            eng.wait_ge(keys_free, count(NK, b, 1))
                        else:
                            eng.wait_ge(front_free, count(NF, b, NF - 1))
                    if g % GP == 0:
                        eng.wait_ge(out_free, count(NF_OUT, b, g // GP - 1))
                    pt = prob_t[g % 2]
                    for c in range(NV):
                        for hh in range(HG):
                            r, sub = hh // G, hh % G
                            o = sub * S if cross else c * S
                            ins = eng.matmul(ps_o[hh * dv:(hh + 1) * dv, 0:S], v_s[par][0:v_n, c, head_of(g * HG + hh), :],
                                             pt[0:v_n, r, o:o + S], start=(g % GP == 0 and c == 0),
                                             stop=(g % GP == GP - 1 and c == NV - 1))
                    ins.then_inc(out_done, 1)

                def step(kind, b, par, i):
                    u = unit(kind, b, i)
                    if u:
                        turn(u[0], par, u[2])
                    if kind != "first" and i % UG == 0 and i >= UG:
                        values(b, par, i // UG - 1)
                    if kind in ("mid", "last") and i == 0:
                        values(b - 1, 1 - par, NG - 1)
                    if kind in ("mid", "last") and i == 1:
                        projection(b - 1)
                    if kind in ("mid", "last"):
                        route_step(b - 1, 1 - par, i)
                    u = unit(kind, b, i + LOOK)
                    if u:
                        nb, nxt, j = u
                        scores(nb, (par + nxt) % 2, j)

                def route_step(b, par, i):
                    if not route or i not in (3, 4, 6):
                        return
                    e = (3, 4, 6).index(i)
                    eng.wait_ge(r_emptied, count(3, b, e - 1))
                    if e == 0:
                        eng.wait_ge(r_xn_done, count(1, b, 0))
                        for c in range(DT):
                            for q in range(QT_N):
                                ins = eng.transpose(ps_r[:, c * S + q * P:c * S + (q + 1) * P],
                                                    xr[:, par, q, c * P:(c + 1) * P], ident[:, :])
                    elif e == 1:
                        for q in range(QT_N):
                            for t in range(DT):
                                ins = eng.matmul(ps_r[:, q * EXPERTS:(q + 1) * EXPERTS], xr_t[:, t, q * P:(q + 1) * P],
                                                 route["wr"][:, t, :], start=(t == 0), stop=(t == DT - 1))
                    else:
                        eng.wait_ge(both_done, count(1, b, 0))
                        w = QT_N * EXPERTS
                        for a, m in enumerate((route["before"], route["ones"])):
                            ins = eng.matmul(ps_r[:, a * w:(a + 1) * w], m[:, :], both[:, :, :].rearrange("p q e -> p (q e)"),
                                             start=True, stop=True)
                    ins.then_inc(r_filled, 1)

                def tail(b, par):
                    values(b, par, NG - 1)
                    projection(b)
                    for i in range(NU):
                        route_step(b, par, i)

                def projection(b):
                    eng.wait_ge(out_free, count(NF_OUT, b, NT - 1))
                    for q in range(QT_N):
                        for g in range(NT):
                            ins = eng.matmul(ps_o[:, q * D:(q + 1) * D], o_t[:, g, q * P:(q + 1) * P], wo[:, g, :],
                                             start=(g == 0), stop=(g == NT - 1))
                    ins.then_inc(out_done, 1)

                run(step, front, tail, eng)
        nc.clear_and_free_semaphores(used)
        nc.all_engine_barrier()


MAX_BLOCKS = TILES * TOP + EXPERTS
ROWS = TABLE_BLOCKS * P
LISTED = MAX_BLOCKS + 2


def moe(nc, name, env, hidden, gated, wa_dram, wb_dram, wd_dram, b1_dram=None, b2_dram=None, route=None):
    X, ident = env["X"], env["ident"]
    HC = (hidden + 3) // 4 * 2
    halves = [(0, HC), (HC, hidden - HC)]
    ktiles = [[(o + k, min(P, n - k)) for k in range(0, n, P)] for o, n in halves]
    KT = len(ktiles[0])
    NH = 2 if gated else 1
    PIECES = 1 if gated else 2
    PW = HC // PIECES
    n_w = 2 * KT + NH + (0 if gated else 2)

    used = []

    def sem(n):
        used.append(nc.alloc_semaphore(f"{name}_{n}"))
        return used[-1]

    with ExitStack() as stack:
        def sb(n, shape, dt=F32):
            return stack.enter_context(nc.sbuf_tensor(f"{name}_{n}", shape, dt))

        gate, slot, table = route["gate"], route["slot"], route["table"]
        blocks_i = sb("blocks_i", [P, EXPERTS], I32)
        base_i = sb("base_i", [P, EXPERTS + 1], I32)
        list_i = sb("list_i", [P, LISTED], I32)
        rows_landed, y_stored = sem("rows_landed"), sem("y_stored")
        with ExitStack() as inner:
            def tb(n, shape, dt=F32):
                return inner.enter_context(nc.sbuf_tensor(f"{name}_{n}", shape, dt))

            tokens = tb("tokens", [P, EXPERTS])
            blocks_f = tb("blocks_f", [P, EXPERTS])
            cum_f = tb("cum_f", [P, EXPERTS + 1])
            past = tb("past", [P, LISTED, EXPERTS - 1])
            list_f = tb("list_f", [P, LISTED])
            link_v = sem("link_v")
            with nc.Block() as block:
                @block.vector
                def _(eng):
                    n = [0]

                    def linked(ins):
                        n[0] += 1
                        ins.then_inc(link_v, 1)
                        eng.wait_ge(link_v, n[0])

                    linked(eng.tensor_tensor(tokens[:, :], route["taken"][:, :], env["regions"][:, :], ALU.subtract))
                    linked(eng.tensor_scalar(blocks_i[:, :], tokens[:, :], float(P - 1), None, ALU.add))
                    linked(eng.tensor_scalar(blocks_i[:, :], blocks_i[:, :], 7, None, ALU.logical_shift_right))
                    linked(eng.tensor_copy(blocks_f[:, :], blocks_i[:, :]))
                    linked(eng.tensor_scalar(blocks_f[:, :], blocks_f[:, :], 1.0, None, ALU.max))
                    eng.tensor_copy(blocks_i[:, :], blocks_f[:, :])
                    linked(eng.memset(cum_f[:, :], 0.0))
                    linked(eng.tensor_tensor_scan(cum_f[:, 1:EXPERTS + 1], env["ones"][:, 0:EXPERTS], blocks_f[:, :], 0.0,
                                                  ALU.mult, ALU.add))
                    eng.tensor_copy(base_i[:, :], cum_f[:, :])
                    linked(eng.tensor_scalar(blocks_f[:, :], blocks_f[:, :], -1.0, float(REGION), ALU.mult, ALU.add))
                    shape = [P, LISTED, EXPERTS - 1]
                    linked(eng.tensor_tensor(past[:, :, :], env["numbers"][:, 0:LISTED].unsqueeze(2).to_broadcast(shape),
                                             cum_f[:, 1:EXPERTS].unsqueeze(1).to_broadcast(shape), ALU.is_ge))
                    linked(eng.tensor_tensor(past[:, :, :], past[:, :, :],
                                             blocks_f[:, 0:EXPERTS - 1].unsqueeze(1).to_broadcast(shape), ALU.mult))
                    linked(eng.tensor_reduce(list_f[:, :], past[:, :, :], AX.X, ALU.add))
                    eng.tensor_tensor(list_i[:, :], list_f[:, :], env["numbers"][:, 0:LISTED], ALU.add)

        with ExitStack() as inner:
            def tb(n, shape, dt=F32):
                return inner.enter_context(nc.sbuf_tensor(f"{name}_{n}", shape, dt))

            ps_h = inner.enter_context(nc.psum_tensor(f"{name}_ps_h", [P, 2, 2, 512], F32))
            ps_t = inner.enter_context(nc.psum_tensor(f"{name}_ps_t", [P, 2, 512], F32))
            ps_y = inner.enter_context(nc.psum_tensor(f"{name}_ps_y", [P, 512], F32))
            ps_x = inner.enter_context(nc.psum_tensor(f"{name}_ps_x", [P, 512], F32))
            w_up = [tb(f"w_up{i}", [P, NH, DT, hidden]) for i in range(2)]
            w_down = [tb(f"w_down{i}", [P, 2 * KT, D]) for i in range(2)]
            b_up = [tb(f"b_up{i}", [P, hidden]) for i in range(2)] if not gated else None
            b_down = [tb(f"b_down{i}", [P, D]) for i in range(2)] if not gated else None
            rows = tb("rows", [P, D])
            rows_t = tb("rows_t", [P, DT, P])
            mid = tb("mid", [P, 2, HC])
            hid = tb("hid", [P, 2, HC])
            hid_t = tb("hid_t", [P, 2, KT, P])
            y = tb("y", [P, D])
            weights_landed = [sem("weights0"), sem("weights1")]
            rows_turned, rows_ready = sem("rows_turned"), sem("rows_ready")
            up_done, mid_done, hid_done = sem("up"), sem("mid"), sem("hid")
            hid_turned, hid_t_done = sem("hid_turned"), [sem("hid_t0"), sem("hid_t1")]
            cleared = sem("cleared")
            down_done, y_done = sem("down"), sem("y")

            def experts_loop(eng, body):
                with eng.Fori(0, EXPERTS // 2) as pair:
                    for par in range(2):
                        e = pair * 2 + par
                        count_e = eng.value_load(blocks_i[0:1, bass.ds(e, 1)], min_val=1, max_val=TILES)
                        base_e = eng.value_load(base_i[0:1, bass.ds(e, 1)], min_val=0, max_val=MAX_BLOCKS)
                        with eng.Fori(0, count_e) as i:
                            n = nc.s_assert_within(base_e + i, 0, MAX_BLOCKS - 1, skip_runtime_bounds_check_because=
                                                   "the experts' block counts sum to MAX_BLOCKS at most")
                            body(n, par, pair, e * REGION + i)

            with nc.Block() as block:
                @block.sync
                def _(eng):
                    eng.sem_inc(y_stored, 16)

                    def load(n):
                        at = eng.value_load(list_i[0:1, bass.ds(n, 1)], min_val=0, max_val=TABLE_BLOCKS - 1)
                        eng.dma_start(rows[:, :], table[bass.ds(at * P, P), :]).then_inc(rows_landed, 16)

                    load(0)
                    eng.wait_ge(rows_turned, count(1, 0, 0))
                    load(1)

                    def body(n, par, pair, place):
                        eng.wait_ge(rows_turned, count(1, n + 1, 0))
                        load(n + 2)
                        eng.wait_ge(y_done, count(1, n, 0))
                        at = nc.s_assert_within(place, 0, TABLE_BLOCKS - 3, skip_runtime_bounds_check_because=
                                                "an expert has REGION blocks at most")
                        eng.dma_start(table[bass.ds(at * P, P), :], y[:, :]).then_inc(y_stored, 16)

                    experts_loop(eng, body)

                @block.gpsimd
                def _(eng):
                    def load(e, par):
                        s = weights_landed[par]
                        one = lambda d: d[bass.ds(e, 1)].rearrange("a r c -> (a r) c")
                        for j, d in enumerate((wa_dram, wb_dram)[:NH]):
                            eng.dma_start(w_up[par][:, j, :, :], one(d).rearrange("(c p) h -> p c h", p=P)).then_inc(s, 16)
                        for c in range(2):
                            for k, (r0, n) in enumerate(ktiles[c]):
                                eng.dma_start(w_down[par][0:n, c * KT + k, :], one(wd_dram)[r0:r0 + n, :]).then_inc(s, 16)
                        if not gated:
                            eng.dma_start(b_up[par][:, :], b1_dram[bass.ds(e, 1), :].to_broadcast([P, hidden])).then_inc(s, 16)
                            eng.dma_start(b_down[par][:, :], b2_dram[bass.ds(e, 1), :].to_broadcast([P, D])).then_inc(s, 16)

                    load(0, 0)
                    load(1, 1)
                    with eng.Fori(0, EXPERTS // 2 - 1) as pair:
                        for par in range(2):
                            e = pair * 2 + par
                            done = eng.value_load(base_i[0:1, bass.ds(e + 1, 1)], min_val=1, max_val=MAX_BLOCKS)
                            eng.wait_ge(y_done, count(1, done - 1, 0))
                            load(e + 2, par)

                @block.tensor
                def _(eng):
                    for s, n in ((rows_turned, 1), (up_done, 4), (hid_turned, 2), (down_done, 1)):
                        eng.sem_inc(s, n)

                    def turn_rows(n):
                        eng.wait_ge(rows_landed, (n + 1) * 16)
                        eng.wait_ge(rows_ready, count(1, n - 1, 0))
                        for c in range(DT):
                            ins = eng.transpose(ps_x[:, c * P:(c + 1) * P], rows[:, c * P:(c + 1) * P], ident[:, :])
                        ins.then_inc(rows_turned, 1)

                    def up(n, par, c, products=range(2)):
                        if products[0] == 0:
                            eng.wait_ge(hid_done if gated else mid_done, count(2 * PIECES, n - 1, (c + 1) * PIECES - 1))
                        o, w = halves[c]
                        for j in products:
                            m, p0 = (j, 0) if gated else (0, j * PW)
                            pw = w if gated else PW
                            for t in range(DT):
                                ins = eng.matmul(ps_h[:, c, j, 0:pw], rows_t[:, t, :],
                                                 w_up[par][:, m, t, o + p0:o + p0 + pw], start=(t == 0), stop=(t == DT - 1))
                            ins.then_inc(up_done, 1)

                    def turn_hidden(n, c):
                        eng.wait_ge(hid_done, count(2 * PIECES, n, (c + 1) * PIECES - 1))
                        eng.wait_ge(hid_t_done[c], count(1, n - 1, 0))
                        for k, (r0, w) in enumerate(ktiles[c]):
                            o = r0 - halves[c][0]
                            ins = eng.transpose(ps_t[0:w, c, k * P:(k + 1) * P], hid[:, c, o:o + w], ident[:, :])
                        ins.then_inc(hid_turned, 1)

                    def down(n, par, c, ks=range(KT)):
                        if ks[0] == 0:
                            eng.wait_ge(hid_t_done[c], count(1, n, 0))
                        if c == 0 and ks[0] == 0:
                            eng.wait_ge(y_done, count(1, n - 1, 0))
                        for k in ks:
                            w = ktiles[c][k][1]
                            ins = eng.matmul(ps_y[:, 0:D], hid_t[0:w, c, k, :], w_down[par][0:w, c * KT + k, :],
                                             start=(c == 0 and k == 0), stop=(c == 1 and k == KT - 1))
                        if c == 1 and ks[-1] == KT - 1:
                            ins.then_inc(down_done, 1)

                    turn_rows(0)
                    eng.wait_ge(cleared, 2)

                    def body(n, par, pair, place):
                        eng.wait_ge(weights_landed[par], (pair + 1) * (16 * n_w))
                        eng.wait_ge(rows_ready, count(1, n, 0))
                        up(n, par, 0)
                        up(n, par, 1, [0])
                        turn_hidden(n, 0)
                        up(n, par, 1, [1])
                        turn_rows(n + 1)
                        down(n, par, 0, range(2))
                        turn_hidden(n, 1)
                        down(n, par, 0, range(2, KT))
                        down(n, par, 1)

                    experts_loop(eng, body)

                @block.scalar
                def _(eng):
                    eng.preload_act_table(ACT.Silu if gated else ACT.Gelu)
                    eng.sem_inc(rows_ready, 1)
                    eng.sem_inc(hid_t_done[0], 1)
                    eng.sem_inc(mid_done if gated else hid_done, 2 * PIECES)

                    def rows_out(n):
                        eng.wait_ge(rows_turned, count(1, n, 0))
                        eng.activation(rows_t[:, :, :], ps_x[:, 0:D].rearrange("p (c s) -> p c s", c=DT),
                                       ACT.Copy).then_inc(rows_ready, 1)

                    def turned(n, c):
                        eng.wait_ge(hid_turned, count(2, n, c))
                        eng.wait_ge(down_done, count(1, n - 1, 0))
                        eng.activation(hid_t[:, c, :, :], ps_t[:, c, 0:KT * P].rearrange("p (k s) -> p k s", s=P),
                                       ACT.Copy).then_inc(hid_t_done[0], 1)

                    rows_out(0)

                    def body(n, par, pair, place):
                        if gated:
                            for c in range(2):
                                w = halves[c][1]
                                eng.wait_ge(up_done, count(4, n, c * 2))
                                eng.wait_ge(hid_done, count(2, n - 1, c))
                                eng.activation(mid[:, c, 0:w], ps_h[:, c, 0, 0:w], ACT.Silu).then_inc(mid_done, 1)
                            turned(n, 0)
                        else:
                            for i in range(4):
                                c, o = i // 2, i % 2 * PW
                                if i == 3:
                                    turned(n, 0)
                                eng.wait_ge(mid_done, count(4, n, i))
                                eng.wait_ge(hid_turned, count(2, n - 1, c))
                                eng.activation(hid[:, c, o:o + PW], mid[:, c, o:o + PW], ACT.Gelu).then_inc(hid_done, 1)
                        rows_out(n + 1)

                    experts_loop(eng, body)

                @block.vector
                def _(eng):
                    eng.sem_inc(hid_done if gated else mid_done, 2 * PIECES)
                    eng.sem_inc(hid_t_done[1], 1)
                    for c in range(2):
                        eng.memset(ps_t[:, c, :], 0.0).then_inc(cleared, 1)
                    eng.sem_inc(y_done, 1)

                    def first(n, par, c):
                        w = halves[c][1]
                        if gated:
                            eng.wait_ge(up_done, count(4, n, c * 2 + 1))
                            eng.wait_ge(mid_done, count(2, n, c))
                            eng.wait_ge(hid_turned, count(2, n - 1, c))
                            eng.tensor_tensor(hid[:, c, 0:w], mid[:, c, 0:w], ps_h[:, c, 1, 0:w], ALU.mult).then_inc(hid_done, 1)
                            return
                        for i in range(2):
                            o = i * PW
                            eng.wait_ge(up_done, count(4, n, c * 2 + i))
                            eng.wait_ge(hid_done, count(4, n - 1, c * 2 + i))
                            eng.tensor_tensor(mid[:, c, o:o + PW], ps_h[:, c, i, 0:PW],
                                              b_up[par][:, c * HC + o:c * HC + o + PW], ALU.add).then_inc(mid_done, 1)

                    def turned(n):
                        eng.wait_ge(hid_turned, count(2, n, 1))
                        eng.wait_ge(down_done, count(1, n - 1, 0))
                        eng.tensor_copy(hid_t[:, 1, :, :], ps_t[:, 1, 0:KT * P].rearrange("p (k s) -> p k s", s=P)
                                        ).then_inc(hid_t_done[1], 1)

                    def body(n, par, pair, place):
                        if not gated:
                            eng.wait_ge(weights_landed[par], (pair + 1) * (16 * n_w))
                        first(n, par, 0)
                        first(n, par, 1)
                        turned(n)
                        eng.wait_ge(down_done, count(1, n, 0))
                        eng.wait_ge(y_stored, (n + 1) * 16)
                        if gated:
                            eng.tensor_copy(y[:, :], ps_y[:, 0:D]).then_inc(y_done, 1)
                        else:
                            eng.tensor_tensor(y[:, :], ps_y[:, 0:D], b_down[par][:, :], ALU.add).then_inc(y_done, 1)

                    experts_loop(eng, body)

        with ExitStack() as inner:
            got = inner.enter_context(nc.sbuf_tensor(f"{name}_got", [P, TILES, TOP, D], F32))
            gathered = [sem(f"gathered{i}") for i in range(TILES)]
            first_added, carried = sem("first_added"), sem("carried")
            carrier = inner.enter_context(nc.sbuf_tensor(f"{name}_carrier", [P, 1], F32))
            with nc.Block() as block:
                @block.gpsimd
                def _(eng):
                    last = eng.value_load(base_i[0:1, EXPERTS:EXPERTS + 1], min_val=EXPERTS, max_val=MAX_BLOCKS)
                    eng.wait_ge(y_stored, (last + 1) * 16)
                    eng.wait_ge(rows_landed, (last + 2) * 16)
                    eng.tensor_tensor(carrier[:, :], gate[:, 0, 0:1], gate[:, 0, 0:1], ALU.add).then_inc(carried, 1)
                    eng.wait_ge(carried, 1)
                    for t in range(TILES):
                        for k in range(TOP):
                            eng.indirect_dma_start(got[:, t, k, :], None, table,
                                                   bass.IndirectOffsetOnAxis(ap=slot[:, t, k:k + 1], axis=0)
                                                   ).then_inc(gathered[t], 16)

                @block.vector
                def _(eng):
                    def second(t):
                        eng.wait_ge(first_added, t + 1)
                        eng.scalar_tensor_tensor(out=X[:, t, :], in0=got[:, t, 1, :], scalar=gate[:, t, 1:2],
                                                 in1=X[:, t, :], op0=ALU.mult, op1=ALU.add)

                    for t in range(TILES):
                        eng.wait_ge(gathered[t], 16 * TOP)
                        eng.scalar_tensor_tensor(out=X[:, t, :], in0=got[:, t, 0, :], scalar=gate[:, t, 0:1],
                                                 in1=X[:, t, :], op0=ALU.mult, op1=ALU.add).then_inc(first_added, 1)
                        if t >= 1:
                            second(t - 1)
                    second(TILES - 1)
    nc.clear_and_free_semaphores(used)
    nc.all_engine_barrier()


OUT_NAME = "out_0_dram"


def decoder(nc, a):
    with ExitStack() as stack:
        def sb(n, shape, dt=F32):
            return stack.enter_context(nc.sbuf_tensor(n, shape, dt))

        def sem(n):
            return nc.alloc_semaphore(n)

        X = sb("X", [P, TILES, D])
        ident, identb = sb("ident", [P, P]), sb("identb", [P, P], BF16)
        hmask16, hmask64 = sb("hmask16", [P, 8]), sb("hmask64", [P, 2])
        wmask = sb("wmask", [P, QT_N, S - HALF_WINDOW], BF16)
        neg_half, eps = sb("neg_half", [P, QT_N]), sb("eps", [P, QT_N])
        env = dict(X=X, ident=ident, identb=identb, hmask16=hmask16, hmask64=hmask64, wmask=wmask, neg_half=neg_half, eps=eps)
        before, ones = sb("before", [P, P]), sb("ones", [P, P])
        numbers, regions = sb("numbers", [P, LISTED]), sb("regions", [P, EXPERTS])
        env.update(ones=ones, numbers=numbers, regions=regions)
        zero = sb("zero", [P, 1, D])
        taken = [sb(f"taken{i}", [P, EXPERTS]) for i in range(2)]
        gate, slot = sb("gate", [P, TILES, TOP]), sb("slot", [P, TILES, TOP], I32)
        wq0, wk0, wv0 = sb("wq0", [P, DT, D]), sb("wk0", [P, DT, D]), sb("wv0", [P, DT, D])
        wo0, bo0 = sb("wo0", [P, DT, D]), sb("bo0", [P, D])
        wq1, wk1, wv1 = sb("wq1", [P, DT, D]), sb("wk1", [P, DT, D]), sb("wv1", [P, DT, D])
        wo1, bo1, bv1 = sb("wo1", [P, DT, D]), sb("bo1", [P, D]), sb("bv1", [P, D])
        bq1, bq1s, bk1 = sb("bq1", [P, DT]), sb("bq1s", [P, DT]), sb("bk1", [P, DT])
        wr0, wr1 = sb("wr0", [P, DT, EXPERTS]), sb("wr1", [P, DT, EXPERTS])
        wq3, wk3, wv3 = sb("wq3", [P, DT, D]), sb("wk3", [P, DT, D]), sb("wv3", [P, DT, D])
        wo3, bo3 = sb("wo3", [P, DT, D]), sb("bo3", [P, D])
        gamma, beta = sb("gamma", [P, DT]), sb("beta", [P, DT])

        consts, cleared, x_first, x_rest = sem("consts"), sem("cleared"), sem("x_first"), sem("x_rest")
        w0_landed, w1_landed, w3_landed = sem("w0_landed"), sem("w1_landed"), sem("w3_landed")
        wr_landed, ln_landed = sem("wr_landed"), sem("ln_landed")
        bias_scaled, zeroed, stored = sem("bias_scaled"), sem("zeroed"), sem("stored")
        table = nc.dram_tensor("expert_table", [ROWS, D], F32, kind="Internal").ap()

        x_v = a["x"].rearrange("b (q p) d -> p (b q) d", p=P)
        out_v = a["out"].rearrange("b (q p) d -> p (b q) d", p=P)

        def tiled(w):
            return w.rearrange("(t p) n -> p t n", p=P)

        with nc.Block() as block:
            @block.vector
            def _(eng):
                for m in (wq3, wk3, wv3):
                    eng.memset(m[:, :, :], 0.0).then_inc(cleared, 1)
                eng.memset(zero[:, :, :], 0.0).then_inc(cleared, 1)

            @block.gpsimd
            def _(eng):
                n = [0]

                def linked(ins):
                    n[0] += 1
                    ins.then_inc(consts, 1)
                    eng.wait_ge(consts, n[0])

                for m in (ident, identb):
                    linked(eng.memset(m[:, :], 0.0))
                    linked(eng.affine_select(out=m[:, :], in_=m[:, :], compare_op=ALU.not_equal, fill=1.0, base=0,
                                             pattern=[[-1, P]], channel_multiplier=1))
                for m, w in ((hmask16, 16), (hmask64, 64)):
                    linked(eng.memset(m[:, :], 1.0))
                    linked(eng.affine_select(out=m[:, :], in_=m[:, :], compare_op=ALU.is_ge, fill=0.0, base=0,
                                             pattern=[[-w, P // w]], channel_multiplier=1))
                    linked(eng.affine_select(out=m[:, :], in_=m[:, :], compare_op=ALU.is_ge, fill=0.0, base=w - 1,
                                             pattern=[[w, P // w]], channel_multiplier=-1))
                linked(eng.memset(wmask[:, :, :], 0.0))
                for q in range(QT_N):
                    apart = q * (P - HALF_WINDOW)
                    m = wmask[:, q, :]
                    for sign in (1, -1):
                        linked(eng.affine_select(out=m, in_=m, compare_op=ALU.is_ge, fill=MASKED,
                                                 base=HALF_WINDOW - sign * apart, pattern=[[sign, S - HALF_WINDOW]],
                                                 channel_multiplier=-sign))
                linked(eng.memset(neg_half[:, :], -0.5))
                linked(eng.memset(eps[:, :], LN_EPS))
                linked(eng.memset(ones[:, :], 1.0))
                linked(eng.affine_select(out=before[:, :], in_=ones[:, :], compare_op=ALU.is_gt, fill=0.0,
                                         base=0, pattern=[[1, P]], channel_multiplier=-1))
                linked(eng.iota(numbers[:, :], pattern=[[1, LISTED]], base=0, channel_multiplier=0,
                                allow_small_or_imprecise_dtypes=True))
                for m in (regions, *taken):
                    linked(eng.iota(m[:, :], pattern=[[REGION * P, EXPERTS]], base=0, channel_multiplier=0,
                                    allow_small_or_imprecise_dtypes=True))

            @block.scalar
            def _(eng):
                for dst, w in ((wq0, "wq0"), (wk0, "wk0"), (wv0, "wv0"), (wo0, "wo0")):
                    eng.dma_start(dst[:, :, :], tiled(a[w])).then_inc(w0_landed, 16)
                eng.dma_start(bo0[:, :], a["bo0"].unsqueeze(0).to_broadcast([P, D])).then_inc(w0_landed, 16)

            @block.sync
            def _(eng):
                eng.dma_start(X[:, 0:QT_N, :], x_v[:, 0:QT_N, :]).then_inc(x_first, 16)
                eng.dma_start(X[:, QT_N:TILES, :], x_v[:, QT_N:TILES, :]).then_inc(x_rest, 16)

                def column(dst, v, s):
                    eng.dma_start(dst[:, :], v.rearrange("(t p) -> p t", p=P), allow_slow_non_contiguous=True).then_inc(s, 16)

                def row(dst, v, s):
                    eng.dma_start(dst[:, :], v.unsqueeze(0).to_broadcast([P, D])).then_inc(s, 16)

                for dst, w in ((wq1, "wq1"), (wk1, "wk1"), (wv1, "wv1"), (wo1, "wo1")):
                    eng.dma_start(dst[:, :, :], tiled(a[w])).then_inc(w1_landed, 16)
                column(bq1, a["bq1"], w1_landed)
                column(bk1, a["bk1"], w1_landed)
                row(bv1, a["bv1"], w1_landed)
                row(bo1, a["bo1"], w1_landed)
                eng.wait_ge(cleared, 4)
                eng.dma_start(table[0:ROWS - 2 * P, :].rearrange("(k p) d -> p k d", p=P), zero[:, :, :].to_broadcast([P, ROWS // P - 2, D])
                              ).then_inc(zeroed, 16)
                for dst, w in ((wr0, "wr0"), (wr1, "wr1")):
                    eng.dma_start(dst[:, :, :], tiled(a[w])).then_inc(wr_landed, 16)
                column(gamma, a["gamma"], ln_landed)
                column(beta, a["beta"], ln_landed)
                for dst, w in ((wq3, "wq3"), (wk3, "wk3"), (wv3, "wv3")):
                    for h in range(HEADS):
                        r = h % 8 * 16
                        eng.dma_start(dst[r:r + 16, h // 8, h * 16:(h + 1) * 16], a[w]).then_inc(w3_landed, 16)
                eng.dma_start(wo3[:, :, :], tiled(a["wo3"])).then_inc(w3_landed, 16)
                row(bo3, a["bo3"], w3_landed)

        W0, W1, W3 = 5 * 16, 8 * 16, (3 * HEADS + 2) * 16
        routes = [dict(wr=wr, taken=t, experts=numbers[:, 0:EXPERTS], before=before, ones=ones, gate=gate, slot=slot,
                       table=table, zero=zero, zeroed=((zeroed, 16),)) for wr, t in ((wr0, taken[0]), (wr1, taken[1]))]
        attention(nc, "L0a", env, dh=16, windowed=True, q_scale=16 ** -0.5, wq=wq0, wk=wk0, wv=wv0, wo=wo0, bo=bo0,
                  x_landed=((x_first, 16), (x_rest, 16)), w_landed=((w0_landed, W0),))
        with nc.Block() as block:
            @block.scalar
            def _(eng):
                eng.wait_ge(w1_landed, W1)
                eng.activation(bq1s[:, :], bq1[:, :], ACT.Copy, scale=16 ** -0.5).then_inc(bias_scaled, 1)
                eng.wait_ge(bias_scaled, 1)
        attention(nc, "L0x", env, dh=16, cross=True, q_scale=16 ** -0.5, wq=wq1, wk=wk1, wv=wv1, wo=wo1, bq=bq1s,
                  bk=bk1, bv=bv1, bo=bo1, ctx_dram=a["ctx"], w_landed=((w1_landed, W1), (wr_landed, 32)), route=routes[0])
        moe(nc, "L0f", env, 682, True, a["w1_0"], a["w2_0"], a["w3_0"], route=routes[0])
        with ExitStack() as inner:
            wq2, wk2, wv2 = (inner.enter_context(nc.sbuf_tensor(n, [P, DT, 1024], F32)) for n in ("wq2", "wk2", "wv2"))
            wo2 = inner.enter_context(nc.sbuf_tensor("wo2", [P, 8, D], F32))
            w2_landed = sem("w2_landed")
            with nc.Block() as block:
                @block.sync
                def _(eng):
                    for dst, w in ((wq2, "wq2"), (wk2, "wk2"), (wv2, "wv2"), (wo2, "wo2")):
                        eng.dma_start(dst[:, :, :], tiled(a[w])).then_inc(w2_landed, 16)
            attention(nc, "L1a", env, dh=64, q_scale=1 / 8, wq=wq2, wk=wk2, wv=wv2, wo=wo2, affine=(gamma, beta),
                      w_landed=((w2_landed, 64), (ln_landed, 32)))
        attention(nc, "L1x", env, dh=16, cross=True, q_scale=D ** -0.5, wq=wq3, wk=wk3, wv=wv3, wo=wo3, bo=bo3,
                  ctx_dram=a["ctx"], w_landed=((w3_landed, W3),), route=routes[1])
        moe(nc, "L1f", env, 1024, False, a["w1_1"], None, a["w2_1"], a["b1_1"], a["b2_1"], route=routes[1])
        with nc.Block() as block:
            @block.sync
            def _(eng):
                eng.dma_start(out_v, X[:, :, :]).then_inc(stored, 16)
                eng.wait_ge(stored, 16)


def kernel(**inputs):
    import numpy as np
    import concourse.bacc as bacc
    from concourse.bass_utils import run_bass_kernel_spmd

    i = {k: np.asarray(v) for k, v in inputs.items()}
    qkv = i["L0_attn_W_qkv"]
    laid = {
        "x": i["x"], "ctx": i["ctx_1024"],
        "wq0": qkv[:, 0:256], "wk0": qkv[:, 256:512], "wv0": qkv[:, 512:768],
        "wo0": i["L0_attn_W_proj"], "bo0": i["L0_attn_b_proj"],
        "wq1": i["L0_xattn_wq"].T, "wk1": i["L0_xattn_wk"].T, "wv1": i["L0_xattn_wv"].T, "wo1": i["L0_xattn_wo"].T,
        "bq1": i["L0_xattn_bq"], "bk1": i["L0_xattn_bk"], "bv1": i["L0_xattn_bv"], "bo1": i["L0_xattn_bo"],
        "wr0": i["L0_ffn_Wg"].T, "w1_0": i["L0_ffn_W1"].transpose(0, 2, 1), "w2_0": i["L0_ffn_W2"].transpose(0, 2, 1),
        "w3_0": i["L0_ffn_W3"].transpose(0, 2, 1),
        "gamma": i["L1_attn_ln_gamma"], "beta": i["L1_attn_ln_beta"],
        "wq2": i["L1_attn_Wq"], "wk2": i["L1_attn_Wk"], "wv2": i["L1_attn_Wv"], "wo2": i["L1_attn_Wo"],
        "wq3": i["L1_xattn_Wq"].T, "wk3": i["L1_xattn_Wk"].T, "wv3": i["L1_xattn_Wv"].T, "wo3": i["L1_xattn_Wo"].T,
        "bo3": i["L1_xattn_bo"],
        "wr1": i["L1_ffn_Wr"].T, "w1_1": i["L1_ffn_W1"].transpose(0, 2, 1), "b1_1": i["L1_ffn_b1"],
        "w2_1": i["L1_ffn_W2"].transpose(0, 2, 1), "b2_1": i["L1_ffn_b2"],
    }
    nc = bacc.Bacc("TRN2", target_bir_lowering=False, num_devices=1)
    arrays, aps = {}, {}
    for name, v in laid.items():
        v = np.ascontiguousarray(v)
        arrays[f"in_{name}_dram"] = v
        aps[name] = nc.dram_tensor(f"in_{name}_dram", v.shape, mybir.dt.from_np(v.dtype), kind="ExternalInput").ap()
    aps["out"] = nc.dram_tensor(OUT_NAME, (B, S, D), F32, kind="ExternalOutput").ap()
    decoder(nc, aps)
    r = run_bass_kernel_spmd(nc, [arrays], core_ids=[0])
    return r.results[0][OUT_NAME]
```

```python
from contextlib import ExitStack

import concourse.bass as bass
from concourse import mybir

P = 128
ALU = mybir.AluOpType
ACT = mybir.ActivationFunctionType
AX = mybir.AxisListType
F32 = mybir.dt.float32
BF16 = mybir.dt.bfloat16
I32 = mybir.dt.int32
U32 = mybir.dt.uint32

B, S, D = 8, 256, 256
SC = 77
HEADS = 16
QT_N = S // P
DT = D // P
TILES = B * QT_N
LN_EPS = 1e-5
LOOK = 4
TL = 2
NB = 4
HALF_WINDOW = 64
MASKED = -1.0e30
EXPERTS = 8
TOP = 2
REGION = TILES
SPARES = QT_N * TOP + 1
TABLE_BLOCKS = EXPERTS * REGION + SPARES


def count(per_batch, b, j):
    return (b + 1) * per_batch + j + 1


def attention(nc, name, env, dh, windowed=False, cross=False, affine=None, q_scale=1.0,
              wq=None, wk=None, wv=None, wo=None, bq=None, bk=None, bv=None, bo=None,
              ctx_dram=None, x_landed=(), w_landed=(), route=None,
              other_loads=None, pending=None):
    X, ident, identb, neg_half, eps = env["X"], env["ident"], env["identb"], env["neg_half"], env["eps"]
    wmask = env.get("wmask")
    hpc = P // dh
    nct = HEADS // hpc
    hmask = env["hmask16"] if dh == 16 else env["hmask64"]
    G = 2 if cross else 1
    OUT_EARLY = cross
    NU = HEADS // G
    keys = SC if cross else S
    width = SC if cross else (S - HALF_WINDOW if windowed else S)
    first_key = (0, HALF_WINDOW) if windowed else (0, 0)
    dv = 32 if dh == 16 else 64
    HG = P // dv
    NG = HEADS // HG
    UG = HG // G
    GP = dv // dh
    NT = NG // GP
    NF_OUT = NT + 1
    NV = 1 if cross else S // P
    v_n = SC if cross else P

    def head_of(slot):
        return slot // 8 * 8 + slot % 4 * 2 + slot % 8 // 4 if dh == 16 else slot

    vw = HEADS * dh
    per_bank = 512 // S
    fev = [("ct", 0), ("xt", 0)] if cross else [("xt", 0)]
    qev = [("q", i) for i in range((nct + per_bank - 1) // per_bank)]
    if cross:
        kev = [("k", c) for c in range(nct)] + [("v", 0)]
        vev = []
    else:
        kev = [("k", i) for i in range((nct + per_bank - 1) // per_bank)]
        vev = [("v", v, i) for v in range(NV) for i in range((vw + 511) // 512)]
        if vw < 512:
            vev = [("v", 0, 0)]
    fev += qev + vev
    NF, NK = len(fev), len(kev)
    f_at = {e: i for i, e in enumerate(fev)}
    plan = {}
    start = 2
    if cross:
        plan = {1: [("f", ("ct", 0))], 2: [("f", ("xt", 0))], 3: [("f", qev[0]), ("k", kev[0])], 4: [("k", kev[1])],
                6: [("k", kev[2])]}
    else:
        plan[start] = [("f", ("xt", 0))]
        order = []
        for a, c in zip(qev, kev):
            order += [("k", c), ("f", a)]
        order += [("f", e) for e in vev]
        per_step = (len(order) + NU - LOOK - start - 3) // (NU - LOOK - start - 2)
        for i, o in enumerate(order):
            plan.setdefault(start + 1 + i // per_step, []).append(o)

    with ExitStack() as stack:
        def sb(n, shape, dt=F32):
            return stack.enter_context(nc.sbuf_tensor(f"{name}_{n}", shape, dt))

        used = []

        def sem(n):
            used.append(nc.alloc_semaphore(f"{name}_{n}"))
            return used[-1]

        ps_s = stack.enter_context(nc.psum_tensor(f"{name}_ps_s", [P, 2, 512], F32))
        ps_t = stack.enter_context(nc.psum_tensor(f"{name}_ps_t", [P, 2, 512], F32))
        ps_o = stack.enter_context(nc.psum_tensor(f"{name}_ps_o", [P, 512], F32))
        RING = 1 if route else 2
        ps_f = stack.enter_context(nc.psum_tensor(f"{name}_ps_f", [P, RING, 512], F32))
        ps_r = stack.enter_context(nc.psum_tensor(f"{name}_ps_r", [P, 512], F32)) if route else None
        ps_k = stack.enter_context(nc.psum_tensor(f"{name}_ps_k", [P, 512], F32))

        stats = sb("stats", [P, QT_N, 6])
        mv = sb("mv", [P, QT_N, 2])
        veps = sb("veps", [P, QT_N])
        rstd = sb("rstd", [P, QT_N])
        carrier = sb("carrier", [P, 1])
        xn = sb("xn", [P, QT_N, D])
        xt = sb("xt", [P, DT, S])
        ctx_in = sb("ctx_in", [P, 2, D]) if cross else None
        ct = sb("ct", [P, DT, SC]) if cross else None
        q_t = [sb(f"q_t{i}", [P, nct, S]) for i in range(2)]
        k_m = [sb(f"k_m{i}", [P, HEADS, keys]) for i in range(2)]
        v_w = dv if dh == 16 else dh
        v_s = [sb(f"v_s{i}", [P, NV, HEADS, v_w]) for i in range(2)]
        pitch = S + HALF_WINDOW if windowed else width
        prob = sb("prob", [P, NB, QT_N * G, pitch])
        prob_flat = prob[:, :, :, :].rearrange("p j r k -> p j (r k)")
        nmax = sb("nmax", [P, NB, QT_N * G])
        total = sb("total", [P, NB, QT_N * G])
        rtot = sb("rtot", [P, NB, QT_N * G])
        prob_t = [sb(f"prob_t{i}", [P, UG, 512]) for i in range(2)]
        o_t = sb("o_t", [P, NT, S])

        stats_done, var_done, rstd_done, xn_done = sem("stats"), sem("var"), sem("rstd"), sem("xn")
        ctx_landed = [sem("ctx0"), sem("ctx1")] if cross else None
        front_done, front_free = sem("front_done"), sem("front_free")
        keys_done, keys_free = sem("keys_done"), sem("keys_free")
        scores_done, max_done = sem("scores"), sem("max")
        exp_done, rtot_done, norm_done = sem("exp"), sem("rtot"), sem("norm")
        turned, turned_free = sem("turned"), [sem("turned_free0"), sem("turned_free1")]
        out_done, out_free = sem("out_done"), sem("out_free")
        init_done = sem("init")
        INITS = (2 if dh == 16 else 0) + (NB if windowed else 0)
        NO = NG + 1
        bias_done, veps_done, carried = sem("bias"), sem("veps"), sem("carried")
        if route:
            r_stats, r_mv = sb("r_stats", [P, QT_N, 6]), sb("r_mv", [P, QT_N, 2])
            r_veps, r_rstd = sb("r_veps", [P, QT_N]), sb("r_rstd", [P, QT_N])
            xr, xr_t = sb("xr", [P, 2, QT_N, D]), sb("xr_t", [P, DT, S])
            logits, top = sb("logits", [P, QT_N, EXPERTS]), sb("top", [P, QT_N, 8])
            index, index_f = sb("index", [P, QT_N, 8], U32), sb("index_f", [P, QT_N, TOP])
            chosen, both = sb("chosen", [P, TOP, QT_N, EXPERTS]), sb("both", [P, QT_N, EXPERTS])
            counts = sb("counts", [P, 2, QT_N, EXPERTS])
            place, picked = sb("place", [P, QT_N, EXPERTS]), sb("picked", [P, TOP, QT_N, EXPERTS])
            slot_f, slot_i = sb("slot_f", [P, TOP, QT_N]), sb("slot_i", [P, 2, QT_N, TOP], I32)
            apart, odds, first_gate = sb("apart", [P, QT_N]), sb("odds", [P, QT_N]), sb("first_gate", [P, QT_N])
            r_carrier = sb("r_carrier", [P, 1])
            r_carried, r_copied = sem("r_carried"), sem("r_copied")
            r_cell = sb("r_cell", [P, 1])
            r_init = sem("r_init")
            r_link = sem("r_link")
            r_var_done, r_veps_done, r_rstd_done, r_xn_done = (sem(n) for n in ("r_var", "r_veps", "r_rstd", "r_xn"))
            r_filled, r_emptied = sem("r_filled"), sem("r_emptied")
            both_done, apart_done, odds_done = sem("both"), sem("apart"), sem("odds")
            slot_done, scattered = sem("slot"), [sem("scattered0"), sem("scattered1")]
            LINKS = 15

        def unit(kind, b, j):
            nb = 0
            if j >= NU:
                if kind == "last":
                    return None
                return b + 1, 1, j - NU
            if kind == "first":
                return None
            return b, 0, j

        def run(step, front, tail, eng):
            front(-1, 0)
            for i in range(NU - LOOK, NU):
                step("first", -1, 1, i)

            def batch(kind, b, par):
                for i in range(NU):
                    if kind != "last":
                        front(b, 1 - par, i)
                    step(kind, b, par, i)

            batch("start", 0, 0)
            with eng.Fori(0, B // 2 - 1) as pair:
                for par in (1, 0):
                    batch("mid", pair * 2 + 2 - par, par)
            batch("last", B - 1, 1)
            tail(B - 1, 1)

        with nc.Block() as block:
            def spaced(v):
                return v.rearrange("p (a two) (half d) -> p a (two half) d", two=2, half=2)[:, :, 0::3, :]

            def pairs(v):
                return v.rearrange("p (a two d) -> p a two d", two=2, d=16)

            def evacuate(eng, which, b, par, j):
                g, r = j // UG, j % UG
                eng.wait_ge(turned, count(NU, b, j))
                if r < 2:
                    eng.wait_ge(out_done, count(NO, b, g - 2) if g >= 2 else count(NO, b - 1, NG - 2 + g))
                dst, src = prob_t[g % 2], ps_t
                if which == "vector":
                    ins = eng.tensor_copy(dst[0:v_n, r, :], src[0:v_n, j % 2, :])
                else:
                    ins = eng.activation(dst[0:v_n, r, :], src[0:v_n, j % 2, :], ACT.Copy)
                ins.then_inc(turned_free[j % 2], 1)

            @block.sync
            def _(eng):
                if not cross:
                    if other_loads:
                        other_loads(eng)
                    return

                def load(b, par, i):
                    if i is not None and i != 0:
                        return
                    if i is not None:
                        eng.wait_ge(front_done, count(NF, b - 1, f_at[("ct", 0)]))
                    eng.dma_start(ctx_in[0:SC, par, :], ctx_dram[bass.ds(b + 1, 1)].rearrange("a s d -> (a s) d")
                                  ).then_inc(ctx_landed[par], 16)

                def step(kind, b, par, i):
                    if kind == "start" and i == 1 and other_loads:
                        other_loads(eng)

                run(step, lambda b, par, i=None: load(b, par, i), lambda b, par: None, eng)

            @block.vector
            def _(eng):
                if route:
                    for s, n in ((r_link, LINKS), (r_var_done, 1), (r_xn_done, 1), (r_copied, 3), (both_done, 1), (apart_done, 1), (slot_done, 1)):
                        eng.sem_inc(s, n)
                for s, n in ((stats_done, QT_N), (var_done, 1), (xn_done, QT_N), (keys_free, NK),
                             (max_done, NU), (rtot_done, NU),
                             (turned_free[1], NU // 2)):
                    eng.sem_inc(s, n)
                eng.sem_inc(out_free, 1)
                for s, v in x_landed[:1]:
                    eng.wait_ge(s, v)

                def front(b, par, i=None):
                    nb = b + 1
                    if i is None or i == 0:
                        if i == 0:
                            for s, v in x_landed[1:]:
                                eng.wait_ge(s, v)
                        if pending and isinstance(b, int):
                            for t in range((b + 1) * QT_N, (b + 2) * QT_N):
                                pending["add"](eng, t)
                            eng.wait_ge(pending["added"], (b + 2) * QT_N)
                        for q in range(QT_N):
                            eng.bn_stats(stats[:, q, :], X[:, bass.ds(nb * QT_N + q, 1), :].rearrange("p a d -> p (a d)")
                                         ).then_inc(stats_done, 1)
                        if i is not None:
                            eng.wait_ge(carried, nb)
                        eng.wait_ge(stats_done, count(QT_N, nb, QT_N - 1))
                        eng.tensor_copy(carrier[:, :], stats[:, 0, 0:1]).then_inc(carried, 1)
                        for q in range(QT_N):
                            ins = eng.bn_aggr(mv[:, q, :], stats[:, q, :])
                        ins.then_inc(var_done, 1)
                    if i is None or i == 1:
                        eng.wait_ge(rstd_done, count(1, nb, 0))
                        for q in range(QT_N):
                            if q == 0:
                                eng.wait_ge(front_done, count(NF, nb - 1, f_at[("xt", 0)]))
                            eng.tensor_scalar(xn[:, q, :], X[:, bass.ds(nb * QT_N + q, 1), :].rearrange("p a d -> p (a d)"),
                                              mv[:, q, 0:1], rstd[:, q:q + 1], ALU.subtract, ALU.mult
                                              ).then_inc(xn_done, 1)
                    if i is None:
                        if dh == 16:
                            for p in range(2):
                                eng.memset(v_s[p][:, :, :, :], 0.0).then_inc(init_done, 1)
                        if windowed:
                            for j in range(NB):
                                eng.memset(prob[:, j, :, :], 0.0).then_inc(init_done, 1)
                    for st, evs in sorted(plan.items()):
                        if i is not None and st != i:
                            continue
                        for ring, ev in evs:
                            if ring == "k" and (i is None or not windowed):
                                key_event(nb, par, ev)
                    if windowed and i is not None and 0 <= i - key_step < HEADS // 2:
                        masked_keys(nb, par, (i - key_step) * 2 // hpc, (i - key_step) * 2 % hpc)

                key_step = [st for st, evs in plan.items() for ring, _ in evs if ring == "k"][0]

                def masked_keys(nb, par, c, h0):
                    eng.wait_ge(keys_done, count(NK, nb, c // per_bank))
                    src = ps_k[:, c % per_bank * S:(c % per_bank + 1) * S].unsqueeze(1).to_broadcast([P, 2, S])
                    m = hmask[:, h0:h0 + 2].unsqueeze(2).to_broadcast([P, 2, S])
                    ins = eng.tensor_tensor(k_m[par][:, c * hpc + h0:c * hpc + h0 + 2, :], src, m, ALU.mult)
                    if (c + 1) % per_bank == 0 and h0 + 2 == hpc:
                        ins.then_inc(keys_free, 1)

                def key_event(nb, par, ev):
                    e = kev.index(ev)
                    eng.wait_ge(keys_done, count(NK, nb, e))
                    if ev[0] == "k" and cross:
                        for c in [ev[1]]:
                            src = ps_k[:, c * SC:(c + 1) * SC].unsqueeze(1).to_broadcast([P, hpc, SC])
                            m = hmask[:, 0:hpc].unsqueeze(2).to_broadcast([P, hpc, SC])
                            dst = k_m[par][:, c * hpc:(c + 1) * hpc, :]
                            if bk is not None:
                                ins = eng.scalar_tensor_tensor(out=dst, in0=src, scalar=bk[:, c:c + 1], in1=m,
                                                               op0=ALU.add, op1=ALU.mult)
                            else:
                                ins = eng.tensor_tensor(dst, src, m, ALU.mult)
                        ins.then_inc(keys_free, 1)
                    elif ev[0] == "v":
                        dst = spaced(v_s[par][0:SC, 0, :, :])
                        src = pairs(ps_k[0:SC, 0:D])
                        eng.wait_ge(init_done, INITS)
                        if bv is not None:
                            ins = eng.tensor_tensor(dst, src, pairs(bv[0:SC, :]), ALU.add)
                        else:
                            ins = eng.tensor_copy(dst, src)
                        ins.then_inc(keys_free, 1)
                    else:
                        for c in range(ev[1] * per_bank, (ev[1] + 1) * per_bank):
                            for h0 in range(0, hpc, 2):
                                masked_keys(nb, par, c, h0)

                def step(kind, b, par, i):
                    u = unit(kind, b, i + TL)
                    if u:
                        totals(u[0], u[2])
                    u = unit(kind, b, i)
                    if u and u[2] % 2 == 1:
                        evacuate(eng, "vector", u[0], par, u[2])
                    u = unit(kind, b, i + LOOK)
                    if u:
                        nb, nxt, j = u
                        eng.wait_ge(scores_done, count(NU, nb, j))
                        eng.wait_ge(exp_done, count(NU, nb, j - NB))
                        src = ps_s[:, j % 2, 0:QT_N * G * width].rearrange("p (a k) -> p a k", k=width)
                        eng.tensor_reduce(nmax[:, j % NB, :], src, AX.X, ALU.max, negate=True).then_inc(max_done, 1)
                    if kind in ("mid", "last") and i == 1:
                        add_projection(b - 1)
                    if kind in ("mid", "last"):
                        route_step(b - 1, 1 - par, i)
                    if pending and kind == "start" and i >= 2:
                        if i + 2 < TILES:
                            pending["add"](eng, i + 2)
                        if i == NU - 1:
                            eng.wait_ge(pending["added"], TILES)

                def route_step(b, par, i):
                    if not route:
                        return
                    links = [{1: 0, 5: 1, 6: 5, 7: 8}.get(i, 0)]

                    def linked(ins):
                        ins.then_inc(r_link, 1)
                        eng.wait_ge(r_link, count(LINKS, b, links[0]))
                        links[0] += 1

                    def carry(j):
                        eng.wait_ge(r_copied, count(3, b, j - 1))
                        eng.tensor_copy(r_carrier[:, :], eps[:, 0:1]).then_inc(r_copied, 1)

                    if i == 1:
                        eng.wait_ge(out_free, count(NF_OUT, b, NT))
                        carry(0)
                        for q in range(QT_N):
                            ins = eng.bn_stats(r_stats[:, q, :], X[:, bass.ds(b * QT_N + q, 1), :].rearrange("p a d -> p (a d)"))
                        linked(ins)
                        carry(1)
                        for q in range(QT_N):
                            ins = eng.bn_aggr(r_mv[:, q, :], r_stats[:, q, :])
                        ins.then_inc(r_var_done, 1)
                    elif i == 2:
                        eng.wait_ge(r_rstd_done, count(1, b, 0))
                        eng.wait_ge(scattered[par], 32 * (b - par) + (64 if par else 16))
                        for q in range(QT_N):
                            ins = eng.tensor_scalar(xr[:, par, q, :], X[:, bass.ds(b * QT_N + q, 1), :].rearrange("p a d -> p (a d)"),
                                                    r_mv[:, q, 0:1], r_rstd[:, q:q + 1], ALU.subtract, ALU.mult)
                        ins.then_inc(r_xn_done, 1)
                    elif i == 5:
                        eng.wait_ge(r_emptied, count(3, b, 1))
                        carry(2)
                        for q in range(QT_N):
                            ins = eng.max(top[:, q, :], logits[:, q, :])
                        linked(ins)
                        eng.tensor_tensor(apart[:, :], top[:, :, 1], top[:, :, 0], ALU.subtract).then_inc(apart_done, 1)
                        for q in range(QT_N):
                            ins = eng.max_index(index[:, q, :], top[:, q, :], logits[:, q, :])
                        linked(ins)
                        linked(eng.tensor_copy(index_f[:, :, :], index[:, :, 0:TOP]))
                        for k in range(TOP):
                            ins = eng.tensor_tensor(chosen[:, k, :, :], route["experts"][:, :].unsqueeze(1).to_broadcast([P, QT_N, EXPERTS]),
                                                    index_f[:, :, k].unsqueeze(2).to_broadcast([P, QT_N, EXPERTS]), ALU.is_equal)
                        linked(ins)
                        eng.tensor_tensor(both[:, :, :], chosen[:, 0, :, :], chosen[:, 1, :, :], ALU.add).then_inc(both_done, 1)
                        assert links[0] == 5
                    elif i == 6:
                        eng.wait_ge(odds_done, count(1, b, 0))
                        gate = route["gate"][:, bass.ds(b * QT_N, QT_N), :]
                        linked(eng.tensor_scalar(first_gate[:, :], odds[:, :], 1.0, None, ALU.add))
                        linked(eng.reciprocal(first_gate[:, :], first_gate[:, :]))
                        eng.tensor_copy(gate[:, :, 0], first_gate[:, :])
                        linked(eng.tensor_tensor(gate[:, :, 1], first_gate[:, :], odds[:, :], ALU.mult))
                        assert links[0] == 8
                    elif i == 7:
                        taken = route["taken"]
                        eng.wait_ge(r_emptied, count(3, b, 2))
                        for q in range(QT_N):
                            linked(eng.tensor_tensor(place[:, q, :], counts[:, 0, q, :], taken[:, :], ALU.add))
                            linked(eng.tensor_tensor(taken[:, :], counts[:, 1, q, :], taken[:, :], ALU.add))
                        linked(eng.tensor_tensor(picked[:, :, :, :], chosen[:, :, :, :],
                                                 place[:, :, :].unsqueeze(1).to_broadcast([P, TOP, QT_N, EXPERTS]), ALU.mult))
                        linked(eng.tensor_reduce(slot_f[:, :, :], picked[:, :, :, :], AX.X, ALU.add))
                        by_token = slot_f[:, :, :].rearrange("p k t -> p t k")
                        eng.tensor_copy(route["slot"][:, bass.ds(b * QT_N, QT_N), :], by_token)
                        eng.wait_ge(scattered[par], 32 * (b - par) + (64 if par else 16))
                        linked(eng.tensor_copy(slot_i[:, par, :, :], by_token))
                        assert links[0] == LINKS
                        eng.sem_inc(slot_done, 1)

                def totals(nb, j):
                    eng.wait_ge(exp_done, count(NU, nb, j))
                    eng.wait_ge(norm_done, count(NU, nb, j - NB))
                    eng.reciprocal(rtot[:, j % NB, :], total[:, j % NB, :]).then_inc(rtot_done, 1)

                def add_projection(b):
                    eng.wait_ge(out_done, count(NO, b, NG))
                    xb = X[:, bass.ds(b * QT_N, QT_N), :]
                    if bo is not None:
                        eng.wait_ge(bias_done, count(1, b, 0))
                    eng.tensor_tensor(xb, xb, ps_o[:, :].rearrange("p (q d) -> p q d", q=QT_N), ALU.add
                                      ).then_inc(out_free, 1)

                def tail(b, par):
                    add_projection(b)
                    for i in range(NU):
                        route_step(b, par, i)
                    if route:
                        route["list_blocks"](eng)

                run(step, front, tail, eng)

            @block.scalar
            def _(eng):
                for s, n in ((front_free, NF), (exp_done, NU), (turned_free[0], NU // 2)):
                    eng.sem_inc(s, n)
                eng.sem_inc(out_free, NT)
                if route:
                    eng.sem_inc(r_emptied, 3)
                    eng.sem_inc(odds_done, 1)

                def front(b, par, i=None):
                    nb = b + 1
                    for st, evs in sorted(plan.items()):
                        if i is not None and st != i:
                            continue
                        for ring, ev in evs:
                            if ring == "f":
                                event(nb, par, ev)

                def event(nb, par, ev):
                    e = f_at[ev]
                    bank = ps_f[:, e % RING, :]
                    eng.wait_ge(front_done, count(NF, nb, e))
                    if ev[0] == "xt":
                        if affine is None:
                            ins = eng.activation(xt[:, :, :], bank.rearrange("p (c s) -> p c s", c=DT), ACT.Copy)
                        else:
                            for c in range(DT):
                                ins = eng.activation(xt[:, c, :], bank[:, c * S:(c + 1) * S], ACT.Identity,
                                                     bias=affine[1][:, c:c + 1], scale=affine[0][:, c:c + 1])
                    elif ev[0] == "ct":
                        ins = eng.activation(ct[:, :, :], bank[:, 0:DT * SC].rearrange("p (c s) -> p c s", c=DT), ACT.Copy)
                    elif ev[0] == "q":
                        for cc in range(per_bank):
                            c = ev[1] * per_bank + cc
                            if bq is not None:
                                ins = eng.activation(q_t[par][:, c, :], bank[:, cc * S:(cc + 1) * S], ACT.Identity,
                                                     bias=bq[:, c:c + 1], scale=q_scale)
                            elif cc == 0:
                                ins = eng.activation(q_t[par][:, c:c + per_bank, :],
                                                     bank.rearrange("p (c s) -> p c s", c=per_bank), ACT.Copy,
                                                     scale=q_scale)
                    else:
                        if dh == 16:
                            eng.wait_ge(init_done, INITS)
                            for v in range(NV):
                                ins = eng.activation(spaced(v_s[par][:, v, :, :]), pairs(bank[:, v * D:(v + 1) * D]), ACT.Copy)
                        else:
                            hh = 512 // dh
                            ins = eng.activation(v_s[par][:, ev[1], ev[2] * hh:(ev[2] + 1) * hh, :],
                                                 bank.rearrange("p (h d) -> p h d", d=dh), ACT.Copy)
                    ins.then_inc(front_free, 1)

                def group_out(b, g):
                    if (g + 1) % GP:
                        return
                    eng.wait_ge(out_done, count(NO, b, g))
                    eng.activation(o_t[:, g // GP, :], ps_o[:, 0:S], ACT.Copy).then_inc(out_free, 1)

                def step(kind, b, par, i):
                    u = unit(kind, b, i)
                    if u and u[2] % 2 == 0:
                        evacuate(eng, "scalar", u[0], par, u[2])
                    if OUT_EARLY:
                        step_group_out(kind, b, i)
                    if kind in ("mid", "last") and i < 5:
                        route_step(b - 1, i)
                    u = unit(kind, b, i + LOOK)
                    if u:
                        nb, nxt, j = u
                        eng.wait_ge(turned, count(NU, nb, j - NB))
                        eng.wait_ge(max_done, count(NU, nb, j))
                        eng.wait_ge(rtot_done, count(NU, nb, j - NB))
                        for r in range(QT_N * G):
                            ins = eng.activation(prob[:, j % NB, r, 0:width], ps_s[:, j % 2, r * width:(r + 1) * width],
                                                 ACT.Exp, bias=nmax[:, j % NB, r:r + 1],
                                                 accum_out=total[:, j % NB, r:r + 1])
                        ins.then_inc(exp_done, 1)
                    if not OUT_EARLY:
                        step_group_out(kind, b, i)
                    if kind in ("mid", "last") and i >= 5:
                        route_step(b - 1, i)

                def step_group_out(kind, b, i):
                    if kind != "first" and i % UG == 0 and i >= UG:
                        group_out(b, i // UG - 1)
                    if kind in ("mid", "last") and i == 0:
                        group_out(b - 1, NG - 1)

                def route_step(b, i):
                    if not route or i not in (3, 4, 5, 6):
                        return
                    if i == 5:
                        eng.wait_ge(apart_done, count(1, b, 0))
                        eng.activation(odds[:, :], apart[:, :], ACT.Exp).then_inc(odds_done, 1)
                        return
                    e = (3, 4, 6).index(i)
                    eng.wait_ge(r_filled, count(3, b, e))
                    w = QT_N * EXPERTS
                    if e == 0:
                        ins = eng.activation(xr_t[:, :, :], ps_r[:, :].rearrange("p (c s) -> p c s", c=DT), ACT.Copy)
                    elif e == 1:
                        ins = eng.activation(logits[:, :, :].rearrange("p q e -> p (q e)"), ps_r[:, 0:w], ACT.Copy)
                    else:
                        ins = eng.activation(counts[:, :, :, :].rearrange("p a q e -> p (a q e)"), ps_r[:, 0:2 * w], ACT.Copy)
                    ins.then_inc(r_emptied, 1)

                def tail(b, par):
                    group_out(b, NG - 1)
                    for i in range(NU):
                        route_step(b, i)

                def front_and_init(b, par, i=None):
                    front(b, par, i)
                    if windowed and i is None:
                        eng.wait_ge(init_done, INITS)

                run(step, front_and_init, tail, eng)

            @block.gpsimd
            def _(eng):
                if route:
                    for s, n in ((r_rstd_done, 1), (r_carried, 1)):
                        eng.sem_inc(s, n)
                    eng.dma_start(route["table"][(TABLE_BLOCKS - 1) * P:TABLE_BLOCKS * P, :],
                                  route["zero"][:, 0, :]).then_inc(scattered[0], 16)
                    eng.iota(slot_i[:, 1, :, :], pattern=[[TOP * P, QT_N], [P, TOP]], base=EXPERTS * REGION * P,
                             channel_multiplier=1).then_inc(r_init, 1)
                    eng.memset(xr[:, 1, :, :], 0.0).then_inc(r_init, 1)
                    eng.wait_ge(r_init, 2)
                eng.sem_inc(rstd_done, 1)
                eng.sem_inc(bias_done, 1)
                eng.sem_inc(norm_done, NU)
                if pending:
                    for t in range(QT_N):
                        pending["gather"](eng, t)

                def front(b, par, i=None):
                    nb = b + 1
                    if i is None or i == 0:
                        eng.wait_ge(var_done, count(1, nb, 0))
                        eng.tensor_tensor(veps[:, :], mv[:, :, 1], eps[:, 0:QT_N], ALU.add).then_inc(veps_done, 1)
                        eng.wait_ge(veps_done, nb + 1)
                        eng.tensor_tensor(rstd[:, :], veps[:, :], neg_half[:, 0:QT_N], ALU.pow).then_inc(rstd_done, 1)

                def route_step(b, par, i):
                    if not route:
                        return
                    if 1 <= i <= QT_N * TOP:
                        send(b - 1, 1 - par, i - 1)
                    if i == 1:
                        eng.wait_ge(r_var_done, count(1, b, 0))
                        eng.tensor_tensor(r_veps[:, :], r_mv[:, :, 1], eps[:, 0:QT_N], ALU.add).then_inc(r_veps_done, 1)
                        eng.wait_ge(r_veps_done, b + 1)
                        eng.tensor_tensor(r_rstd[:, :], r_veps[:, :], neg_half[:, 0:QT_N], ALU.pow).then_inc(r_rstd_done, 1)

                def send(b, par, j):
                    if j == 0:
                        eng.wait_ge(slot_done, count(1, b, 0))
                        eng.wait_ge(r_carried, count(1, b, 0))
                        eng.tensor_tensor(r_cell[:, :], eps[:, 0:1], eps[:, 0:1], ALU.add).then_inc(r_carried, 1)
                        for s, v in route["zeroed"]:
                            eng.wait_ge(s, v)
                    q, k = j // TOP, j % TOP
                    eng.indirect_dma_start(route["table"], bass.IndirectOffsetOnAxis(ap=slot_i[:, par, q, k:k + 1], axis=0),
                                           xr[:, par, q, :], None).then_inc(scattered[par], 16)

                def step(kind, b, par, i):
                    if pending and kind == "first" and i == NU - LOOK:
                        for t in range(QT_N, 2 * QT_N):
                            pending["gather"](eng, t)
                    normalise(kind, b, i)
                    if pending and kind == "start" and i + 2 * QT_N < TILES:
                        pending["gather"](eng, i + 2 * QT_N)
                    if kind in ("mid", "last"):
                        route_step(b - 1, 1 - par, i)
                    if bo is not None and i == 6 and kind != "first":
                        xb = X[:, bass.ds(b * QT_N, QT_N), :]
                        eng.wait_ge(xn_done, count(QT_N, b, QT_N - 1))
                        eng.tensor_tensor(xb, xb, bo[:, :].unsqueeze(1).to_broadcast([P, QT_N, D]), ALU.add
                                          ).then_inc(bias_done, 1)

                def normalise(kind, b, i):
                    u = unit(kind, b, i + TL)
                    if not u:
                        return
                    nb, nxt, j = u
                    eng.wait_ge(rtot_done, count(NU, nb, j))
                    eng.tensor_tensor(prob[:, j % NB, :, 0:width], prob[:, j % NB, :, 0:width],
                                      rtot[:, j % NB, :].unsqueeze(2).to_broadcast([P, QT_N * G, width]), ALU.mult
                                      ).then_inc(norm_done, 1)

                def tail(b, par):
                    if route:
                        for i in range(NU):
                            route_step(b, par, i)
                        for j in range(QT_N * TOP):
                            send(b, par, j)
                        eng.wait_ge(scattered[0], B // 2 * 64 + 16)
                        eng.wait_ge(scattered[1], (B // 2 + 1) * 64)

                run(step, front, tail, eng)

            @block.tensor
            def _(eng):
                for s, n in ((front_done, NF), (keys_done, NK), (scores_done, NU), (turned, NU), (out_done, NO)):
                    eng.sem_inc(s, n)
                if route:
                    eng.sem_inc(r_filled, 3)
                for s, v in w_landed:
                    eng.wait_ge(s, v)

                def front(b, par, i=None):
                    nb = b + 1
                    for st, evs in sorted(plan.items()):
                        if i is not None and st != i:
                            continue
                        for ring, ev in evs:
                            if ring == "f":
                                front_event(nb, par, ev)
                            else:
                                key_event(nb, par, ev)

                def project(out, w, c0, n, rhs, kt_rows=P):
                    for t in range(DT):
                        ins = eng.matmul(out, w[:, t, c0:c0 + n], rhs[:, t, :], start=(t == 0), stop=(t == DT - 1))
                    return ins

                def front_event(nb, par, ev):
                    e = f_at[ev]
                    bank = ps_f[:, e % RING, :]
                    before = e - RING if e >= RING else max(p for p in range(NF) if p % RING == e % RING) - NF
                    eng.wait_ge(front_free, count(NF, nb, before))
                    if ev[0] == "xt":
                        eng.wait_ge(xn_done, count(QT_N, nb, QT_N - 1))
                        for c in range(DT):
                            for q in range(QT_N):
                                ins = eng.transpose(bank[:, c * S + q * P:c * S + (q + 1) * P],
                                                    xn[:, q, c * P:(c + 1) * P], ident[:, :])
                    elif ev[0] == "ct":
                        eng.wait_ge(ctx_landed[par], nb * 8 + 16 - 8 * par)
                        for c in range(DT):
                            ins = eng.transpose(bank[:, c * SC:(c + 1) * SC], ctx_in[0:SC, par, c * P:(c + 1) * P],
                                                ident[0:SC, 0:SC])
                    elif ev[0] == "q":
                        eng.wait_ge(front_free, count(NF, nb, f_at[("xt", 0)]))
                        for cc in range(per_bank):
                            ins = project(bank[:, cc * S:(cc + 1) * S], wq, (ev[1] * per_bank + cc) * P, P, xt)
                    else:
                        eng.wait_ge(front_free, count(NF, nb, f_at[("xt", 0)]))
                        if dh == 16:
                            pieces = [(v * P, v * D, 0, D) for v in range(NV)]
                        else:
                            pieces = [(ev[1] * P, 0, ev[2] * 512, 512)]
                        for r0, o, c0, w in pieces:
                            for t in range(DT):
                                ins = eng.matmul(bank[:, o:o + w], xt[:, t, r0:r0 + P], wv[:, t, c0:c0 + w],
                                                 start=(t == 0), stop=(t == DT - 1))
                    ins.then_inc(front_done, 1)

                def key_event(nb, par, ev):
                    e = kev.index(ev)
                    eng.wait_ge(keys_free, count(NK, nb, e - 1))
                    if cross:
                        eng.wait_ge(front_free, count(NF, nb, f_at[("ct", 0)]))
                    else:
                        eng.wait_ge(front_free, count(NF, nb, f_at[("xt", 0)]))
                    if cross and ev[0] == "k":
                        c = ev[1]
                        ins = project(ps_k[:, c * SC:(c + 1) * SC], wk, c * P, P, ct)
                    elif cross:
                        for t in range(DT):
                            ins = eng.matmul(ps_k[0:SC, 0:D], ct[:, t, :], wv[:, t, :], start=(t == 0), stop=(t == DT - 1))
                    else:
                        for cc in range(per_bank):
                            ins = project(ps_k[:, cc * S:(cc + 1) * S], wk, (ev[1] * per_bank + cc) * P, P, xt)
                    ins.then_inc(keys_done, 1)

                def scores(nb, par, j):
                    eng.wait_ge(exp_done, count(NU, nb, j - 2))
                    c = j * G // hpc
                    last_k = c if cross else c // per_bank
                    eng.wait_ge(keys_free, count(NK, nb, last_k))
                    eng.wait_ge(front_free, count(NF, nb, f_at[("q", c // per_bank)]))
                    for q in range(QT_N):
                        n = G * width
                        out = ps_s[:, j % 2, q * n:(q + 1) * n]
                        k0 = first_key[q]
                        h = head_of(j * G)
                        rhs = k_m[par][:, h:h + 3:2, :] if cross else k_m[par][:, h, k0:k0 + width]
                        ins = eng.matmul(out, q_t[par][:, c, q * P:(q + 1) * P], rhs, start=True, stop=not windowed)
                        if windowed:
                            ins = eng.matmul(out, identb[:, :], wmask[:, q, :], start=False, stop=True)
                    ins.then_inc(scores_done, 1)

                def turn(b, par, j):
                    eng.wait_ge(norm_done, count(NU, b, j))
                    eng.wait_ge(turned_free[j % 2], count(NU // 2, b, j // 2 - 1))
                    if cross:
                        for g in range(G):
                            for q in range(QT_N):
                                o = (g * QT_N + q) * P
                                ins = eng.transpose(ps_t[0:SC, j % 2, o:o + P], prob[:, j % NB, q * G + g, :], ident[:, :])
                    else:
                        for q in range(QT_N):
                            for c in range(NV):
                                o = (c * QT_N + q) * P
                                ins = eng.transpose(ps_t[:, j % 2, o:o + P], prob_flat[:, j % NB, q * S + c * P:q * S + (c + 1) * P],
                                                    ident[:, :])
                    ins.then_inc(turned, 1)

                def values(b, par, g):
                    for p2 in range(2):
                        last = [j for j in range(g * UG, (g + 1) * UG) if j % 2 == p2][-1]
                        eng.wait_ge(turned_free[p2], count(NU // 2, b, last // 2))
                    if g == 0:
                        if cross:
                            eng.wait_ge(keys_free, count(NK, b, NK - 1))
                        else:
                            eng.wait_ge(front_free, count(NF, b, NF - 1))
                    if g % GP == 0:
                        eng.wait_ge(out_free, count(NF_OUT, b, g // GP - 1))
                    pt = prob_t[g % 2]
                    for c in range(NV):
                        for hh in range(HG):
                            r, sub = hh // G, hh % G
                            o = sub * S if cross else c * S
                            ins = eng.matmul(ps_o[hh * dv:(hh + 1) * dv, 0:S], v_s[par][0:v_n, c, head_of(g * HG + hh), :],
                                             pt[0:v_n, r, o:o + S], start=(g % GP == 0 and c == 0),
                                             stop=(g % GP == GP - 1 and c == NV - 1))
                    ins.then_inc(out_done, 1)

                def step(kind, b, par, i):
                    u = unit(kind, b, i)
                    if u:
                        turn(u[0], par, u[2])
                    if OUT_EARLY:
                        step_values(kind, b, par, i)
                    if kind in ("mid", "last") and i < 5:
                        route_step(b - 1, 1 - par, i)
                    u = unit(kind, b, i + LOOK)
                    if u:
                        nb, nxt, j = u
                        scores(nb, (par + nxt) % 2, j)
                    if not OUT_EARLY:
                        step_values(kind, b, par, i)
                    if kind in ("mid", "last") and i == 1:
                        projection(b - 1)
                    if kind in ("mid", "last") and i >= 5:
                        route_step(b - 1, 1 - par, i)

                def step_values(kind, b, par, i):
                    if kind != "first" and i % UG == 0 and i >= UG:
                        values(b, par, i // UG - 1)
                    if kind in ("mid", "last") and i == 0:
                        values(b - 1, 1 - par, NG - 1)

                def route_step(b, par, i):
                    if not route or i not in (3, 4, 6):
                        return
                    e = (3, 4, 6).index(i)
                    eng.wait_ge(r_emptied, count(3, b, e - 1))
                    if e == 0:
                        eng.wait_ge(r_xn_done, count(1, b, 0))
                        for c in range(DT):
                            for q in range(QT_N):
                                ins = eng.transpose(ps_r[:, c * S + q * P:c * S + (q + 1) * P],
                                                    xr[:, par, q, c * P:(c + 1) * P], ident[:, :])
                    elif e == 1:
                        for q in range(QT_N):
                            for t in range(DT):
                                ins = eng.matmul(ps_r[:, q * EXPERTS:(q + 1) * EXPERTS], xr_t[:, t, q * P:(q + 1) * P],
                                                 route["wr"][:, t, :], start=(t == 0), stop=(t == DT - 1))
                    else:
                        eng.wait_ge(both_done, count(1, b, 0))
                        w = QT_N * EXPERTS
                        for a, m in enumerate((route["before"], route["ones"])):
                            ins = eng.matmul(ps_r[:, a * w:(a + 1) * w], m[:, :], both[:, :, :].rearrange("p q e -> p (q e)"),
                                             start=True, stop=True)
                    ins.then_inc(r_filled, 1)

                def tail(b, par):
                    values(b, par, NG - 1)
                    projection(b)
                    for i in range(NU):
                        route_step(b, par, i)

                def projection(b):
                    eng.wait_ge(out_free, count(NF_OUT, b, NT - 1))
                    for q in range(QT_N):
                        for g in range(NT):
                            ins = eng.matmul(ps_o[:, q * D:(q + 1) * D], o_t[:, g, q * P:(q + 1) * P], wo[:, g, :],
                                             start=(g == 0), stop=(g == NT - 1))
                    ins.then_inc(out_done, 1)

                run(step, front, tail, eng)
        nc.clear_and_free_semaphores(used)
        nc.all_engine_barrier()


MAX_BLOCKS = TILES * TOP + EXPERTS
ROWS = TABLE_BLOCKS * P
LISTED = MAX_BLOCKS + 2


def hidden_tiles(hidden):
    first = (hidden + 3) // 4 * 2
    halves = [(0, first), (first, hidden - first)]
    return halves, [[(o + k, min(P, n - k)) for k in range(0, n, P)] for o, n in halves]


def expert_weights(nc, stack, name, hidden, wa, wb, wd, b1=None, b2=None):
    halves, tiles = hidden_tiles(hidden)
    KT, first = len(tiles[0]), (wa,) if wb is None else (wa, wb)

    def sb(n, shape):
        return stack.enter_context(nc.sbuf_tensor(f"{name}_{n}", shape, F32))

    w = dict(up=[sb(f"w_up{i}", [P, len(first), DT, hidden]) for i in range(2)],
             down=[sb(f"w_down{i}", [P, 2 * KT, D]) for i in range(2)],
             b_up=[sb(f"b_up{i}", [P, hidden]) for i in range(2)] if b1 is not None else None,
             b_down=[sb(f"b_down{i}", [P, D]) for i in range(2)] if b1 is not None else None,
             landed=[nc.alloc_semaphore(f"{name}_weights{i}") for i in range(2)], loads=0)

    def load(eng, e, par):
        n = [0]

        def dma(dst, src):
            eng.dma_start(dst, src).then_inc(w["landed"][par], 16)
            n[0] += 1

        def one(d):
            return d[bass.ds(e, 1)].rearrange("a r c -> (a r) c")

        for j, d in enumerate(first):
            dma(w["up"][par][:, j, :, :], one(d).rearrange("(c p) h -> p c h", p=P))
        for c in range(2):
            full = [t for t in tiles[c] if t[1] == P]
            r0 = full[0][0]
            dma(w["down"][par][:, c * KT:c * KT + len(full), :],
                one(wd)[r0:r0 + len(full) * P, :].rearrange("(k p) d -> p k d", p=P))
            for r0, rows in tiles[c][len(full):]:
                dma(w["down"][par][0:rows, c * KT + KT - 1, :], one(wd)[r0:r0 + rows, :])
        if b1 is not None:
            dma(w["b_up"][par][:, :], b1[bass.ds(e, 1), :].to_broadcast([P, hidden]))
            dma(w["b_down"][par][:, :], b2[bass.ds(e, 1), :].to_broadcast([P, D]))
        w["loads"] = n[0]

    w["load"] = load
    return w


def combination(nc, stack, name, X, route):
    gate, slot, table = route["gate"], route["slot"], route["table"]
    ring = 2 * QT_N
    got = stack.enter_context(nc.sbuf_tensor(f"{name}_got", [P, ring, TOP, D], F32))
    gathered = [nc.alloc_semaphore(f"{name}_gathered{i}") for i in range(ring)]
    first_added, added = nc.alloc_semaphore(f"{name}_first_added"), nc.alloc_semaphore(f"{name}_added")

    def gather(eng, t):
        if t >= ring:
            eng.wait_ge(added, t - ring + 1)
        for k in range(TOP):
            eng.indirect_dma_start(got[:, t % ring, k, :], None, table,
                                   bass.IndirectOffsetOnAxis(ap=slot[:, t, k:k + 1], axis=0)).then_inc(gathered[t % ring], 16)

    def add(eng, t):
        eng.wait_ge(gathered[t % ring], (t // ring + 1) * 16 * TOP)
        for k, s in enumerate((first_added, added)):
            eng.scalar_tensor_tensor(out=X[:, t, :], in0=got[:, t % ring, k, :], scalar=gate[:, t, k:k + 1],
                                     in1=X[:, t, :], op0=ALU.mult, op1=ALU.add).then_inc(s, 1)
            if k == 0:
                eng.wait_ge(first_added, t + 1)

    return dict(gather=gather, add=add, added=added, sems=[*gathered, first_added, added])


def block_list(nc, stack, name, env, route):
    def tb(n, shape, dt=F32):
        return stack.enter_context(nc.sbuf_tensor(f"{name}_{n}", shape, dt))

    blocks_i = tb("blocks_i", [P, EXPERTS], I32)
    base_i = tb("base_i", [P, EXPERTS + 1], I32)
    list_i = tb("list_i", [P, LISTED], I32)
    tokens = tb("tokens", [P, EXPERTS])
    blocks_f = tb("blocks_f", [P, EXPERTS])
    cum_f = tb("cum_f", [P, EXPERTS + 1])
    past = tb("past", [P, LISTED, EXPERTS - 1])
    list_f = tb("list_f", [P, LISTED])
    link_v = nc.alloc_semaphore(f"{name}_link_v")

    def compute(eng):
        n = [0]

        def linked(ins):
            n[0] += 1
            ins.then_inc(link_v, 1)
            eng.wait_ge(link_v, n[0])

        linked(eng.tensor_tensor(tokens[:, :], route["taken"][:, :], env["regions"][:, :], ALU.subtract))
        linked(eng.tensor_scalar(blocks_i[:, :], tokens[:, :], float(P - 1), None, ALU.add))
        linked(eng.tensor_scalar(blocks_i[:, :], blocks_i[:, :], 7, None, ALU.logical_shift_right))
        linked(eng.tensor_copy(blocks_f[:, :], blocks_i[:, :]))
        linked(eng.tensor_scalar(blocks_f[:, :], blocks_f[:, :], 1.0, None, ALU.max))
        eng.tensor_copy(blocks_i[:, :], blocks_f[:, :])
        linked(eng.memset(cum_f[:, :], 0.0))
        linked(eng.tensor_tensor_scan(cum_f[:, 1:EXPERTS + 1], env["ones"][:, 0:EXPERTS], blocks_f[:, :], 0.0,
                                      ALU.mult, ALU.add))
        eng.tensor_copy(base_i[:, :], cum_f[:, :])
        linked(eng.tensor_scalar(blocks_f[:, :], blocks_f[:, :], -1.0, float(REGION), ALU.mult, ALU.add))
        shape = [P, LISTED, EXPERTS - 1]
        linked(eng.tensor_tensor(past[:, :, :], env["numbers"][:, 0:LISTED].unsqueeze(2).to_broadcast(shape),
                                 cum_f[:, 1:EXPERTS].unsqueeze(1).to_broadcast(shape), ALU.is_ge))
        linked(eng.tensor_tensor(past[:, :, :], past[:, :, :],
                                 blocks_f[:, 0:EXPERTS - 1].unsqueeze(1).to_broadcast(shape), ALU.mult))
        linked(eng.tensor_reduce(list_f[:, :], past[:, :, :], AX.X, ALU.add))
        eng.tensor_tensor(list_i[:, :], list_f[:, :], env["numbers"][:, 0:LISTED], ALU.add)

    route["list_blocks"] = compute
    return dict(blocks=blocks_i, base=base_i, list=list_i, sems=[link_v])


def moe(nc, name, env, hidden, gated, weights, listed, route=None):
    X, ident = env["X"], env["ident"]
    halves, ktiles = hidden_tiles(hidden)
    HC = halves[0][1]
    KT = len(ktiles[0])
    NH = 2 if gated else 1
    PIECES = 1 if gated else 2
    PW = HC // PIECES
    n_w = weights["loads"]

    used = list(listed["sems"])

    def sem(n):
        used.append(nc.alloc_semaphore(f"{name}_{n}"))
        return used[-1]

    with ExitStack() as stack:
        def sb(n, shape, dt=F32):
            return stack.enter_context(nc.sbuf_tensor(f"{name}_{n}", shape, dt))

        table = route["table"]
        blocks_i, base_i, list_i = listed["blocks"], listed["base"], listed["list"]
        rows_landed, y_stored = sem("rows_landed"), sem("y_stored")
        with ExitStack() as inner:
            def tb(n, shape, dt=F32):
                return inner.enter_context(nc.sbuf_tensor(f"{name}_{n}", shape, dt))

            ps_h = inner.enter_context(nc.psum_tensor(f"{name}_ps_h", [P, 2, 2, 512], F32))
            ps_t = inner.enter_context(nc.psum_tensor(f"{name}_ps_t", [P, 2, 512], F32))
            ps_y = inner.enter_context(nc.psum_tensor(f"{name}_ps_y", [P, 512], F32))
            ps_x = inner.enter_context(nc.psum_tensor(f"{name}_ps_x", [P, 512], F32))
            w_up, w_down, b_up, b_down = (weights[k] for k in ("up", "down", "b_up", "b_down"))
            weights_landed = weights["landed"]
            rows = tb("rows", [P, D])
            rows_t = tb("rows_t", [P, DT, P])
            mid = tb("mid", [P, 2, HC])
            hid = tb("hid", [P, 2, HC])
            hid_t = tb("hid_t", [P, 2, KT, P])
            y = tb("y", [P, D])
            rows_turned, rows_ready = sem("rows_turned"), sem("rows_ready")
            up_done, mid_done, hid_done = sem("up"), sem("mid"), sem("hid")
            hid_turned, hid_t_done = sem("hid_turned"), [sem("hid_t0"), sem("hid_t1")]
            cleared = sem("cleared")
            down_done, y_done = sem("down"), sem("y")
            through = sem("through")

            def experts_loop(eng, body, after=None):
                def experts(pair):
                    for par in range(2):
                        e = pair * 2 + par
                        count_e = eng.value_load(blocks_i[0:1, bass.ds(e, 1)], min_val=1, max_val=TILES)
                        base_e = eng.value_load(base_i[0:1, bass.ds(e, 1)], min_val=0, max_val=MAX_BLOCKS)
                        with eng.Fori(0, count_e) as i:
                            n = nc.s_assert_within(base_e + i, 0, MAX_BLOCKS - 1, skip_runtime_bounds_check_because=
                                                   "the experts' block counts sum to MAX_BLOCKS at most")
                            body(n, par, pair, e * REGION + i)
                        if after and pair is not last:
                            after(e, par)

                last = EXPERTS // 2 - 1
                with eng.Fori(0, last if after else last + 1) as pair:
                    experts(pair)
                if after:
                    experts(last)

            with nc.Block() as block:
                @block.sync
                def _(eng):
                    eng.sem_inc(y_stored, 16)

                    def load(n):
                        at = eng.value_load(list_i[0:1, bass.ds(n, 1)], min_val=0, max_val=TABLE_BLOCKS - 1)
                        eng.dma_start(rows[:, :], table[bass.ds(at * P, P), :]).then_inc(rows_landed, 16)

                    load(0)
                    eng.wait_ge(rows_turned, count(1, 0, 0))
                    load(1)

                    def body(n, par, pair, place):
                        eng.wait_ge(rows_turned, count(1, n + 1, 0))
                        load(n + 2)
                        eng.wait_ge(y_done, count(1, n, 0))
                        at = nc.s_assert_within(place, 0, TABLE_BLOCKS - SPARES - 1, skip_runtime_bounds_check_because=
                                                "an expert has REGION blocks at most")
                        eng.dma_start(table[bass.ds(at * P, P), :], y[:, :]).then_inc(y_stored, 16)

                    experts_loop(eng, body, after=lambda e, par: weights["load"](eng, e + 2, par))
                    last = eng.value_load(base_i[0:1, EXPERTS:EXPERTS + 1], min_val=EXPERTS, max_val=MAX_BLOCKS)
                    eng.wait_ge(y_stored, (last + 1) * 16)
                    eng.wait_ge(rows_landed, (last + 2) * 16)
                    eng.sem_inc(through, 1)

                @block.tensor
                def _(eng):
                    for s, n in ((rows_turned, 1), (up_done, 4), (hid_turned, 2), (down_done, 1)):
                        eng.sem_inc(s, n)

                    def turn_rows(n):
                        eng.wait_ge(rows_landed, (n + 1) * 16)
                        eng.wait_ge(rows_ready, count(1, n - 1, 0))
                        for c in range(DT):
                            ins = eng.transpose(ps_x[:, c * P:(c + 1) * P], rows[:, c * P:(c + 1) * P], ident[:, :])
                        ins.then_inc(rows_turned, 1)

                    def up(n, par, c, products=range(2)):
                        if products[0] == 0:
                            eng.wait_ge(hid_done if gated else mid_done, count(2 * PIECES, n - 1, (c + 1) * PIECES - 1))
                        o, w = halves[c]
                        for j in products:
                            m, p0 = (j, 0) if gated else (0, j * PW)
                            pw = w if gated else PW
                            for t in range(DT):
                                ins = eng.matmul(ps_h[:, c, j, 0:pw], rows_t[:, t, :],
                                                 w_up[par][:, m, t, o + p0:o + p0 + pw], start=(t == 0), stop=(t == DT - 1))
                            ins.then_inc(up_done, 1)

                    def turn_hidden(n, c):
                        eng.wait_ge(hid_done, count(2 * PIECES, n, (c + 1) * PIECES - 1))
                        eng.wait_ge(hid_t_done[c], count(1, n - 1, 0))
                        for k, (r0, w) in enumerate(ktiles[c]):
                            o = r0 - halves[c][0]
                            ins = eng.transpose(ps_t[0:w, c, k * P:(k + 1) * P], hid[:, c, o:o + w], ident[:, :])
                        ins.then_inc(hid_turned, 1)

                    def down(n, par, c, ks=range(KT)):
                        if ks[0] == 0:
                            eng.wait_ge(hid_t_done[c], count(1, n, 0))
                        if c == 0 and ks[0] == 0:
                            eng.wait_ge(y_done, count(1, n - 1, 0))
                        for k in ks:
                            w = ktiles[c][k][1]
                            ins = eng.matmul(ps_y[:, 0:D], hid_t[0:w, c, k, :], w_down[par][0:w, c * KT + k, :],
                                             start=(c == 0 and k == 0), stop=(c == 1 and k == KT - 1))
                        if c == 1 and ks[-1] == KT - 1:
                            ins.then_inc(down_done, 1)

                    turn_rows(0)
                    eng.wait_ge(cleared, 2)

                    def body(n, par, pair, place):
                        eng.wait_ge(weights_landed[par], (pair + 1) * (16 * n_w))
                        eng.wait_ge(rows_ready, count(1, n, 0))
                        up(n, par, 0)
                        up(n, par, 1, [0])
                        turn_hidden(n, 0)
                        up(n, par, 1, [1])
                        turn_rows(n + 1)
                        down(n, par, 0, range(KT - 2))
                        turn_hidden(n, 1)
                        down(n, par, 0, range(KT - 2, KT))
                        down(n, par, 1)

                    experts_loop(eng, body)

                @block.scalar
                def _(eng):
                    eng.preload_act_table(ACT.Silu if gated else ACT.Gelu)
                    eng.sem_inc(rows_ready, 1)
                    eng.sem_inc(hid_t_done[0], 1)
                    eng.sem_inc(mid_done if gated else hid_done, 2 * PIECES)

                    def rows_out(n):
                        eng.wait_ge(rows_turned, count(1, n, 0))
                        eng.activation(rows_t[:, :, :], ps_x[:, 0:D].rearrange("p (c s) -> p c s", c=DT),
                                       ACT.Copy).then_inc(rows_ready, 1)

                    def turned(n, c):
                        eng.wait_ge(hid_turned, count(2, n, c))
                        eng.wait_ge(down_done, count(1, n - 1, 0))
                        eng.activation(hid_t[:, c, :, :], ps_t[:, c, 0:KT * P].rearrange("p (k s) -> p k s", s=P),
                                       ACT.Copy).then_inc(hid_t_done[0], 1)

                    rows_out(0)

                    def body(n, par, pair, place):
                        if gated:
                            for c in range(2):
                                w = halves[c][1]
                                eng.wait_ge(up_done, count(4, n, c * 2))
                                eng.wait_ge(hid_done, count(2, n - 1, c))
                                eng.activation(mid[:, c, 0:w], ps_h[:, c, 0, 0:w], ACT.Silu).then_inc(mid_done, 1)
                            turned(n, 0)
                        else:
                            for i in range(4):
                                c, o = i // 2, i % 2 * PW
                                if i == 3:
                                    turned(n, 0)
                                eng.wait_ge(mid_done, count(4, n, i))
                                eng.wait_ge(hid_turned, count(2, n - 1, c))
                                eng.activation(hid[:, c, o:o + PW], mid[:, c, o:o + PW], ACT.Gelu).then_inc(hid_done, 1)
                        rows_out(n + 1)

                    experts_loop(eng, body)

                @block.vector
                def _(eng):
                    eng.sem_inc(hid_done if gated else mid_done, 2 * PIECES)
                    eng.sem_inc(hid_t_done[1], 1)
                    for c in range(2):
                        eng.memset(ps_t[:, c, :], 0.0).then_inc(cleared, 1)
                    eng.sem_inc(y_done, 1)

                    def first(n, par, c):
                        w = halves[c][1]
                        if gated:
                            eng.wait_ge(up_done, count(4, n, c * 2 + 1))
                            eng.wait_ge(mid_done, count(2, n, c))
                            eng.wait_ge(hid_turned, count(2, n - 1, c))
                            eng.tensor_tensor(hid[:, c, 0:w], mid[:, c, 0:w], ps_h[:, c, 1, 0:w], ALU.mult).then_inc(hid_done, 1)
                            return
                        for i in range(2):
                            o = i * PW
                            eng.wait_ge(up_done, count(4, n, c * 2 + i))
                            eng.wait_ge(hid_done, count(4, n - 1, c * 2 + i))
                            eng.tensor_tensor(mid[:, c, o:o + PW], ps_h[:, c, i, 0:PW],
                                              b_up[par][:, c * HC + o:c * HC + o + PW], ALU.add).then_inc(mid_done, 1)

                    def turned(n):
                        eng.wait_ge(hid_turned, count(2, n, 1))
                        eng.wait_ge(down_done, count(1, n - 1, 0))
                        eng.tensor_copy(hid_t[:, 1, :, :], ps_t[:, 1, 0:KT * P].rearrange("p (k s) -> p k s", s=P)
                                        ).then_inc(hid_t_done[1], 1)

                    def body(n, par, pair, place):
                        if not gated:
                            eng.wait_ge(weights_landed[par], (pair + 1) * (16 * n_w))
                        first(n, par, 0)
                        first(n, par, 1)
                        turned(n)
                        eng.wait_ge(down_done, count(1, n, 0))
                        eng.wait_ge(y_stored, (n + 1) * 16)
                        if gated:
                            eng.tensor_copy(y[:, :], ps_y[:, 0:D]).then_inc(y_done, 1)
                        else:
                            eng.tensor_tensor(y[:, :], ps_y[:, 0:D], b_down[par][:, :], ALU.add).then_inc(y_done, 1)

                    experts_loop(eng, body)

    nc.clear_and_free_semaphores(used)
    nc.all_engine_barrier()


OUT_NAME = "out_0_dram"


def decoder(nc, a):
    with ExitStack() as stack:
        def sb(n, shape, dt=F32):
            return stack.enter_context(nc.sbuf_tensor(n, shape, dt))

        def sem(n):
            return nc.alloc_semaphore(n)

        X = sb("X", [P, TILES, D])
        ident, identb = sb("ident", [P, P]), sb("identb", [P, P], BF16)
        hmask16, hmask64 = sb("hmask16", [P, 8]), sb("hmask64", [P, 2])
        wmask = sb("wmask", [P, QT_N, S - HALF_WINDOW], BF16)
        neg_half, eps = sb("neg_half", [P, QT_N]), sb("eps", [P, QT_N])
        env = dict(X=X, ident=ident, identb=identb, hmask16=hmask16, hmask64=hmask64, wmask=wmask, neg_half=neg_half, eps=eps)
        before, ones = sb("before", [P, P]), sb("ones", [P, P])
        numbers, regions = sb("numbers", [P, LISTED]), sb("regions", [P, EXPERTS])
        env.update(ones=ones, numbers=numbers, regions=regions)
        zero = sb("zero", [P, 1, D])
        taken = [sb(f"taken{i}", [P, EXPERTS]) for i in range(2)]
        gate, slot = sb("gate", [P, TILES, TOP]), sb("slot", [P, TILES, TOP], I32)
        wq0, wk0, wv0 = sb("wq0", [P, DT, D]), sb("wk0", [P, DT, D]), sb("wv0", [P, DT, D])
        wo0, bo0 = sb("wo0", [P, DT, D]), sb("bo0", [P, D])
        wq1, wk1, wv1 = sb("wq1", [P, DT, D]), sb("wk1", [P, DT, D]), sb("wv1", [P, DT, D])
        wo1, bo1, bv1 = sb("wo1", [P, DT, D]), sb("bo1", [P, D]), sb("bv1", [P, D])
        bq1, bq1s, bk1 = sb("bq1", [P, DT]), sb("bq1s", [P, DT]), sb("bk1", [P, DT])
        wr0, wr1 = sb("wr0", [P, DT, EXPERTS]), sb("wr1", [P, DT, EXPERTS])
        wq3, wk3, wv3 = sb("wq3", [P, DT, D]), sb("wk3", [P, DT, D]), sb("wv3", [P, DT, D])
        wo3, bo3 = sb("wo3", [P, DT, D]), sb("bo3", [P, D])
        wq2, wk2, wv2, wo2 = sb("wq2", [P, DT, 1024]), sb("wk2", [P, DT, 1024]), sb("wv2", [P, DT, 1024]), sb("wo2", [P, 8, D])
        w2_landed = sem("w2_landed")
        gamma, beta = sb("gamma", [P, DT]), sb("beta", [P, DT])

        consts, cleared, x_first, x_rest = sem("consts"), sem("cleared"), sem("x_first"), sem("x_rest")
        w0_landed, w1_landed, w3_landed = sem("w0_landed"), sem("w1_landed"), sem("w3_landed")
        wr_landed, ln_landed = sem("wr_landed"), sem("ln_landed")
        bias_scaled, zeroed, stored = sem("bias_scaled"), sem("zeroed"), sem("stored")
        table = nc.dram_tensor("expert_table", [ROWS, D], F32, kind="Internal").ap()

        x_v = a["x"].rearrange("b (q p) d -> p (b q) d", p=P)
        out_v = a["out"].rearrange("b (q p) d -> p (b q) d", p=P)

        def tiled(w):
            return w.rearrange("(t p) n -> p t n", p=P)

        with nc.Block() as block:
            @block.vector
            def _(eng):
                for m in (wq3, wk3, wv3):
                    eng.memset(m[:, :, :], 0.0).then_inc(cleared, 1)
                eng.memset(zero[:, :, :], 0.0).then_inc(cleared, 1)

            @block.gpsimd
            def _(eng):
                n = [0]

                def linked(ins):
                    n[0] += 1
                    ins.then_inc(consts, 1)
                    eng.wait_ge(consts, n[0])

                for m in (ident, identb):
                    linked(eng.memset(m[:, :], 0.0))
                    linked(eng.affine_select(out=m[:, :], in_=m[:, :], compare_op=ALU.not_equal, fill=1.0, base=0,
                                             pattern=[[-1, P]], channel_multiplier=1))
                for m, w in ((hmask16, 16), (hmask64, 64)):
                    linked(eng.memset(m[:, :], 1.0))
                    linked(eng.affine_select(out=m[:, :], in_=m[:, :], compare_op=ALU.is_ge, fill=0.0, base=0,
                                             pattern=[[-w, P // w]], channel_multiplier=1))
                    linked(eng.affine_select(out=m[:, :], in_=m[:, :], compare_op=ALU.is_ge, fill=0.0, base=w - 1,
                                             pattern=[[w, P // w]], channel_multiplier=-1))
                linked(eng.memset(wmask[:, :, :], 0.0))
                for q in range(QT_N):
                    apart = q * (P - HALF_WINDOW)
                    m = wmask[:, q, :]
                    for sign in (1, -1):
                        linked(eng.affine_select(out=m, in_=m, compare_op=ALU.is_ge, fill=MASKED,
                                                 base=HALF_WINDOW - sign * apart, pattern=[[sign, S - HALF_WINDOW]],
                                                 channel_multiplier=-sign))
                linked(eng.memset(neg_half[:, :], -0.5))
                linked(eng.memset(eps[:, :], LN_EPS))
                linked(eng.memset(ones[:, :], 1.0))
                linked(eng.affine_select(out=before[:, :], in_=ones[:, :], compare_op=ALU.is_gt, fill=0.0,
                                         base=0, pattern=[[1, P]], channel_multiplier=-1))
                linked(eng.iota(numbers[:, :], pattern=[[1, LISTED]], base=0, channel_multiplier=0,
                                allow_small_or_imprecise_dtypes=True))
                for m in (regions, *taken):
                    linked(eng.iota(m[:, :], pattern=[[REGION * P, EXPERTS]], base=0, channel_multiplier=0,
                                    allow_small_or_imprecise_dtypes=True))

            @block.scalar
            def _(eng):
                for dst, w in ((wq0, "wq0"), (wk0, "wk0"), (wv0, "wv0"), (wo0, "wo0")):
                    eng.dma_start(dst[:, :, :], tiled(a[w])).then_inc(w0_landed, 16)
                eng.dma_start(bo0[:, :], a["bo0"].unsqueeze(0).to_broadcast([P, D])).then_inc(w0_landed, 16)

            @block.sync
            def _(eng):
                eng.dma_start(X[:, 0:QT_N, :], x_v[:, 0:QT_N, :]).then_inc(x_first, 16)
                eng.dma_start(X[:, QT_N:TILES, :], x_v[:, QT_N:TILES, :]).then_inc(x_rest, 16)

        def later_loads(eng):
            def column(dst, v, s):
                eng.dma_start(dst[:, :], v.rearrange("(t p) -> p t", p=P), allow_slow_non_contiguous=True).then_inc(s, 16)

            def row(dst, v, s):
                eng.dma_start(dst[:, :], v.unsqueeze(0).to_broadcast([P, D])).then_inc(s, 16)

            for dst, w in ((wq1, "wq1"), (wk1, "wk1"), (wv1, "wv1"), (wo1, "wo1")):
                eng.dma_start(dst[:, :, :], tiled(a[w])).then_inc(w1_landed, 16)
            column(bq1, a["bq1"], w1_landed)
            column(bk1, a["bk1"], w1_landed)
            row(bv1, a["bv1"], w1_landed)
            row(bo1, a["bo1"], w1_landed)
            for dst, w in ((wq2, "wq2"), (wk2, "wk2"), (wv2, "wv2"), (wo2, "wo2")):
                eng.dma_start(dst[:, :, :], tiled(a[w])).then_inc(w2_landed, 16)
            eng.wait_ge(cleared, 4)
            eng.dma_start(table[0:ROWS - SPARES * P, :].rearrange("(k p) d -> p k d", p=P), zero[:, :, :].to_broadcast([P, ROWS // P - SPARES, D])
                          ).then_inc(zeroed, 16)
            for dst, w in ((wr0, "wr0"), (wr1, "wr1")):
                eng.dma_start(dst[:, :, :], tiled(a[w])).then_inc(wr_landed, 16)
            column(gamma, a["gamma"], ln_landed)
            column(beta, a["beta"], ln_landed)
            for dst, w in ((wq3, "wq3"), (wk3, "wk3"), (wv3, "wv3")):
                for h in range(HEADS):
                    r = h % 8 * 16
                    eng.dma_start(dst[r:r + 16, h // 8, h * 16:(h + 1) * 16], a[w]).then_inc(w3_landed, 16)
            eng.dma_start(wo3[:, :, :], tiled(a["wo3"])).then_inc(w3_landed, 16)
            row(bo3, a["bo3"], w3_landed)

        W0, W1, W3 = 5 * 16, 8 * 16, (3 * HEADS + 2) * 16
        routes = [dict(wr=wr, taken=t, experts=numbers[:, 0:EXPERTS], before=before, ones=ones, gate=gate, slot=slot,
                       table=table, zero=zero, zeroed=((zeroed, 16),)) for wr, t in ((wr0, taken[0]), (wr1, taken[1]))]
        attention(nc, "L0a", env, dh=16, windowed=True, q_scale=16 ** -0.5, wq=wq0, wk=wk0, wv=wv0, wo=wo0, bo=bo0,
                  x_landed=((x_first, 16), (x_rest, 16)), w_landed=((w0_landed, W0),), other_loads=later_loads)
        with nc.Block() as block:
            @block.scalar
            def _(eng):
                eng.wait_ge(w1_landed, W1)
                eng.activation(bq1s[:, :], bq1[:, :], ACT.Copy, scale=16 ** -0.5).then_inc(bias_scaled, 1)
                eng.wait_ge(bias_scaled, 1)
        def first_experts(weights):
            def loads(eng):
                for e in range(2):
                    weights["load"](eng, e, e)
            return loads

        with ExitStack() as inner:
            weights = expert_weights(nc, inner, "L0f", 682, a["w1_0"], a["w2_0"], a["w3_0"])
            listed = block_list(nc, inner, "L0r", env, routes[0])
            attention(nc, "L0x", env, dh=16, cross=True, q_scale=16 ** -0.5, wq=wq1, wk=wk1, wv=wv1, wo=wo1, bq=bq1s,
                      bk=bk1, bv=bv1, bo=bo1, ctx_dram=a["ctx"], w_landed=((w1_landed, W1), (wr_landed, 32)),
                      route=routes[0], other_loads=first_experts(weights))
            moe(nc, "L0f", env, 682, True, weights, listed, route=routes[0])
        with ExitStack() as inner:
            pending = combination(nc, inner, "L0c", X, routes[0])
            attention(nc, "L1a", env, dh=64, q_scale=1 / 8, wq=wq2, wk=wk2, wv=wv2, wo=wo2, affine=(gamma, beta),
                      w_landed=((w2_landed, 64), (ln_landed, 32)), pending=pending)
            nc.clear_and_free_semaphores(pending["sems"])
            nc.all_engine_barrier()
        with ExitStack() as inner:
            weights = expert_weights(nc, inner, "L1f", 1024, a["w1_1"], None, a["w2_1"], a["b1_1"], a["b2_1"])
            listed = block_list(nc, inner, "L1r", env, routes[1])
            attention(nc, "L1x", env, dh=16, cross=True, q_scale=D ** -0.5, wq=wq3, wk=wk3, wv=wv3, wo=wo3, bo=bo3,
                      ctx_dram=a["ctx"], w_landed=((w3_landed, W3),), route=routes[1],
                      other_loads=first_experts(weights))
            moe(nc, "L1f", env, 1024, False, weights, listed, route=routes[1])
        with ExitStack() as inner:
            last = combination(nc, inner, "L1c", X, routes[1])
            with nc.Block() as block:
                @block.gpsimd
                def _(eng):
                    for t in range(TILES):
                        last["gather"](eng, t)

                @block.vector
                def _(eng):
                    for t in range(TILES):
                        last["add"](eng, t)

                @block.sync
                def _(eng):
                    for t in range(TILES):
                        eng.wait_ge(last["added"], t + 1)
                        eng.dma_start(out_v[:, t, :], X[:, t, :]).then_inc(stored, 16)
                    eng.wait_ge(stored, 16 * TILES)


def kernel(**inputs):
    import numpy as np
    import concourse.bacc as bacc
    from concourse.bass_utils import run_bass_kernel_spmd

    i = {k: np.asarray(v) for k, v in inputs.items()}
    qkv = i["L0_attn_W_qkv"]
    laid = {
        "x": i["x"], "ctx": i["ctx_1024"],
        "wq0": qkv[:, 0:256], "wk0": qkv[:, 256:512], "wv0": qkv[:, 512:768],
        "wo0": i["L0_attn_W_proj"], "bo0": i["L0_attn_b_proj"],
        "wq1": i["L0_xattn_wq"].T, "wk1": i["L0_xattn_wk"].T, "wv1": i["L0_xattn_wv"].T, "wo1": i["L0_xattn_wo"].T,
        "bq1": i["L0_xattn_bq"], "bk1": i["L0_xattn_bk"], "bv1": i["L0_xattn_bv"], "bo1": i["L0_xattn_bo"],
        "wr0": i["L0_ffn_Wg"].T, "w1_0": i["L0_ffn_W1"].transpose(0, 2, 1), "w2_0": i["L0_ffn_W2"].transpose(0, 2, 1),
        "w3_0": i["L0_ffn_W3"].transpose(0, 2, 1),
        "gamma": i["L1_attn_ln_gamma"], "beta": i["L1_attn_ln_beta"],
        "wq2": i["L1_attn_Wq"], "wk2": i["L1_attn_Wk"], "wv2": i["L1_attn_Wv"], "wo2": i["L1_attn_Wo"],
        "wq3": i["L1_xattn_Wq"].T, "wk3": i["L1_xattn_Wk"].T, "wv3": i["L1_xattn_Wv"].T, "wo3": i["L1_xattn_Wo"].T,
        "bo3": i["L1_xattn_bo"],
        "wr1": i["L1_ffn_Wr"].T, "w1_1": i["L1_ffn_W1"].transpose(0, 2, 1), "b1_1": i["L1_ffn_b1"],
        "w2_1": i["L1_ffn_W2"].transpose(0, 2, 1), "b2_1": i["L1_ffn_b2"],
    }
    nc = bacc.Bacc("TRN2", target_bir_lowering=False, num_devices=1)
    arrays, aps = {}, {}
    for name, v in laid.items():
        v = np.ascontiguousarray(v)
        arrays[f"in_{name}_dram"] = v
        aps[name] = nc.dram_tensor(f"in_{name}_dram", v.shape, mybir.dt.from_np(v.dtype), kind="ExternalInput").ap()
    aps["out"] = nc.dram_tensor(OUT_NAME, (B, S, D), F32, kind="ExternalOutput").ap()
    decoder(nc, aps)
    r = run_bass_kernel_spmd(nc, [arrays], core_ids=[0])
    return r.results[0][OUT_NAME]
```
